# Optimizing a Trainium2 kernel written in Bass

```python
import numpy as np
import jax
import jax.numpy as jnp

def _softmax(x, axis=-1):
    return jax.nn.softmax(x, axis=axis)

def _gelu(x):
    return jax.nn.gelu(x, approximate=True)

def _silu(x):
    return jax.nn.silu(x)

def _sigmoid(x):
    return jax.nn.sigmoid(x)

def _layernorm(x, axis=-1, eps=1e-05):
    m = jnp.mean(x, axis=axis, keepdims=True)
    v = jnp.var(x, axis=axis, keepdims=True)
    return (x - m) / jnp.sqrt(v + eps)

def _scatter_add(tgt, idx, src, axis=0):
    return tgt.at[idx].add(src)

def _segment_sum(src, seg, n):
    return jax.ops.segment_sum(src, seg, n)
kernel_name = 'mk_xattn_ffn_d2_seqx_r8_1077e9'

def setup_inputs(seed: int=0):
    np.random.seed(seed)
    _w = jnp.asarray

    def _rec_inputs():
        import jax
        import jax.numpy as jnp
        _rk = jax.random.key(seed)
        x = -0.0005207 + 1.001 * jax.random.normal(jax.random.fold_in(_rk, 1), (4, 256, 256), jnp.float32)
        _lenS = 256 - jax.random.randint(jax.random.fold_in(_rk, 7), (4,), 0, max(1, 256 // 4) + 1, jnp.int32)
        _lenS2 = 1601 - jax.random.randint(jax.random.fold_in(_rk, 8), (4,), 0, max(1, 1601 // 4) + 1, jnp.int32)
        _ctx_2048P = jax.random.normal(jax.random.fold_in(_rk, 11), (4, 16, 256), jnp.float32)
        _ctx_2048c = jax.random.dirichlet(jax.random.fold_in(_rk, 511), 0.3 * jnp.ones((16,), jnp.float32), (4, 1601))
        _ctx_2048t = jnp.einsum('bsk,bkd->bsd', _ctx_2048c, _ctx_2048P)
        _ctx_2048t = _ctx_2048t * jax.lax.rsqrt(jnp.mean(jnp.square(_ctx_2048t)) + 1e-12) * 0.953939
        ctx_2048 = 2.81802e-05 + 1.00001 * (_ctx_2048t + 0.3 * jax.random.normal(jax.random.fold_in(_rk, 611), (4, 1601, 256), jnp.float32))
        pos_BxS2 = jnp.broadcast_to(jnp.arange(1601, dtype=jnp.int32), (4, 1601))
        itok_BxS_4096_4607 = jax.random.randint(jax.random.fold_in(_rk, 13), (4, 256), 512, 576, jnp.int32)
        itok_BxS_0_1023 = jax.random.randint(jax.random.fold_in(_rk, 14), (4, 256), 0, 128, jnp.int32)
        return (x, ctx_2048, pos_BxS2, itok_BxS_4096_4607, itok_BxS_0_1023)
    x, ctx_2048, pos_BxS2, itok_BxS_4096_4607, itok_BxS_0_1023 = _rec_inputs()

    def _L0_xattn_setup():
        import jax, jax.numpy as jnp
        import numpy as np
        B, CTX, DRAFT, D = (2, 512, 64, 256)
        H, KVH, HD = (16, 4, 128)
        N_REP = H // KVH
        EPS = 1e-06
        THETA = 10000.0
        SCALE = 1.0 / np.sqrt(HD).astype(np.float32)

        def _rms_norm(x, w):
            v = jnp.mean(jnp.square(x.astype(jnp.float32)), axis=-1, keepdims=True)
            return (w * (x.astype(jnp.float32) * jax.lax.rsqrt(v + EPS))).astype(x.dtype)

        def _rotate_half(x):
            x1, x2 = jnp.split(x, 2, axis=-1)
            return jnp.concatenate((-x2, x1), axis=-1)

        def _rope(x, pos):
            inv_freq = 1.0 / THETA ** (jnp.arange(0, HD, 2, dtype=jnp.float32) / HD)
            freqs = pos.astype(jnp.float32)[:, None, :, None] * inv_freq
            emb = jnp.concatenate((freqs, freqs), axis=-1)
            return x * jnp.cos(emb) + _rotate_half(x) * jnp.sin(emb)
        key = jax.random.key(seed)
        ks = jax.random.split(key, 6)
        return {'draft_hidden': jax.random.normal(ks[0], (B, DRAFT, D), jnp.float32), 'context_hidden': jax.random.normal(ks[1], (B, CTX, D), jnp.float32), 'Wq': jax.random.normal(ks[2], (H * HD, D), jnp.float32) * 0.02, 'Wk': jax.random.normal(ks[3], (KVH * HD, D), jnp.float32) * 0.02, 'Wv': jax.random.normal(ks[4], (KVH * HD, D), jnp.float32) * 0.02, 'Wo': jax.random.normal(ks[5], (D, H * HD), jnp.float32) * 0.02, 'q_norm_w': jnp.ones((HD,), jnp.float32), 'k_norm_w': jnp.ones((HD,), jnp.float32), 'context_position_ids': jnp.broadcast_to(jnp.arange(CTX, dtype=jnp.int32), (B, CTX)), 'draft_position_ids': jnp.broadcast_to(CTX + jnp.arange(DRAFT, dtype=jnp.int32), (B, DRAFT))}
    _L0_xattn_all = _L0_xattn_setup()
    _L0_xattn_in = {k: v for k, v in _L0_xattn_all.items() if k in ('Wq', 'Wk', 'Wv', 'Wo', 'q_norm_w', 'k_norm_w')}
    del _L0_xattn_all

    def _L0_ffn_setup():
        import jax, jax.numpy as jnp
        import numpy as np
        NUM_EXPERTS = 32
        TOP_K = 6
        N_GROUPS = 4
        N_LIMITED_GROUPS = 2
        key = jax.random.key(seed)
        ks = jax.random.split(key, 8)
        H, M = (256, 176)
        SH = 2 * M
        s = 0.02
        return {'hidden_states': jax.random.normal(ks[0], (4, 256, H), jnp.float32), 'gate_w': jax.random.normal(ks[1], (H, NUM_EXPERTS), jnp.float32) * s, 'w_gate': jax.random.normal(ks[2], (NUM_EXPERTS, H, M), jnp.float32) * s, 'w_up': jax.random.normal(ks[3], (NUM_EXPERTS, H, M), jnp.float32) * s, 'w_down': jax.random.normal(ks[4], (NUM_EXPERTS, M, H), jnp.float32) * s, 'sw_gate': jax.random.normal(ks[5], (H, SH), jnp.float32) * s, 'sw_up': jax.random.normal(ks[6], (H, SH), jnp.float32) * s, 'sw_down': jax.random.normal(ks[7], (SH, H), jnp.float32) * s}
    _L0_ffn_all = _L0_ffn_setup()
    _L0_ffn_in = {k: v for k, v in _L0_ffn_all.items() if k in ('gate_w', 'w_gate', 'w_up', 'w_down', 'sw_gate', 'sw_up', 'sw_down')}
    del _L0_ffn_all

    def _L1_xattn_setup():
        import jax, jax.numpy as jnp
        import numpy as np
        B, Lq, Lk = (2, 512, 128)
        Q_DIM, KV_DIM = (256, 256)
        H, HD = (16, 128)
        KVC, QC, R = (64, 96, 64)
        LOOKBACK = 8
        NEG = -1e+30

        def _rope(x, L):
            half = x.shape[-1] // 2
            inv_freq = 1.0 / 10000.0 ** (jnp.arange(half, dtype=jnp.float32) / half)
            ang = jnp.arange(L, dtype=jnp.float32)[:, None] * inv_freq
            cos, sin = (jnp.cos(ang), jnp.sin(ang))
            x1, x2 = (x[..., :half], x[..., half:])
            return jnp.concatenate([x1 * cos - x2 * sin, x1 * sin + x2 * cos], axis=-1)
        key = jax.random.key(seed)
        ks = jax.random.split(key, 11)

        def w(k, shape, fan_in):
            return jax.random.normal(k, shape, jnp.float32) / np.sqrt(fan_in).astype(np.float32)
        return {'q': jax.random.normal(ks[0], (B, Lq, Q_DIM), jnp.float32), 'kv': jax.random.normal(ks[1], (B, Lk, KV_DIM), jnp.float32), 'seg_id': jnp.sort(jax.random.randint(ks[2], (B, Lq), 0, Lk), axis=-1), 'W_kvc': w(ks[3], (KV_DIM, KVC), KV_DIM), 'W_dq': w(ks[4], (Q_DIM, QC), Q_DIM), 'W_uq': w(ks[5], (QC, H * HD), QC), 'W_qr': w(ks[6], (QC, H * R), QC), 'W_uk': w(ks[7], (KVC, H * HD), KVC), 'W_kr': w(ks[8], (KVC, R), KVC), 'W_uv': w(ks[9], (KVC, H * HD), KVC), 'W_o': w(ks[10], (H * HD, Q_DIM), H * HD)}
    _L1_xattn_all = _L1_xattn_setup()
    _L1_xattn_in = {k: v for k, v in _L1_xattn_all.items() if k in ('W_kvc', 'W_dq', 'W_uq', 'W_qr', 'W_uk', 'W_kr', 'W_uv', 'W_o')}
    del _L1_xattn_all

    def _L1_ffn_setup():
        import jax, jax.numpy as jnp
        import numpy as np
        B, S, H, I = (1, 64, 256, 768)

        def _quantized_matmul(x, w, scale):
            wq = w.astype(jnp.float8_e4m3fn).astype(x.dtype)
            y = jnp.einsum('bsi,io->bso', x, wq)
            return y * scale
        key = jax.random.key(seed)
        ks = jax.random.split(key, 7)
        return {'x': jax.random.normal(ks[0], (B, S, H), dtype=jnp.float32), 'gate_w': jax.random.normal(ks[1], (H, I), dtype=jnp.float32) * 0.02, 'up_w': jax.random.normal(ks[2], (H, I), dtype=jnp.float32) * 0.02, 'down_w': jax.random.normal(ks[3], (I, H), dtype=jnp.float32) * 0.02, 'gate_scale': jax.random.uniform(ks[4], (I,), dtype=jnp.float32, minval=0.5, maxval=1.5), 'up_scale': jax.random.uniform(ks[5], (I,), dtype=jnp.float32, minval=0.5, maxval=1.5), 'down_scale': jax.random.uniform(ks[6], (H,), dtype=jnp.float32, minval=0.5, maxval=1.5)}
    _L1_ffn_all = _L1_ffn_setup()
    _L1_ffn_in = {k: v for k, v in _L1_ffn_all.items() if k in ('gate_w', 'up_w', 'down_w', 'gate_scale', 'up_scale', 'down_scale')}
    del _L1_ffn_all
    return {'x': x, 'ctx_2048': ctx_2048, 'pos_BxS2': pos_BxS2, 'itok_BxS_4096_4607': itok_BxS_4096_4607, 'itok_BxS_0_1023': itok_BxS_0_1023, 'L0_xattn_Wq': _L0_xattn_in['Wq'], 'L0_xattn_Wk': _L0_xattn_in['Wk'], 'L0_xattn_Wv': _L0_xattn_in['Wv'], 'L0_xattn_Wo': _L0_xattn_in['Wo'], 'L0_xattn_q_norm_w': _L0_xattn_in['q_norm_w'], 'L0_xattn_k_norm_w': _L0_xattn_in['k_norm_w'], 'L0_ffn_gate_w': _L0_ffn_in['gate_w'], 'L0_ffn_w_gate': _L0_ffn_in['w_gate'], 'L0_ffn_w_up': _L0_ffn_in['w_up'], 'L0_ffn_w_down': _L0_ffn_in['w_down'], 'L0_ffn_sw_gate': _L0_ffn_in['sw_gate'], 'L0_ffn_sw_up': _L0_ffn_in['sw_up'], 'L0_ffn_sw_down': _L0_ffn_in['sw_down'], 'L1_xattn_W_kvc': _L1_xattn_in['W_kvc'], 'L1_xattn_W_dq': _L1_xattn_in['W_dq'], 'L1_xattn_W_uq': _L1_xattn_in['W_uq'], 'L1_xattn_W_qr': _L1_xattn_in['W_qr'], 'L1_xattn_W_uk': _L1_xattn_in['W_uk'], 'L1_xattn_W_kr': _L1_xattn_in['W_kr'], 'L1_xattn_W_uv': _L1_xattn_in['W_uv'], 'L1_xattn_W_o': _L1_xattn_in['W_o'], 'L1_ffn_gate_w': _L1_ffn_in['gate_w'], 'L1_ffn_up_w': _L1_ffn_in['up_w'], 'L1_ffn_down_w': _L1_ffn_in['down_w'], 'L1_ffn_gate_scale': _L1_ffn_in['gate_scale'], 'L1_ffn_up_scale': _L1_ffn_in['up_scale'], 'L1_ffn_down_scale': _L1_ffn_in['down_scale']}

def reference(x, ctx_2048, pos_BxS2, itok_BxS_4096_4607, itok_BxS_0_1023, L0_xattn_Wq, L0_xattn_Wk, L0_xattn_Wv, L0_xattn_Wo, L0_xattn_q_norm_w, L0_xattn_k_norm_w, L0_ffn_gate_w, L0_ffn_w_gate, L0_ffn_w_up, L0_ffn_w_down, L0_ffn_sw_gate, L0_ffn_sw_up, L0_ffn_sw_down, L1_xattn_W_kvc, L1_xattn_W_dq, L1_xattn_W_uq, L1_xattn_W_qr, L1_xattn_W_uk, L1_xattn_W_kr, L1_xattn_W_uv, L1_xattn_W_o, L1_ffn_gate_w, L1_ffn_up_w, L1_ffn_down_w, L1_ffn_gate_scale, L1_ffn_up_scale, L1_ffn_down_scale):
    import jax
    import jax.numpy as jnp

    def _L0_xattn_ref(draft_hidden, context_hidden, Wq, Wk, Wv, Wo, q_norm_w, k_norm_w, context_position_ids, draft_position_ids):
        import jax, jax.numpy as jnp
        import numpy as np
        B, CTX, DRAFT, D = (2, 512, 64, 256)
        H, KVH, HD = (16, 4, 128)
        N_REP = H // KVH
        EPS = 1e-06
        THETA = 10000.0
        SCALE = 1.0 / np.sqrt(HD).astype(np.float32)

        def _rms_norm(x, w):
            v = jnp.mean(jnp.square(x.astype(jnp.float32)), axis=-1, keepdims=True)
            return (w * (x.astype(jnp.float32) * jax.lax.rsqrt(v + EPS))).astype(x.dtype)

        def _rotate_half(x):
            x1, x2 = jnp.split(x, 2, axis=-1)
            return jnp.concatenate((-x2, x1), axis=-1)

        def _rope(x, pos):
            inv_freq = 1.0 / THETA ** (jnp.arange(0, HD, 2, dtype=jnp.float32) / HD)
            freqs = pos.astype(jnp.float32)[:, None, :, None] * inv_freq
            emb = jnp.concatenate((freqs, freqs), axis=-1)
            return x * jnp.cos(emb) + _rotate_half(x) * jnp.sin(emb)
        bsz, draft_len, _ = draft_hidden.shape
        ctx_len = context_hidden.shape[1]
        total_len = ctx_len + draft_len
        q = (draft_hidden @ Wq.T).reshape(bsz, draft_len, H, HD)
        q = _rms_norm(q, q_norm_w).transpose(0, 2, 1, 3)
        kv_in = jnp.concatenate([context_hidden, draft_hidden], axis=1)
        k = (kv_in @ Wk.T).reshape(bsz, total_len, KVH, HD)
        v = (kv_in @ Wv.T).reshape(bsz, total_len, KVH, HD).transpose(0, 2, 1, 3)
        k = _rms_norm(k, k_norm_w).transpose(0, 2, 1, 3)
        full_position_ids = jnp.concatenate([context_position_ids, draft_position_ids], axis=1)
        q = _rope(q, draft_position_ids)
        k = _rope(k, full_position_ids)
        k = jnp.repeat(k, N_REP, axis=1)
        v = jnp.repeat(v, N_REP, axis=1)
        scores = jnp.einsum('bhqd,bhkd->bhqk', q, k) * SCALE
        probs = jax.nn.softmax(scores, axis=-1)
        attn = jnp.einsum('bhqk,bhkd->bhqd', probs, v)
        attn = attn.transpose(0, 2, 1, 3).reshape(bsz, draft_len, H * HD)
        return attn @ Wo.T

    def _L0_ffn_ref(hidden_states, gate_w, w_gate, w_up, w_down, sw_gate, sw_up, sw_down):
        import jax, jax.numpy as jnp
        import numpy as np
        NUM_EXPERTS = 32
        TOP_K = 6
        N_GROUPS = 4
        N_LIMITED_GROUPS = 2
        B, S, H = hidden_states.shape
        E, K = (NUM_EXPERTS, TOP_K)
        x = hidden_states.reshape(-1, H)
        T = x.shape[0]
        scores = jax.nn.sigmoid(x @ gate_w)
        original_scores = scores
        epg = E // N_GROUPS
        sg = scores.reshape(T, N_GROUPS, epg)
        group_scores = jnp.max(sg, axis=-1)
        _, top_groups = jax.lax.top_k(group_scores, N_LIMITED_GROUPS)
        mask = jnp.ones((T, N_GROUPS), dtype=bool)
        mask = mask.at[jnp.arange(T)[:, None], top_groups].set(False)
        sg = jnp.where(mask[:, :, None], -jnp.inf, sg)
        masked_scores = sg.reshape(T, E)
        _, selected_experts = jax.lax.top_k(masked_scores, K)
        weights = jnp.take_along_axis(original_scores, selected_experts, axis=-1)
        weights = weights / jnp.sum(weights, axis=-1, keepdims=True)
        sel_flat = selected_experts.ravel()
        x_exp = jnp.repeat(x, K, axis=0)
        sort_idx = jnp.argsort(sel_flat)
        xs = x_exp[sort_idx]
        group_sizes = jnp.bincount(sel_flat, length=E).astype(jnp.int32)
        g = jax.lax.ragged_dot(xs, w_gate, group_sizes)
        u = jax.lax.ragged_dot(xs, w_up, group_sizes)
        d = jax.lax.ragged_dot(jax.nn.silu(g) * u, w_down, group_sizes)
        unsort_idx = jnp.argsort(sort_idx)
        out = d[unsort_idx].reshape(T, K, H)
        expert_out = jnp.sum(out * weights[..., None], axis=1)
        shared = jax.nn.silu(x @ sw_gate) * (x @ sw_up) @ sw_down
        return (expert_out + shared).reshape(B, S, H)

    def _L1_xattn_ref(q, kv, seg_id, W_kvc, W_dq, W_uq, W_qr, W_uk, W_kr, W_uv, W_o):
        import jax, jax.numpy as jnp
        import numpy as np
        B, Lq, Lk = (2, 512, 128)
        Q_DIM, KV_DIM = (256, 256)
        H, HD = (16, 128)
        KVC, QC, R = (64, 96, 64)
        LOOKBACK = 8
        NEG = -1e+30

        def _rope(x, L):
            half = x.shape[-1] // 2
            inv_freq = 1.0 / 10000.0 ** (jnp.arange(half, dtype=jnp.float32) / half)
            ang = jnp.arange(L, dtype=jnp.float32)[:, None] * inv_freq
            cos, sin = (jnp.cos(ang), jnp.sin(ang))
            x1, x2 = (x[..., :half], x[..., half:])
            return jnp.concatenate([x1 * cos - x2 * sin, x1 * sin + x2 * cos], axis=-1)
        b, lq, _ = q.shape
        lk = kv.shape[1]
        kv_c = kv @ W_kvc
        q_c = q @ W_dq
        q_nope = (q_c @ W_uq).reshape(b, lq, H, HD).transpose(0, 2, 1, 3)
        q_rope = (q_c @ W_qr).reshape(b, lq, H, R).transpose(0, 2, 1, 3)
        k_nope = (kv_c @ W_uk).reshape(b, lk, H, HD)
        v = (kv_c @ W_uv).reshape(b, lk, H, HD)
        k_rope = kv_c @ W_kr
        q_rope = _rope(q_rope, lq)
        k_rope = _rope(k_rope, lk)
        scale = 1.0 / np.sqrt(HD + R).astype(np.float32)
        scores = (jnp.einsum('bhqd,bkhd->bhqk', q_nope, k_nope) + jnp.einsum('bhqr,bkr->bhqk', q_rope, k_rope)) * scale
        k_ids = jnp.arange(lk)[None, None, :]
        qs = seg_id[:, :, None]
        good = (k_ids <= qs) & (k_ids >= qs - LOOKBACK)
        scores = jnp.where(good[:, None, :, :], scores, NEG)
        attn = jax.nn.softmax(scores, axis=-1)
        out = jnp.einsum('bhqk,bkhd->bqhd', attn, v).reshape(b, lq, H * HD)
        return out @ W_o

    def _L1_ffn_ref(x, gate_w, up_w, down_w, gate_scale, up_scale, down_scale):
        import jax, jax.numpy as jnp
        import numpy as np
        B, S, H, I = (1, 64, 256, 768)

        def _quantized_matmul(x, w, scale):
            wq = w.astype(jnp.float8_e4m3fn).astype(x.dtype)
            y = jnp.einsum('bsi,io->bso', x, wq)
            return y * scale
        gate = jax.nn.silu(_quantized_matmul(x, gate_w, gate_scale))
        up = _quantized_matmul(x, up_w, up_scale)
        fuse = gate * up
        return _quantized_matmul(fuse, down_w, down_scale)
    x = x + _L0_xattn_ref(_layernorm(x, axis=-1), ctx_2048, L0_xattn_Wq, L0_xattn_Wk, L0_xattn_Wv, L0_xattn_Wo, L0_xattn_q_norm_w, L0_xattn_k_norm_w, pos_BxS2, itok_BxS_4096_4607)
    x = x + _L0_ffn_ref(_layernorm(x, axis=-1), L0_ffn_gate_w, L0_ffn_w_gate, L0_ffn_w_up, L0_ffn_w_down, L0_ffn_sw_gate, L0_ffn_sw_up, L0_ffn_sw_down)
    x = x + _L1_xattn_ref(_layernorm(x, axis=-1), ctx_2048, itok_BxS_0_1023, L1_xattn_W_kvc, L1_xattn_W_dq, L1_xattn_W_uq, L1_xattn_W_qr, L1_xattn_W_uk, L1_xattn_W_kr, L1_xattn_W_uv, L1_xattn_W_o)
    x = x + _L1_ffn_ref(_layernorm(x, axis=-1), L1_ffn_gate_w, L1_ffn_up_w, L1_ffn_down_w, L1_ffn_gate_scale, L1_ffn_up_scale, L1_ffn_down_scale)
    return x

_drawn_inputs = setup_inputs


def setup_inputs(seed=0):
    import zlib

    import numpy as np

    out = dict(_drawn_inputs(seed))
    spreads = {'L0_xattn_q_norm_w': (1.0, 0.6), 'L0_xattn_k_norm_w': (1.0, 0.6)}
    factors = {'L0_ffn_gate_w': 8.0,
     'L0_ffn_w_gate': 8.0,
     'L0_ffn_w_up': 8.0,
     'L0_ffn_w_down': 8.0,
     'L0_ffn_sw_gate': 3.329,
     'L0_ffn_sw_up': 3.294,
     'L0_ffn_sw_down': 3.29,
     'L1_ffn_gate_scale': 6.484,
     'L1_ffn_up_scale': 7.586,
     'L1_ffn_down_scale': 7.243}
    for name, (base, spread) in spreads.items():
        noise = np.random.default_rng([zlib.crc32(name.encode()), seed]).standard_normal(out[name].shape)
        drawn = base * np.exp(spread * noise) if base else spread * noise
        out[name] = jnp.asarray(drawn.astype(out[name].dtype))
    for name, factor in factors.items():
        out[name] = (out[name] * factor).astype(out[name].dtype)
    return out
```

```python
import concourse.bass as bass
from concourse import mybir
from contextlib import ExitStack
import numpy as np

F32 = mybir.dt.float32
BF16 = mybir.dt.bfloat16
I32 = mybir.dt.int32
U32 = mybir.dt.uint32
ALU = mybir.AluOpType
ACT = mybir.ActivationFunctionType
AX = mybir.AxisListType

P = 128
B, S, D = 4, 256, 256
TOK = B * S
TT = TOK // P
CTX = 1601
DC = D // P
KVH, REP, HD = 4, 4, 128
NK = S + CTX
KT = -(-NK // P)
KP = KT * P
BANKS = [(k, min(512, NK - k)) for k in range(0, NK, 512)]
NB = len(BANKS)
PAIRS = (KT + 1) // 2
HALF = HD // 2
ROUND = 1.5 * 2 ** 23
TURN = (6.28125, 0.0019340515136718750, 2 * np.pi - 6.28125 - 0.0019340515136718750)
PI_DOWN = float(np.nextafter(np.float32(np.pi), np.float32(0)))
LN_EPS = 1e-5
RMS_EPS = 1e-6
TILES = 2 * REP
GROUPS = B * KVH


class Scope:

    def __init__(self, nc, name):
        self.nc, self.name, self.stack, self.sems = nc, name, ExitStack(), []

    def __enter__(self):
        self.stack.__enter__()
        return self

    def __exit__(self, *a):
        if self.sems:
            self.nc.clear_and_free_semaphores(self.sems)
            self.nc.all_engine_barrier()
        return self.stack.__exit__(*a)

    def sb(self, name, shape, dt=F32):
        return self.stack.enter_context(self.nc.sbuf_tensor(f"{self.name}_{name}", shape, dt))

    def ps(self, name, shape, dt=F32):
        return self.stack.enter_context(self.nc.psum_tensor(f"{self.name}_{name}", shape, dt))

    def sem(self, name):
        self.sems.append(self.nc.alloc_semaphore(name=f"{self.name}_{name}"))
        return self.sems[-1]


def wait(eng, sem, value):
    if not isinstance(value, int) or value > 0:
        eng.wait_ge(sem, value)


def prepare(nc, t):
    with Scope(nc, "prep") as sc:
        x = sc.sb("x", [P, TT, D])
        xh = sc.sb("xhat", [P, TT, D])
        stats = sc.sb("stats", [P, TT, 6])
        mv = sc.sb("mv", [P, TT, 2])
        ident = sc.sb("ident", [P, P])
        kv32 = sc.sb("kv32", [P, 2, DC, KP])
        kvhl = sc.sb("kvhl", [P, 2, 2, DC, KP], BF16)
        w32 = sc.sb("w32", [P, 2, 4096])
        whl = sc.sb("whl", [P, 2, 4096], BF16)
        NA = B * KT * HALF
        pos_i = sc.sb("pos_i", [P, B * KT], I32)
        pos = sc.sb("pos", [P, B * KT])
        invf = sc.sb("invf", [P, HALF])
        ang = sc.sb("ang", [P, B * KT, HALF])
        turn = sc.sb("turn", [P, B * KT, HALF])
        trig = sc.sb("trig", [P, B, 2, KT, HALF])
        nhalf = sc.sb("nhalf", [P, TT])
        xT_ps = [sc.ps(f"xT{i}", [P, DC, P]) for i in range(2)]

        x_in, small_in, kv_in = sc.sem("x_in"), sc.sem("small_in"), [sc.sem(f"kv_in{i}") for i in range(2)]
        w_in = [sc.sem(f"w_in{i}") for i in range(2)]
        kv_out, w_out, t_out = [sc.sem(f"kv_out{i}") for i in range(2)], sc.sem("w_out"), sc.sem("t_out")
        w_hi, w_lo, kv_hi, kv_lo = sc.sem("w_hi"), sc.sem("w_lo"), sc.sem("kv_hi"), sc.sem("kv_lo")
        xT_done, xT_used = sc.sem("xT_done"), sc.sem("xT_used")
        norm, rstd_ready, xhat_ready = sc.sem("norm"), sc.sem("rstd_ready"), sc.sem("xhat_ready")
        ready, table, trig_reduced, trig_ready = sc.sem("ready"), sc.sem("table"), sc.sem("trig_reduced"), sc.sem("trig_ready")

        WEIGHTS = [("wq_l", "wq_s", 4096), ("wkv_l", "wkv_s", 2048), ("wo_l", "wo_s", 4096)]

        with nc.Block() as block:
            @block.sync
            def _(sp):
                sp.dma_start(pos_i[:, :], t["pos_l"]).then_inc(small_in, 16)
                sp.dma_start(invf[:, :], t["invf_l"]).then_inc(small_in, 16)
                sp.dma_start(ident[:, :], t["ident_l"]).then_inc(small_in, 16)
                sp.dma_start(x[:, :, :], t["x_l"]).then_inc(x_in, 16)
                for b in range(2):
                    sp.dma_start(kv32[:, b, :, S:KP], t["ctx_l"][b]).then_inc(kv_in[b], 16)
                for i, (src, _, n) in enumerate(WEIGHTS[:2]):
                    sp.dma_start(w32[:, i, 0:n], t[src]).then_inc(w_in[i], 16)
                for b in range(B):
                    sp.wait_ge(kv_lo, 2 * b + 2)
                    sp.dma_start(t["kv_s"][b], kvhl[:, b % 2, :, :, :].rearrange("p a c k -> p (a c k)")).then_inc(kv_out[b % 2], 16)
                    if b + 2 < B:
                        sp.dma_start(kv32[:, b % 2, :, S:KP], t["ctx_l"][b + 2]).then_inc(kv_in[b % 2], 16)
                    if b == 0:
                        sp.wait_ge(w_lo, 1)
                        sp.dma_start(w32[:, 0, 0:4096], t["wo_l"]).then_inc(w_in[0], 16)
                sp.wait_ge(trig_ready, 2)
                for b in range(B):
                    sp.dma_start(t["tab_s"][b], trig[:, b, :, :, :].rearrange("p a k f -> p (a k f)")).then_inc(t_out, 16)
                for i in range(2):
                    sp.wait_ge(kv_out[i], 16 * (B // 2))
                sp.wait_ge(t_out, 16 * B)

            @block.tensor
            def _(pe):
                pe.wait_ge(small_in, 48)
                for n in range(TT):
                    pe.wait_ge(xhat_ready, n + 1)
                    wait(pe, xT_used, n - 1)
                    for c in range(DC):
                        last = nc.tensor.transpose(xT_ps[n % 2][:, c, :], xh[:, n, c * P:(c + 1) * P], ident[:, :])
                    last.then_inc(xT_done, 1)

            @block.scalar
            def _(act):
                for i, (_, dst, n) in enumerate(WEIGHTS):
                    act.wait_ge(w_in[i % 2], 16 * (i // 2 + 1))
                    wait(act, w_out, 32 * i)
                    nc.scalar.activation(whl[:, 0, 0:n], w32[:, i % 2, 0:n], ACT.Copy).then_inc(w_hi, 1)
                    act.wait_ge(w_hi, i + 1)
                    act.wait_ge(w_lo, i + 1)
                    dram = t[dst].rearrange("g p a n -> a p g n")
                    for a in range(2):
                        act.dma_start(dram[a], whl[:, a, 0:n].rearrange("p (g n) -> p g n", g=4)).then_inc(w_out, 16)
                    if i == 0:
                        for cosine in (0, 1):
                            act.wait_ge(trig_reduced, cosine + 1)
                            row = trig[:, :, 1 - cosine, :, :].rearrange("p b k f -> p b (k f)")
                            nc.scalar.activation(row, row, ACT.Sin).then_inc(trig_ready, 1)
                        for b in range(B):
                            for n2 in (2 * b, 2 * b + 1):
                                act.wait_ge(xT_done, n2 + 1)
                                if b >= 2:
                                    act.wait_ge(kv_lo, 2 * b - 2)
                                o = (n2 % 2) * P
                                nc.scalar.activation(kv32[:, b % 2, :, o:o + P], xT_ps[n2 % 2][:, :, :], ACT.Copy).then_inc(xT_used, 1)
                            act.wait_ge(kv_in[b % 2], 16 * (b // 2 + 1))
                            act.wait_ge(xT_used, 2 * b + 2)
                            wait(act, kv_out[b % 2], 16 * (b // 2))
                            for c in range(DC):
                                nc.scalar.activation(kvhl[:, b % 2, 0, c, :], kv32[:, b % 2, c, :], ACT.Copy).then_inc(kv_hi, 1)
                act.wait_ge(w_out, 32 * len(WEIGHTS))

            @block.gpsimd
            def _(pool):
                nc.gpsimd.memset(nhalf[:, :], -0.5).then_inc(ready, 1)
                pool.wait_ge(ready, 1)
                pool.wait_ge(norm, 2 * TT + 1)
                nc.gpsimd.tensor_tensor(mv[:, :, 1], mv[:, :, 1], nhalf[:, :], ALU.pow).then_inc(rstd_ready, 1)
                for i, (_, _, n) in enumerate(WEIGHTS):
                    pool.wait_ge(w_hi, i + 1)
                    nc.gpsimd.tensor_tensor(whl[:, 1, 0:n], w32[:, i % 2, 0:n], whl[:, 0, 0:n], ALU.subtract).then_inc(w_lo, 1)

            @block.vector
            def _(dve):
                dve.wait_ge(x_in, 16)
                for n in range(TT):
                    nc.vector.bn_stats(stats[:, n, :], x[:, n, :]).then_inc(norm, 1)
                for n in range(TT):
                    dve.wait_ge(norm, n + 1)
                    nc.vector.bn_aggr(mv[:, n, :], stats[:, n, :]).then_inc(norm, 1)
                dve.wait_ge(norm, 2 * TT)
                nc.vector.tensor_scalar(mv[:, :, 1], mv[:, :, 1], LN_EPS, None, ALU.add).then_inc(norm, 1)
                dve.wait_ge(rstd_ready, 1)
                for n in range(TT):
                    nc.vector.tensor_scalar(xh[:, n, :], x[:, n, :], mv[:, n, 0:1], mv[:, n, 1:2], ALU.subtract, ALU.mult).then_inc(xhat_ready, 1)
                dve.wait_ge(small_in, 48)
                steps = [0]

                def link(ins):
                    steps[0] += 1
                    ins.then_inc(table, 1)
                    dve.wait_ge(table, steps[0])

                link(nc.vector.tensor_copy(pos[:, :], pos_i[:, :]))
                link(nc.vector.tensor_tensor(ang[:, :, :], pos[:, :].unsqueeze(2).to_broadcast([P, B * KT, HALF]),
                                             invf[:, :].unsqueeze(1).to_broadcast([P, B * KT, HALF]), ALU.mult))
                angle = ang[:, :, :].rearrange("p (b k) f -> p b (k f)", b=B)
                turns = turn[:, :, :].rearrange("p (b k) f -> p b (k f)", b=B)
                for cosine in (0, 1):
                    red = trig[:, :, 1 - cosine, :, :].rearrange("p b k f -> p b (k f)")
                    link(nc.vector.tensor_scalar(turns, angle, 1 / (2 * np.pi), 0.25 * cosine, ALU.mult, ALU.add))
                    link(nc.vector.tensor_scalar(turns, turns, ROUND, -ROUND, ALU.add, ALU.add))
                    link(nc.vector.scalar_tensor_tensor(red, turns, -TURN[0], angle, ALU.mult, ALU.add))
                    link(nc.vector.scalar_tensor_tensor(red, turns, -TURN[1], red, ALU.mult, ALU.add))
                    link(nc.vector.scalar_tensor_tensor(red, turns, -TURN[2], red, ALU.mult, ALU.add))
                    link(nc.vector.tensor_scalar(red, red, cosine * np.pi / 2, PI_DOWN, ALU.add, ALU.min))
                    nc.vector.tensor_scalar(red, red, -PI_DOWN, None, ALU.max).then_inc(trig_reduced, 1)
                for b in range(B):
                    for c in range(DC):
                        dve.wait_ge(kv_hi, 2 * b + c + 1)
                        nc.vector.tensor_tensor(kvhl[:, b % 2, 1, c, :], kv32[:, b % 2, c, :], kvhl[:, b % 2, 0, c, :], ALU.subtract).then_inc(kv_lo, 1)


SLOTS = [
    ([], [("KV", 0)], [("KV", 1)]),
    ([("AT-", 1)], [("KV", 2)], [("WO-", 1)]),
    ([], [("Q", 0)], [("KV", 3)]),
    ([], [("Q", 1)], [("KV", 4)]),
    ([("KT", 0)], [("KV", 5)], [("QT", 0)]),
    ([("AT", 0)], [("KV", 6)], [("WO", 0)]),
    ([("KT", 1)], [("KV", 7)], [("QT", 1)]),
    ([], [("KT", 2)], [("KT", 3)]),
]
FIRST_GROUP = [("KV", 0), ("KV", 1), ("KV", 2), ("Q", 0), ("KV", 3), ("Q", 1), ("KV", 4), ("KV", 5), ("KV", 6),
               ("KV", 7), ("QT", 0), ("QT", 1), ("KT", 0), ("KT", 1), ("KT", 2), ("KT", 3)]
POOL_ORDER = [x for x in FIRST_GROUP if x[0] in ("KV", "Q")]
PER_GROUP = {"KV": PAIRS, "Q": 2, "KT": NB, "QT": 2, "AT": 2, "WO": 2}
ROPE_STEPS = 8


def tasks_of(place, prep, first, last):
    found = []
    for kind, n in place:
        if kind[-1] == "-":
            if not first:
                found.append((kind[:-1], n, -1))
        elif kind in ("AT", "WO"):
            if not last:
                found.append((kind, n, 0))
        elif prep:
            found.append((kind, n, 1))
    return found


def attend(nc, t, x, groups=GROUPS):
    with Scope(nc, "att") as sc:
        kvT = sc.sb("kvT", [P, 2, 2, DC, KP], BF16)
        tab = sc.sb("tab", [P, 2, 2, KT, HALF])
        wkv = sc.sb("wkv", [P, 2, 2, DC, 2 * HD], BF16)
        wq = sc.sb("wq", [P, 2, 2, DC, REP * HD], BF16)
        wo = sc.sb("wo", [P, 2, 2, REP, D], BF16)
        kw, qw, ident = sc.sb("kw", [P, HD]), sc.sb("qw", [P, HD]), sc.sb("ident", [P, P])
        nhalf = sc.sb("nhalf", [P, REP])
        eps = sc.sb("eps", [P, 2, REP])
        kvraw = sc.sb("kvraw", [P, 4, 2, 2 * HD])
        qraw = sc.sb("qraw", [P, 2, REP, HD])
        kjunk = sc.sb("kjunk", [P, 4, 2, HD], BF16)
        qjunk = sc.sb("qjunk", [P, 2, REP, HD], BF16)
        kss, qss = sc.sb("kss", [P, 4, 2]), sc.sb("qss", [P, 2, REP])
        scaled, cosd, sind = (sc.sb(n, [P, REP, HD]) for n in ("scaled", "cosd", "sind"))
        rs = sc.sb("rs", [P, REP])
        kp = sc.sb("kp", [P, 2 * PAIRS, HD])
        qp = sc.sb("qp", [P, 2, REP, HD])
        K = sc.sb("K", [P, 2, 2, KP], BF16)
        V = sc.sb("V", [P, 2, KT, 2, HD], BF16)
        Q = sc.sb("Q", [P, 2, 2, TILES, P], BF16)
        mx = sc.sb("mx", [P, 2, NB])
        negmax = sc.sb("negmax", [P, 4])
        es = sc.sb("es", [P, 4, NB])
        rsum, rinv = sc.sb("rsum", [P, 4]), sc.sb("rinv", [P, 4])
        prob = sc.sb("prob", [P, 2, KP])
        pT = sc.sb("pT", [P, 2, 2, KT, P], BF16)
        attn = sc.sb("attn", [P, TILES, HD])
        aT = sc.sb("aT", [P, 2, 2, REP, P], BF16)

        scores = sc.ps("scores", [P, NB * 512])
        pT_ps = [sc.ps(f"pT{i}", [P, 4, P]) for i in range(2)]
        out_ps = sc.ps("out", [P, 2, HD])
        aux = sc.ps("aux", [P, 512])

        names = ["const", "pad", "kv_done", "kvraw_ready", "vhi_ready", "k_ss", "v_lo", "q_done", "qraw_ready", "q_ss",
                 "kt_done", "kt_hi", "kt_lo", "qt_done", "qt_hi", "qt_lo", "at_done", "at_hi", "at_lo",
                 "wo_done", "x_added", "kp_done", "qp_done", "rope", "qk_done", "bank_max", "negmax_ready",
                 "exp_done", "pt_done", "pt_hi", "pt_lo", "pv_done", "sum_ready", "rinv_ready", "o_done"]
        s = {n: sc.sem(n) for n in names}
        load = [sc.sem(f"load{i}") for i in range(2)]
        wo_load = [sc.sem(f"wo_load{i}") for i in range(2)]
        DONE = {"KV": "kv_done", "Q": "q_done", "KT": "kt_done", "QT": "qt_done", "AT": "at_done", "WO": "wo_done"}
        FREE = {"KV": "kvraw_ready", "Q": "qraw_ready", "KT": "kt_lo", "QT": "qt_lo", "AT": "at_lo", "WO": "x_added"}

        def nth(kind, n, g):
            return PER_GROUP[kind] * g + n + 1

        def pair(j):
            return min(2, KT - 2 * j)

        def quad(i):
            return min(4, KT - 4 * i)

        def each_group(eng, group, tail):
            group(0, 0, True, groups > 1)
            group(1, 1, False, groups > 2)
            if groups > 4:
                with eng.Fori(1, groups // 2 - 1) as p:
                    group(2 * p, 0, False, True)
                    group(2 * p + 1, 1, False, True)
            if groups > 2:
                group(groups - 2, 0, False, True)
                group(groups - 1, 1, False, False)
            tail(groups)

        with nc.Block() as block:
            @block.sync
            def _(sp):
                for dst, src in ((kw, "kw_l"), (qw, "qw_l"), (ident, "ident_l")):
                    sp.dma_start(dst[:, :], t[src]).then_inc(s["const"], 16)

                def load_group(n, par, b, h):
                    if not isinstance(n, int) or n >= 2:
                        sp.wait_ge(s["kp_done"], nth("KV", PAIRS - 1, n - 2))
                        sp.wait_ge(s["qp_done"], nth("Q", 1, n - 2))
                    for dst, src in ((kvT[:, par, :, :, :].rearrange("p a c k -> p (a c k)"), t["kv_s"][b]),
                                     (tab[:, par, :, :, :].rearrange("p a k f -> p (a k f)"), t["tab_s"][b]),
                                     (wkv[:, par, :, :, :].rearrange("p a c n -> p (a c n)"), t["wkv_s"][h]),
                                     (wq[:, par, :, :, :].rearrange("p a c n -> p (a c n)"), t["wq_s"][h])):
                        sp.dma_start(dst, src).then_inc(load[par], 16)
                    if not isinstance(n, int) or n >= 2:
                        sp.wait_ge(s["wo_done"], nth("WO", 1, n - 2))
                    sp.dma_start(wo[:, par, :, :, :].rearrange("p a h n -> p (a h n)"), t["wo_s"][h]).then_inc(wo_load[par], 16)

                load_group(0, 0, 0, 0)
                load_group(1, 1, 0, 1)
                if groups > 2:
                    with sp.Fori(1, groups // 2) as p:
                        for u in range(2):
                            load_group(2 * p + u, u, p // 2, 2 * (p % 2) + u)

            @block.tensor
            def _(pe):
                before = []

                def task(kind, n, ahead, g, u):
                    gt = g + ahead
                    par = (u + ahead) % 2
                    if before:
                        bk, bn, bg = before.pop()
                        wait(pe, s[FREE[bk]], nth(bk, bn, bg))
                    before.append((kind, n, gt))
                    if kind == "KV":
                        if n == 0:
                            pe.wait_ge(load[par], 64 * ((gt - par) // 2 + 1 if isinstance(gt, int) else gt // 2 + 1))
                        for m in range(pair(n)):
                            o = aux[:, m * 256:(m + 1) * 256]
                            k0 = (2 * n + m) * P
                            for c in range(DC):
                                for a, w in ((0, 0), (0, 1), (1, 0)):
                                    last = nc.tensor.matmul(o, kvT[:, par, a, c, k0:k0 + P], wkv[:, par, w, c, :],
                                                            start=(c, a, w) == (0, 0, 0), stop=(c, a) == (DC - 1, 1))
                    elif kind == "Q":
                        for c in range(DC):
                            for a, w in ((0, 0), (0, 1), (1, 0)):
                                last = nc.tensor.matmul(aux[:, :], kvT[:, par, a, c, n * P:(n + 1) * P], wq[:, par, w, c, :],
                                                        start=(c, a, w) == (0, 0, 0), stop=(c, a) == (DC - 1, 1))
                    elif kind == "KT":
                        pe.wait_ge(s["kp_done"], nth("KV", min(2 * n + 1, PAIRS - 1), gt))
                        for m in range(quad(n)):
                            last = nc.tensor.transpose(aux[:, m * P:(m + 1) * P], kp[:, 4 * n + m, :], ident[:, :])
                    elif kind == "QT":
                        pe.wait_ge(s["qp_done"], nth("Q", n, gt))
                        for m in range(REP):
                            last = nc.tensor.transpose(aux[:, m * P:(m + 1) * P], qp[:, n, m, :], ident[:, :])
                    elif kind == "AT":
                        pe.wait_ge(s["o_done"], TILES * gt + 4 * n + 4)
                        for m in range(REP):
                            last = nc.tensor.transpose(aux[:, m * P:(m + 1) * P], attn[:, 4 * n + m, :], ident[:, :])
                    else:
                        if n == 0:
                            pe.wait_ge(wo_load[par], 16 * (gt // 2 + 1))
                        pe.wait_ge(s["at_lo"], nth("AT", n, gt))
                        for m in range(REP):
                            for a, w in ((0, 0), (0, 1), (1, 0)):
                                last = nc.tensor.matmul(aux[:, 0:D], aT[:, n, a, m, :], wo[:, par, w, m, :],
                                                        start=(m, a, w) == (0, 0, 0), stop=(m, a) == (REP - 1, 1))
                    last.then_inc(s[DONE[kind]], 1)

                def form_scores(g, u, i):
                    tile = TILES * g + i
                    if i == 0:
                        pe.wait_ge(s["qt_lo"], nth("QT", 1, g))
                    for k, (lo, n) in enumerate(BANKS):
                        if i == 0:
                            pe.wait_ge(s["kt_lo"], nth("KT", k, g))
                        wait(pe, s["exp_done"], NB * (tile - 1) + k + 1)
                        for a, w in ((0, 0), (0, 1), (1, 0)):
                            last = nc.tensor.matmul(scores[:, lo:lo + n], Q[:, u, a, i, :], K[:, u, w, lo:lo + n],
                                                    start=(a, w) == (0, 0), stop=a == 1)
                        last.then_inc(s["qk_done"], 1)

                def turn_probs(tile, i, j):
                    wait(pe, s["exp_done"], NB * tile + j + 1)
                    wait(pe, s["pt_lo"], NB * tile + j - 1)
                    for m in range(quad(j)):
                        k0 = (4 * j + m) * P
                        last = nc.tensor.transpose(pT_ps[j % 2][:, m, :], prob[:, i % 2, k0:k0 + P], ident[:, :])
                    last.then_inc(s["pt_done"], 1)

                def apply_values(tile, i, j, g, par):
                    if i == 0 and j == 0:
                        pe.wait_ge(s["v_lo"], nth("KV", PAIRS - 1, g))
                    if j == 0:
                        wait(pe, s["o_done"], tile)
                    pe.wait_ge(s["pt_lo"], NB * tile + j + 1)
                    for m in range(quad(j)):
                        k = 4 * j + m
                        for a, w in ((0, 0), (0, 1), (1, 0)):
                            last = nc.tensor.matmul(out_ps[:, i % 2, :], pT[:, i % 2, a, k, :], V[:, par, k, w, :],
                                                    start=(k, a, w) == (0, 0, 0), stop=(k, a) == (KT - 1, 1))
                    if j == NB - 1:
                        last.then_inc(s["pv_done"], 1)

                def slot(i, g, u, first, prep, last):
                    ahead, amid, behind = (tasks_of(place, prep, first, last) for place in SLOTS[i])
                    old = not (first and i == 0) and not (last and i > 0)
                    tile, oi = TILES * g + i - 1, (i - 1) % TILES
                    og, opar = (g, u) if i else (g - 1, 1 - u)
                    if old:
                        turn_probs(tile, oi, 0)
                        turn_probs(tile, oi, 1)
                    if not last:
                        form_scores(g, u, i)
                    for x_ in ahead:
                        task(*x_, g, u)
                    if old:
                        apply_values(tile, oi, 0, og, opar)
                        turn_probs(tile, oi, 2)
                        apply_values(tile, oi, 1, og, opar)
                        turn_probs(tile, oi, 3)
                    for x_ in amid:
                        task(*x_, g, u)
                    if old:
                        apply_values(tile, oi, 2, og, opar)
                        apply_values(tile, oi, 3, og, opar)
                    for x_ in behind:
                        task(*x_, g, u)

                def group(g, u, first, prep):
                    if before:
                        bk, bn, _ = before.pop()
                        before.append((bk, bn, g if bk in ("KT", "QT", "KV", "Q") else g - 1))
                    for i in range(TILES):
                        slot(i, g, u, first, prep, False)

                def tail(g):
                    bk, bn, _ = before.pop()
                    before.append((bk, bn, g - 1))
                    for i in range(3):
                        slot(i, g, 0, False, False, True)

                pe.wait_ge(s["const"], 48)
                for kind, n in FIRST_GROUP:
                    task(kind, n, 0, 0, 0)
                each_group(pe, group, tail)

            def halves(kind, n, gt, par):
                if kind == "KT":
                    return [K[:, par, a, 512 * n:512 * n + P * quad(n)] for a in range(2)]
                if kind == "QT":
                    return [Q[:, par, a, REP * n:REP * n + REP, :].rearrange("p h q -> p (h q)") for a in range(2)]
                return [aT[:, n, a, :, :].rearrange("p h q -> p (h q)") for a in range(2)]

            @block.scalar
            def _(act):
                def task(kind, n, ahead, g, u):
                    gt = g + ahead
                    par = (u + ahead) % 2
                    if kind == "WO":
                        return
                    act.wait_ge(s[DONE[kind]], nth(kind, n, gt))
                    if kind == "KV":
                        m = pair(n)
                        bank = aux[:, :].rearrange("p (m k) -> p m k", m=2)
                        wait(act, s["kp_done"], nth("KV", n, gt) - 4)
                        wait(act, s["v_lo"], nth("KV", n, gt) - 4)
                        nc.scalar.activation(kvraw[:, n % 4, 0:m, :], bank[:, 0:m, :], ACT.Copy).then_inc(s["kvraw_ready"], 1)
                        if n == 0:
                            wait(act, s["pv_done"], TILES * (gt - 1))
                        act.wait_ge(s["kvraw_ready"], nth("KV", n, gt))
                        nc.scalar.activation(V[:, par, 2 * n:2 * n + m, 0, :], kvraw[:, n % 4, 0:m, HD:2 * HD], ACT.Copy).then_inc(s["vhi_ready"], 1)
                    elif kind == "Q":
                        wait(act, s["qp_done"], nth("Q", n, gt - 1))
                        nc.scalar.activation(qraw[:, n, :, :].rearrange("p h d -> p (h d)"), aux[:, :], ACT.Copy).then_inc(s["qraw_ready"], 1)
                    else:
                        hi, _ = halves(kind, n, gt, par)
                        nc.scalar.activation(hi, aux[:, 0:hi.shape[-1]], ACT.Copy).then_inc(s[kind.lower() + "_hi"], 1)

                def probs_high(tile, i, j):
                    act.wait_ge(s["pt_done"], NB * tile + j + 1)
                    m = quad(j)
                    nc.scalar.activation(pT[:, i % 2, 0, 4 * j:4 * j + m, :], pT_ps[j % 2][:, 0:m, :], ACT.Copy).then_inc(s["pt_hi"], 1)

                def exponent(tile, i, k):
                    if k == 0:
                        act.wait_ge(s["negmax_ready"], tile + 1)
                    lo, n = BANKS[k]
                    nc.scalar.activation(prob[:, i % 2, lo:lo + n], scores[:, lo:lo + n], ACT.Exp, bias=negmax[:, i % 4:i % 4 + 1],
                                         scale=1.0, accum_out=es[:, i % 4, k:k + 1]).then_inc(s["exp_done"], 1)

                def output(tile, i):
                    act.wait_ge(s["pv_done"], tile + 1)
                    act.wait_ge(s["rinv_ready"], tile + 1)
                    nc.scalar.activation(attn[:, i, :], out_ps[:, i % 2, :], ACT.Copy, scale=rinv[:, i % 4:i % 4 + 1]).then_inc(s["o_done"], 1)

                def slot(i, g, u, first, prep, last):
                    ahead, amid, behind = (tasks_of(place, prep, first, last) for place in SLOTS[i])
                    tile, oi = TILES * g + i, (i - 1) % TILES
                    old = not (first and i == 0) and not (last and i > 0)
                    if not (first and i < 2) and not (last and i > 1):
                        output(tile - 2, (i - 2) % TILES)
                    if old:
                        probs_high(tile - 1, oi, 0)
                        probs_high(tile - 1, oi, 1)
                    for x_ in ahead:
                        task(*x_, g, u)
                    if old:
                        probs_high(tile - 1, oi, 2)
                    if not last:
                        exponent(tile, i, 0)
                    if old:
                        probs_high(tile - 1, oi, 3)
                    if not last:
                        exponent(tile, i, 1)
                    for x_ in amid:
                        task(*x_, g, u)
                    if not last:
                        exponent(tile, i, 2)
                        exponent(tile, i, 3)
                    for x_ in behind:
                        task(*x_, g, u)

                act.wait_ge(s["pad"], 4)
                for kind, n in FIRST_GROUP:
                    task(kind, n, 0, 0, 0)
                each_group(act, lambda g, u, first, prep: [slot(i, g, u, first, prep, False) for i in range(TILES)],
                           lambda g: [slot(i, g, 0, False, False, True) for i in range(3)])

            @block.vector
            def _(dve):
                def task(kind, n, ahead, g, u):
                    gt = g + ahead
                    par = (u + ahead) % 2
                    if kind == "KV":
                        m = pair(n)
                        dve.wait_ge(s["kvraw_ready"], nth("KV", n, gt))
                        for q in range(m):
                            k_rows = kvraw[:, n % 4, q, 0:HD]
                            last = nc.vector.scalar_tensor_tensor(kjunk[:, n % 4, q, :], k_rows, 1.0 / HD, k_rows,
                                                                  ALU.mult, ALU.mult, accum_out=kss[:, n % 4, q:q + 1])
                        last.then_inc(s["k_ss"], 1)
                        dve.wait_ge(s["vhi_ready"], nth("KV", n, gt))
                        nc.vector.tensor_tensor(V[:, par, 2 * n:2 * n + m, 1, :], kvraw[:, n % 4, 0:m, HD:2 * HD], V[:, par, 2 * n:2 * n + m, 0, :],
                                                ALU.subtract).then_inc(s["v_lo"], 1)
                    elif kind == "Q":
                        dve.wait_ge(s["qraw_ready"], nth("Q", n, gt))
                        for q in range(REP):
                            last = nc.vector.scalar_tensor_tensor(qjunk[:, n, q, :], qraw[:, n, q, :], 1.0, qraw[:, n, q, :],
                                                                  ALU.mult, ALU.mult, accum_out=qss[:, n, q:q + 1])
                        last.then_inc(s["q_ss"], 1)
                    elif kind == "WO":
                        dve.wait_ge(s["wo_done"], nth("WO", n, gt))
                        tile = 2 * (gt // KVH) + n
                        acc = x[:, tile, :] if isinstance(tile, int) else x[:, bass.ds(tile, 1), :].rearrange("p a d -> p (a d)")
                        nc.vector.tensor_tensor(acc, aux[:, 0:D], acc, ALU.add).then_inc(s["x_added"], 1)
                    else:
                        hi, lo = halves(kind, n, gt, par)
                        dve.wait_ge(s[kind.lower() + "_hi"], nth(kind, n, gt))
                        nc.vector.tensor_tensor(lo, aux[:, 0:hi.shape[-1]], hi, ALU.subtract).then_inc(s[kind.lower() + "_lo"], 1)

                def row_max(tile, i):
                    for k, (lo, n) in enumerate(BANKS):
                        dve.wait_ge(s["qk_done"], NB * tile + k + 1)
                        nc.vector.reduce_max(mx[:, i % 2, k:k + 1], scores[:, lo:lo + n], AX.X).then_inc(s["bank_max"], 1)
                    dve.wait_ge(s["bank_max"], NB * tile + NB)
                    nc.vector.tensor_reduce(negmax[:, i % 4:i % 4 + 1], mx[:, i % 2, :], AX.X, ALU.max, negate=True).then_inc(s["negmax_ready"], 1)

                def row_sum(tile, i):
                    dve.wait_ge(s["exp_done"], NB * tile + NB)
                    nc.vector.reduce_sum(rsum[:, i % 4:i % 4 + 1], es[:, i % 4, :], AX.X).then_inc(s["sum_ready"], 1)
                    dve.wait_ge(s["sum_ready"], tile + 1)
                    nc.vector.reciprocal(rinv[:, i % 4:i % 4 + 1], rsum[:, i % 4:i % 4 + 1]).then_inc(s["rinv_ready"], 1)

                def probs_low(tile, i, j):
                    dve.wait_ge(s["pt_hi"], NB * tile + j + 1)
                    m = quad(j)
                    nc.vector.tensor_tensor(pT[:, i % 2, 1, 4 * j:4 * j + m, :], pT_ps[j % 2][:, 0:m, :], pT[:, i % 2, 0, 4 * j:4 * j + m, :],
                                            ALU.subtract).then_inc(s["pt_lo"], 1)

                def slot(i, g, u, first, prep, last):
                    ahead, amid, behind = (tasks_of(place, prep, first, last) for place in SLOTS[i])
                    tile, oi = TILES * g + i, (i - 1) % TILES
                    old = not (first and i == 0) and not (last and i > 0)
                    if old:
                        probs_low(tile - 1, oi, 0)
                        probs_low(tile - 1, oi, 1)
                    if not last:
                        row_max(tile, i)
                    if old:
                        row_sum(tile - 1, oi)
                    for x_ in ahead:
                        task(*x_, g, u)
                    if old:
                        probs_low(tile - 1, oi, 2)
                        probs_low(tile - 1, oi, 3)
                    for x_ in amid + behind:
                        task(*x_, g, u)

                dve.wait_ge(s["pad"], 4)
                for kind, n in FIRST_GROUP:
                    task(kind, n, 0, 0, 0)
                each_group(dve, lambda g, u, first, prep: [slot(i, g, u, first, prep, False) for i in range(TILES)],
                           lambda g: [slot(i, g, 0, False, False, True) for i in range(3)])

            @block.gpsimd
            def _(pool):
                def rope(order, kind, n, g, par):
                    base = ROPE_STEPS * (len(POOL_ORDER) * g + order)
                    gps = nc.gpsimd

                    def step(k):
                        pool.wait_ge(s["rope"], base + k)

                    if kind == "KV":
                        m, raw, weight, ss, out = pair(n), kvraw[:, n % 4, :, 0:HD], kw, kss[:, n % 4, :], kp[:, 2 * n:2 * n + pair(n), :]
                        cos, sin = (tab[:, par, a, 2 * n:2 * n + m, :] for a in range(2))
                        shape = [P, m, HALF]
                        pool.wait_ge(s["kvraw_ready"], nth("KV", n, g))
                    else:
                        m, raw, weight, ss, out = REP, qraw[:, n, :, :], qw, qss[:, n, :], qp[:, n, :, :]
                        shape = [P, m, HALF]
                        cos, sin = (tab[:, par, a, n:n + 1, :].to_broadcast(shape) for a in range(2))
                        pool.wait_ge(s["qraw_ready"], nth("Q", n, g))
                    a, b, c = scaled[:, 0:m, :], cosd[:, 0:m, :], sind[:, 0:m, :]
                    gps.tensor_tensor(a, raw[:, 0:m, :], weight[:, :].unsqueeze(1).to_broadcast([P, m, HD]), ALU.mult).then_inc(s["rope"], 1)
                    step(1)
                    gps.tensor_tensor(b.rearrange("p m (e f) -> p m e f", e=2), a.rearrange("p m (e f) -> p m e f", e=2),
                                      cos.unsqueeze(2).to_broadcast([P, m, 2, HALF]), ALU.mult).then_inc(s["rope"], 1)
                    gps.tensor_tensor(c[:, :, 0:HALF], a[:, :, HALF:HD], sin, ALU.mult).then_inc(s["rope"], 1)
                    gps.tensor_tensor(c[:, :, HALF:HD], a[:, :, 0:HALF], sin, ALU.mult).then_inc(s["rope"], 1)
                    pool.wait_ge(s["k_ss" if kind == "KV" else "q_ss"], nth(kind, n, g))
                    gps.tensor_tensor(rs[:, 0:m], ss[:, 0:m], eps[:, 0 if kind == "KV" else 1, 0:m], ALU.add).then_inc(s["rope"], 1)
                    step(3)
                    gps.tensor_tensor(b[:, :, 0:HALF], b[:, :, 0:HALF], c[:, :, 0:HALF], ALU.subtract).then_inc(s["rope"], 1)
                    step(5)
                    gps.tensor_tensor(rs[:, 0:m], rs[:, 0:m], nhalf[:, 0:m], ALU.pow).then_inc(s["rope"], 1)
                    gps.tensor_tensor(b[:, :, HALF:HD], b[:, :, HALF:HD], c[:, :, HALF:HD], ALU.add).then_inc(s["rope"], 1)
                    step(8)
                    if kind == "KV":
                        wait(pool, s["kt_done"], nth("KT", n // 2, g - 1))
                    else:
                        wait(pool, s["qt_done"], nth("QT", n, g - 1))
                    gps.tensor_tensor(out, b, rs[:, 0:m].unsqueeze(2).to_broadcast([P, m, HD]), ALU.mult)\
                        .then_inc(s["kp_done" if kind == "KV" else "qp_done"], 1)

                def prep(g, par):
                    pool.wait_ge(load[par], 64 * (g // 2 + 1))
                    for order, (kind, n) in enumerate(POOL_ORDER):
                        rope(order, kind, n, g, par)

                nc.gpsimd.memset(nhalf[:, :], -0.5).then_inc(s["pad"], 1)
                nc.gpsimd.memset(prob[:, :, NK:KP], 0.0).then_inc(s["pad"], 1)
                nc.gpsimd.memset(eps[:, 0, :], RMS_EPS).then_inc(s["pad"], 1)
                nc.gpsimd.memset(eps[:, 1, :], RMS_EPS * HD).then_inc(s["pad"], 1)
                pool.wait_ge(s["pad"], 4)
                pool.wait_ge(s["const"], 48)
                prep(0, 0)
                prep(1, 1)
                if groups > 2:
                    with pool.Fori(1, groups // 2) as p:
                        prep(2 * p, 0)
                        prep(2 * p + 1, 1)


H1, HD1, KVC, QC, R1 = 16, 128, 64, 96, 64
LOOKBACK = 8
WIN = LOOKBACK + 1
ROW = KVC + R1
CT = -(-CTX // P)
TAB_ROWS = CTX + 1
BQ = P // H1
BLOCKS = TOK // BQ
BK = BQ * WIN
STEP_BLOCKS = 4
NEG = -1e30
SCALE1 = 1.0 / float(np.sqrt(np.float32(HD1 + R1)))
RH = R1 // 2
NSTEP = BLOCKS // STEP_BLOCKS

FI = 768
FC = FI // P
E4M3_MAX = 448.0
QUANT_STEPS = 10

E_ALL, TOPK, GRP, TOP_GRP = 32, 6, 4, 2
M = 176
EXPERTS = E_ALL + 2
UP_ROWS = [(0, 64), (64, 64), (128, M - 128)]
UP_COLS = [(0, 128), (128, 128), (256, 64 + M - 128)]
UPW = UP_COLS[-1][0] + UP_COLS[-1][1]
SPAN = 512
STEPS = TOK // SPAN
assert NSTEP == EXPERTS - 2


def normalize(nc, t, name, x, hhl, h32=None):
    with Scope(nc, name) as sc:
        xn = sc.sb("xn", [P, TT, D])
        stats, mv, nhalf, ident = sc.sb("stats", [P, TT, 6]), sc.sb("mv", [P, TT, 2]), sc.sb("nhalf", [P, TT]), sc.sb("ident", [P, P])
        ps = [sc.ps(f"t{i}", [P, DC, P]) for i in range(4)]
        names = ["ident_in", "half_set", "stat", "var_ready", "rstd_ready", "xn_ready", "t_done", "t_f32", "t_hi", "t_lo"]
        s = {n: sc.sem(n) for n in names}
        with nc.Block() as block:
            @block.sync
            def _(sp):
                sp.dma_start(ident[:, :], t["ident_l"]).then_inc(s["ident_in"], 16)

            @block.gpsimd
            def _(pool):
                nc.gpsimd.memset(nhalf[:, :], -0.5).then_inc(s["half_set"], 1)
                pool.wait_ge(s["half_set"], 1)
                pool.wait_ge(s["var_ready"], 1)
                nc.gpsimd.tensor_tensor(mv[:, :, 1], mv[:, :, 1], nhalf[:, :], ALU.pow).then_inc(s["rstd_ready"], 1)

            @block.tensor
            def _(pe):
                pe.wait_ge(s["ident_in"], 16)
                for n in range(TT):
                    pe.wait_ge(s["xn_ready"], n + 1)
                    wait(pe, s["t_lo"], n - 3)
                    for c in range(DC):
                        last = nc.tensor.transpose(ps[n % 4][:, c, :], xn[:, n, c * P:(c + 1) * P], ident[:, :])
                    last.then_inc(s["t_done"], 1)

            @block.scalar
            def _(act):
                for n in range(TT):
                    act.wait_ge(s["t_done"], n + 1)
                    if h32 is not None:
                        nc.scalar.activation(h32[:, :, n * P:(n + 1) * P], ps[n % 4][:, :, :], ACT.Copy)
                    nc.scalar.activation(hhl[:, 0, :, n * P:(n + 1) * P], ps[n % 4][:, :, :], ACT.Copy).then_inc(s["t_hi"], 1)

            @block.vector
            def _(dve):
                for n in range(TT):
                    nc.vector.bn_stats(stats[:, n, :], x[:, n, :]).then_inc(s["stat"], 1)
                for n in range(TT):
                    dve.wait_ge(s["stat"], n + 1)
                    nc.vector.bn_aggr(mv[:, n, :], stats[:, n, :]).then_inc(s["stat"], 1)
                dve.wait_ge(s["stat"], 2 * TT)
                nc.vector.tensor_scalar(mv[:, :, 1], mv[:, :, 1], LN_EPS, None, ALU.add).then_inc(s["var_ready"], 1)
                dve.wait_ge(s["rstd_ready"], 1)
                for n in range(TT):
                    nc.vector.tensor_scalar(xn[:, n, :], x[:, n, :], mv[:, n, 0:1], mv[:, n, 1:2], ALU.subtract, ALU.mult).then_inc(s["xn_ready"], 1)
                for n in range(TT):
                    dve.wait_ge(s["t_hi"], n + 1)
                    nc.vector.tensor_tensor(hhl[:, 1, :, n * P:(n + 1) * P], ps[n % 4][:, :, :], hhl[:, 0, :, n * P:(n + 1) * P],
                                            ALU.subtract).then_inc(s["t_lo"], 1)


def route(nc, t, h32, gates):
    with Scope(nc, "route") as sc:
        gw = sc.sb("gw", [P, DC, E_ALL])
        logit, sig, sel = (sc.sb(n, [P, TT, E_ALL]) for n in ("logit", "sig", "sel"))
        strict, same, pa, pb = (sc.sb(n, [P, TT, E_ALL]) for n in ("strict", "same", "pa", "pb"))
        best = sc.sb("best", [P, TT, 8])
        gmax = sc.sb("gmax", [P, TT, 8])
        gsel = sc.sb("gsel", [P, TT, GRP])
        few = sc.sb("few", [P, TT])
        ps = sc.ps("logits", [P, TT, E_ALL])
        s = {n: sc.sem(n) for n in ["gw_in", "logits_done", "sig_ready", "step"]}
        EPG = E_ALL // GRP
        with nc.Block() as block:
            @block.sync
            def _(sp):
                sp.dma_start(gw[:, :, :], t["gate_w_l"]).then_inc(s["gw_in"], 16)

            @block.tensor
            def _(pe):
                pe.wait_ge(s["gw_in"], 16)
                for n in range(TT):
                    for c in range(DC):
                        last = nc.tensor.matmul(ps[:, n, :], h32[:, c, n * P:(n + 1) * P], gw[:, c, :], start=c == 0, stop=c == DC - 1)
                last.then_inc(s["logits_done"], 1)

            @block.scalar
            def _(act):
                act.wait_ge(s["step"], 1)
                nc.scalar.activation(sig[:, :, :], logit[:, :, :], ACT.Sigmoid).then_inc(s["sig_ready"], 1)

            @block.vector
            def _(dve):
                steps = [0]
                V = nc.vector

                def link(ins):
                    steps[0] += 1
                    ins.then_inc(s["step"], 1)
                    dve.wait_ge(s["step"], steps[0])

                def wide(ap, n):
                    return ap.to_broadcast([P, TT, n])

                def choose(vals, n, k, width, out):
                    for m in range(TT):
                        link(V.max(best[:, m, :], vals[:, m, 0:width]))
                    v, st, eq, a, b = vals[:, :, 0:n], strict[:, :, 0:n], same[:, :, 0:n], pa[:, :, 0:n], pb[:, :, 0:n]
                    link(V.tensor_tensor(st, v, wide(best[:, :, k - 1:k], n), ALU.is_gt))
                    link(V.tensor_tensor(eq, v, wide(best[:, :, k - 1:k], n), ALU.is_equal))
                    link(V.reduce_sum(few[:, :], st, AX.X))
                    link(V.tensor_scalar(few[:, :], few[:, :], -1.0, float(k), ALU.mult, ALU.add))
                    link(V.tensor_copy(a, eq))
                    shift = 1
                    while shift < n:
                        link(V.tensor_copy(b[:, :, 0:shift], a[:, :, 0:shift]))
                        link(V.tensor_tensor(b[:, :, shift:n], a[:, :, shift:n], a[:, :, 0:n - shift], ALU.add))
                        a, b = b, a
                        shift *= 2
                    link(V.tensor_tensor(a, a, wide(few[:, :].unsqueeze(2), n), ALU.is_le))
                    link(V.tensor_tensor(eq, eq, a, ALU.mult))
                    link(V.tensor_tensor(out, st, eq, ALU.add))

                dve.wait_ge(s["logits_done"], 1)
                link(V.tensor_copy(logit[:, :, :], ps[:, :, :]))
                link(V.memset(gmax[:, :, :], -3e38))
                link(V.tensor_reduce(gmax[:, :, 0:GRP], logit[:, :, :].rearrange("p t (g e) -> p t g e", g=GRP), AX.X, ALU.max))
                choose(gmax, GRP, TOP_GRP, 8, gsel[:, :, :])
                dve.wait_ge(s["sig_ready"], 1)
                spread = gsel[:, :, :].unsqueeze(3).to_broadcast([P, TT, GRP, EPG])
                grouped = lambda a: a[:, :, :].rearrange("p t (g e) -> p t g e", g=GRP)
                link(V.tensor_tensor(grouped(logit), grouped(logit), spread, ALU.mult))
                link(V.tensor_scalar(gsel[:, :, :], gsel[:, :, :], 1e30, -1e30, ALU.mult, ALU.add))
                link(V.tensor_tensor(grouped(logit), grouped(logit), spread, ALU.add))
                choose(logit, E_ALL, TOPK, E_ALL, sel[:, :, :])
                link(V.tensor_tensor(sel[:, :, :], sel[:, :, :], sig[:, :, :], ALU.mult))
                link(V.reduce_sum(few[:, :], sel[:, :, :], AX.X))
                link(V.reciprocal(few[:, :], few[:, :]))
                link(V.memset(gates[:, :, E_ALL:EXPERTS], 1.0))
                link(V.tensor_tensor(gates[:, :, 0:E_ALL], sel[:, :, :], wide(few[:, :].unsqueeze(2), E_ALL), ALU.mult))


def experts(nc, t, x, hhl, gates, wq):
    with Scope(nc, "moe") as sc:
        seg_i, seg = sc.sb("seg_i", [BK + 1, BLOCKS], I32), sc.sb("seg", [BK + 1, BLOCKS])
        lim = sc.sb("lim", [BK + 1, 3])
        index = sc.sb("index", [BK + 1, BLOCKS], U32)
        turn = sc.sb("turn", [BK + 1, 2, STEP_BLOCKS], U32)
        rows = sc.sb("rows", [BK + 1, 2, STEP_BLOCKS, ROW])
        held = sc.sb("held", [1, 3])
        zero = sc.sb("zero", [BK + 1, STEP_BLOCKS], U32)
        NQ = 3 * DC * FI
        PART = NQ // NSTEP
        w8 = sc.sb("w8", [P, NQ])
        magic, y8, over = sc.sb("magic", [P, PART]), sc.sb("y8", [P, PART]), sc.sb("over", [P, PART])
        wq_flat = wq[:, :, :].rearrange("p k n -> p (k n)")
        up32, down32 = sc.sb("up32", [P, 2, DC, UPW]), sc.sb("down32", [P, 2, 2, D])
        up, down = sc.sb("up", [P, 2, 2, DC, UPW], BF16), sc.sb("down", [P, 2, 2, 2, D], BF16)
        silu = sc.sb("silu", [P, 2, 3, SPAN])
        h = sc.sb("h", [P, 2, 2, SPAN])
        hs = sc.sb("hs", [P, 2, 2, 2, SPAN], BF16)
        up_ps = [sc.ps(f"up{i}", [P, SPAN]) for i in range(6)]
        y_ps = [sc.ps(f"y{i}", [P, 2, D]) for i in range(2)]
        R = M - P
        names = ["seg_in", "w8_in", "indexed", "turned", "zero_set", "held_set", "quant",
                 "w_hi", "w_lo", "up_done", "silu_done", "h_done", "h_hi", "h_lo", "y_done", "added"]
        s = {n: sc.sem(n) for n in names}
        load = [sc.sem(f"load{i}") for i in range(2)]
        gathered = [sc.sem(f"gathered{i}") for i in range(2)]
        stored = [sc.sem(f"stored{i}") for i in range(2)]
        TILES_STEP = SPAN // P

        def each_pair(eng, expert, tail=None):
            expert(0, 0, True)
            expert(1, 1, False)
            with eng.Fori(1, EXPERTS // 2) as p:
                expert(2 * p, 0, False)
                expert(2 * p + 1, 1, False)
            if tail:
                tail(STEPS * EXPERTS)

        with nc.Block() as block:
            @block.sync
            def _(sp):
                def fetch(e, u):
                    if not (isinstance(e, int) and e < 2):
                        sp.wait_ge(s["w_lo"], 2 * e - 2)
                    src_u, src_d = (t[n][bass.ds(e, 1)] if not isinstance(e, int) else t[n][e:e + 1] for n in ("up_l", "down_l"))
                    sp.dma_start(up32[:, u, :, :], src_u.rearrange("e p c n -> p (e c) n")).then_inc(load[u], 16)
                    sp.dma_start(down32[:, u, :, :], src_d.rearrange("e p c n -> p (e c) n")).then_inc(load[u], 16)

                def store(n, u):
                    sp.wait_ge(gathered[u], 64 * ((n - u) // 2 + 1))
                    dst = t["near_s"][n:n + 1] if isinstance(n, int) else t["near_s"][bass.ds(n, 1)]
                    sp.dma_start(dst.rearrange("s p m -> p (s m)"), rows[:, u, :, :].rearrange("p m n -> p (m n)")).then_inc(stored[u], 16)

                fetch(0, 0)
                sp.dma_start(seg_i[:, :], t["segk_l"]).then_inc(s["seg_in"], 16)
                sp.dma_start(lim[:, :], t["lim_l"]).then_inc(s["seg_in"], 16)
                fetch(1, 1)
                sp.dma_start(w8[:, :], t["f8_l"]).then_inc(s["w8_in"], 16)
                fetch(2, 0)
                fetch(3, 1)
                store(0, 0)
                with sp.Fori(2, EXPERTS // 2) as p:
                    fetch(2 * p, 0)
                    store(2 * p - 3, 1)
                    fetch(2 * p + 1, 1)
                    store(2 * p - 2, 0)
                store(NSTEP - 1, 1)
                for u in range(2):
                    sp.wait_ge(stored[u], 16 * (NSTEP // 2) + 1)

            @block.gpsimd
            def _(pool):
                nc.gpsimd.memset(zero[:, :], 0).then_inc(s["zero_set"], 1)
                nc.gpsimd.memset(held[:, :], 0.0).then_inc(s["held_set"], 1)
                pool.wait_ge(s["zero_set"], 1)
                pool.wait_ge(s["indexed"], 2 + B)

                def split(e, u, first):
                    pool.wait_ge(s["w_hi"], 2 * e + 1)
                    nc.gpsimd.tensor_tensor(up[:, u, 1, :, :], up32[:, u, :, :], up[:, u, 0, :, :], ALU.subtract).then_inc(s["w_lo"], 1)
                    pool.wait_ge(s["w_hi"], 2 * e + 2)
                    nc.gpsimd.tensor_tensor(down[:, u, 1, :, :], down32[:, u, :, :], down[:, u, 0, :, :], ALU.subtract).then_inc(s["w_lo"], 1)
                    if not isinstance(e, int):
                        gather(e - 2, u)

                def gather(n, u):
                    pool.wait_ge(stored[u], 16 * ((n - u) // 2) + 1)
                    nc.gpsimd.tensor_tensor(turn[:, u, :], index[:, bass.ds(STEP_BLOCKS * n, STEP_BLOCKS)], zero[:, :], ALU.add).then_inc(s["turned"], 1)
                    pool.wait_ge(s["held_set"], n + 1)
                    pool.wait_ge(s["turned"], n + 1)
                    nc.gpsimd.tensor_tensor(held[:, u:u + 1], held[:, 2:3], held[:, 2:3], ALU.add).then_inc(s["held_set"], 1)
                    for m in range(STEP_BLOCKS):
                        pool.indirect_dma_start(out=rows[:, u, m, :], out_offset=None, in_=t["ktab_s"],
                                                in_offset=bass.IndirectOffsetOnAxis(ap=turn[:, u, m:m + 1], axis=0)).then_inc(gathered[u], 16)
                each_pair(pool, split)

            def unit_parts():
                return ((0, P), (1, R))

            @block.tensor
            def _(pe):
                def gate_up(q, hf, e, u):
                    if hf == 0:
                        pe.wait_ge(s["w_lo"], 2 * e + 1)
                    for k, (c0, n) in enumerate(UP_COLS):
                        o = up_ps[3 * hf + k][0:n, :]
                        wait(pe, s["h_done"], 3 * (q - 2) + k + 1)
                        for c in range(DC):
                            for a, w in ((0, 0), (0, 1), (1, 0)):
                                last = nc.tensor.matmul(o, up[:, u, w, c, c0:c0 + n], hhl[:, a, c, hf * SPAN:(hf + 1) * SPAN],
                                                        start=(c, a, w) == (0, 0, 0), stop=(c, a) == (DC - 1, 1))
                        last.then_inc(s["up_done"], 1)

                def down_rows(q, hf, e, u):
                    pe.wait_ge(s["w_lo"], 2 * e + 2)
                    pe.wait_ge(s["h_lo"], 2 * q + 2)
                    for m in range(TILES_STEP):
                        if m % 2 == 0:
                            wait(pe, s["added"], TILES_STEP * (q - 1) + m + 2)
                        o = y_ps[m // 2][:, m % 2, :]
                        for part, n in unit_parts():
                            for a, w in ((0, 0), (0, 1), (1, 0)):
                                last = nc.tensor.matmul(o, hs[0:n, hf, a, part, m * P:(m + 1) * P], down[0:n, u, w, part, :],
                                                        start=(part, a, w) == (0, 0, 0), stop=(part, a) == (1, 1))
                        if m % 2:
                            last.then_inc(s["y_done"], 1)

                def expert(e, u, first):
                    q = STEPS * e
                    gate_up(q, 0, e, u)
                    if not first:
                        down_rows(q - 1, 1, e - 1, 1 - u)
                    gate_up(q + 1, 1, e, u)
                    down_rows(q, 0, e, u)

                each_pair(pe, expert, lambda q: down_rows(q - 1, 1, EXPERTS - 1, 1))

            @block.scalar
            def _(act):
                def weights_high(e, u):
                    act.wait_ge(load[u], 32 * (e // 2 + 1) if isinstance(e, int) else 32 * ((e - u) // 2 + 1))
                    wait(act, s["up_done"], 6 * (e - 1))
                    nc.scalar.activation(up[:, u, 0, :, :], up32[:, u, :, :], ACT.Copy).then_inc(s["w_hi"], 1)
                    wait(act, s["y_done"], 4 * (e - 1))
                    nc.scalar.activation(down[:, u, 0, :, :], down32[:, u, :, :], ACT.Copy).then_inc(s["w_hi"], 1)

                def gates_of(q, hf):
                    for k, (_, n) in enumerate(UP_ROWS):
                        act.wait_ge(s["up_done"], 3 * q + k + 1)
                        wait(act, s["h_done"], 3 * (q - 2) + k + 1)
                        nc.scalar.activation(silu[64:64 + n, hf, k, :], up_ps[3 * hf + k][0:n, :], ACT.Silu).then_inc(s["silu_done"], 1)

                def high(q, hf):
                    for part, n in unit_parts():
                        act.wait_ge(s["h_done"], 3 * q + 2 + part)
                        wait(act, s["y_done"], 2 * (q - 1))
                        nc.scalar.activation(hs[0:n, hf, 0, part, :], h[0:n, hf, part, :], ACT.Copy).then_inc(s["h_hi"], 1)

                def expert(e, u):
                    q = STEPS * e
                    gates_of(q, 0)
                    high(q, 0)
                    if not (isinstance(e, int) and e == EXPERTS - 1):
                        weights_high(e + 1, 1 - u)
                    gates_of(q + 1, 1)
                    high(q + 1, 1)

                weights_high(0, 0)
                expert(0, 0)
                expert(1, 1)
                with act.Fori(1, EXPERTS // 2 - 1) as p:
                    expert(2 * p, 0)
                    expert(2 * p + 1, 1)
                expert(EXPERTS - 2, 0)
                expert(EXPERTS - 1, 1)

            @block.vector
            def _(dve):
                V = nc.vector

                def e_in_loop(e):
                    return not isinstance(e, int)

                def hidden(q, hf):
                    for k, (r0, n) in enumerate(UP_ROWS):
                        dve.wait_ge(s["silu_done"], 3 * q + k + 1)
                        if k == 0:
                            wait(dve, s["h_lo"], 2 * (q - 1))
                        out = h[r0 % P:r0 % P + n, hf, r0 // P, :]
                        nc.vector.tensor_tensor(out, up_ps[3 * hf + k][64:64 + n, :], silu[64:64 + n, hf, k, :], ALU.mult).then_inc(s["h_done"], 1)

                def low(q, hf):
                    for part, n in unit_parts():
                        dve.wait_ge(s["h_hi"], 2 * q + part + 1)
                        nc.vector.tensor_tensor(hs[0:n, hf, 1, part, :], h[0:n, hf, part, :], hs[0:n, hf, 0, part, :], ALU.subtract).then_inc(s["h_lo"], 1)

                def add(q, hf, e):
                    for m in range(TILES_STEP):
                        tile = TILES_STEP * hf + m
                        dve.wait_ge(s["y_done"], 2 * q + m // 2 + 1)
                        wait(dve, s["added"], TILES_STEP * (q - 1) + m + 1)
                        g = gates[:, tile, e:e + 1] if isinstance(e, int) else gates[:, tile, bass.ds(e, 1)]
                        nc.vector.scalar_tensor_tensor(x[:, tile, :], y_ps[m // 2][:, m % 2, :], g, x[:, tile, :], ALU.mult, ALU.add).then_inc(s["added"], 1)

                steps = [0]

                def link(ins):
                    steps[0] += 1
                    ins.then_inc(s["indexed"], 1)
                    dve.wait_ge(s["indexed"], steps[0])

                def key_indices():
                    dve.wait_ge(s["seg_in"], 32)
                    link(V.tensor_copy(seg[:, :], seg_i[:, :]))
                    link(V.tensor_scalar(seg[:, :], seg[:, :], lim[:, 0:1], lim[:, 1:2], ALU.add, ALU.max))
                    for b in range(B):
                        cols = slice(b * BLOCKS // B, (b + 1) * BLOCKS // B)
                        link(V.tensor_scalar(index[:, cols], seg[:, cols], lim[:, 2:3], float(b * TAB_ROWS), ALU.min, ALU.add))

                def quantize(n):
                    part = bass.ds(PART * n, PART)
                    w, done = w8[:, part], QUANT_STEPS * n

                    def then(ins, k):
                        ins.then_inc(s["quant"], 1)
                        dve.wait_ge(s["quant"], done + k)

                    then(V.tensor_scalar(magic[:, :].bitcast(I32), w.bitcast(I32), 0x7F800000, None, ALU.bitwise_and), 1)
                    then(V.tensor_scalar(magic[:, :], magic[:, :], 2.0 ** -6, 1.5 * 2 ** 20, ALU.max, ALU.mult), 2)
                    then(V.tensor_tensor(y8[:, :], w, magic[:, :], ALU.add), 3)
                    then(V.tensor_tensor(y8[:, :], y8[:, :], magic[:, :], ALU.subtract), 4)
                    then(V.tensor_scalar(over[:, :], y8[:, :], E4M3_MAX, 3e38, ALU.is_gt, ALU.mult), 5)
                    then(V.tensor_scalar(magic[:, :], y8[:, :], -E4M3_MAX, 3e38, ALU.is_lt, ALU.mult), 6)
                    then(V.tensor_tensor(over[:, :], over[:, :], magic[:, :], ALU.add), 7)
                    then(V.tensor_scalar(over[:, :], over[:, :], 10.0, None, ALU.mult), 8)
                    then(V.scalar_tensor_tensor(y8[:, :], y8[:, :], 1.0, over[:, :], ALU.mult, ALU.add), 9)
                    then(V.tensor_tensor(wq_flat[:, part], y8[:, :], over[:, :], ALU.subtract), QUANT_STEPS)

                for u in range(2):
                    V.memset(rows[:, u, 0, 0:1], 0.0).then_inc(stored[u], 1)
                key_indices()

                dve.wait_ge(s["w8_in"], 16)

                def expert(e, u, first):
                    q = STEPS * e
                    hidden(q, 0)
                    low(q, 0)
                    if not first:
                        add(q - 1, 1, e - 1)
                    hidden(q + 1, 1)
                    low(q + 1, 1)
                    add(q, 0, e)
                    if e_in_loop(e):
                        quantize(e - 2)

                each_pair(dve, expert, lambda q: add(q - 1, 1, EXPERTS - 1))


def key_table(nc, t, wabs, wvo):
    with Scope(nc, "ktab") as sc:
        ctx = sc.sb("ctx", [P, 2, DC, KP - S])
        wcat = sc.sb("wcat", [P, DC, ROW])
        kvcT, wkr = sc.sb("kvcT", [KVC, D]), sc.sb("wkr", [KVC, R1])
        cos, sin = sc.sb("cos", [P, CT, R1]), sc.sb("sin", [P, CT, R1])
        turned = sc.sb("turned", [P, 2, 4, R1])
        rows = sc.sb("rows", [P, 2, CT, ROW])
        ones = sc.sb("ones", [P, 1])
        mean = sc.sb("mean", [1, B, ROW])
        uqT, ukT, uvT, wo1 = sc.sb("uqT", [P, H1, QC]), sc.sb("ukT", [P, H1, KVC]), sc.sb("uvT", [P, H1, KVC]), sc.sb("wo1", [P, H1, D])
        w_ps = sc.ps("w", [P, DC, R1])
        ps = [sc.ps(f"k{i}", [P, 4, ROW]) for i in range(2)]
        mean_ps = sc.ps("mean_sum", [1, KVC])
        a_ps = [sc.ps(f"a{i}", [P, 512]) for i in range(2)]
        GROUPS_K = -(-CT // 4)
        s = {n: sc.sem(n) for n in ["small_in", "wide_in", "filled", "wkr_done", "wcat_ready", "k_done", "k_values", "rope", "k_ready",
                                    "mean_done", "mean_ready", "a_done", "a_used", "mean_out"]}
        ctx_in, rows_out = [sc.sem(f"ctx_in{i}") for i in range(2)], [sc.sem(f"rows_out{i}") for i in range(2)]
        with nc.Block() as block:
            @block.sync
            def _(sp):
                for dst, src in ((wcat[:, :, 0:KVC], "kvc_l"), (kvcT[:, :], "kvcT_l"), (wkr[:, :], "wkr_l"), (cos[:, :, :], "cosk_l"), (sin[:, :, :], "sink_l")):
                    sp.dma_start(dst, t[src]).then_inc(s["small_in"], 16)
                for b in range(2):
                    sp.dma_start(ctx[:, b, :, :], t["ctx_l"][b]).then_inc(ctx_in[b], 16)
                for dst, src in ((uqT, "uqT_l"), (ukT, "ukT_l"), (uvT, "uvT_l"), (wo1, "wo1_l")):
                    sp.dma_start(dst[:, :, :], t[src]).then_inc(s["wide_in"], 16)
                for b in range(B):
                    sp.wait_ge(s["k_ready"], GROUPS_K * (b + 1))
                    sp.wait_ge(s["k_values"], GROUPS_K * (b + 1))
                    base = b * TAB_ROWS
                    full = (CT - 1) * P
                    sp.dma_start(t["ktab_s"][base:base + full, :].rearrange("(j p) n -> p j n", p=P), rows[:, b % 2, 0:CT - 1, :]).then_inc(rows_out[b % 2], 16)
                    sp.dma_start(t["ktab_s"][base + full:base + CTX, :], rows[0:CTX - full, b % 2, CT - 1, :]).then_inc(rows_out[b % 2], 16)
                    if b + 2 < B:
                        sp.wait_ge(s["k_done"], GROUPS_K * (b + 1))
                        sp.dma_start(ctx[:, b % 2, :, :], t["ctx_l"][b + 2]).then_inc(ctx_in[b % 2], 16)
                sp.wait_ge(s["mean_ready"], B)
                for b in range(B):
                    sp.dma_start(t["ktab_s"][b * TAB_ROWS + CTX:(b + 1) * TAB_ROWS, :], mean[:, b, :]).then_inc(s["mean_out"], 16)
                for i in range(2):
                    sp.wait_ge(rows_out[i], 32 * (B // 2))
                sp.wait_ge(s["mean_out"], 16 * B)

            @block.gpsimd
            def _(pool):
                nc.gpsimd.memset(ones[:, :], 1.0).then_inc(s["filled"], 1)
                nc.gpsimd.memset(mean[:, :, :], 0.0).then_inc(s["filled"], 1)

            @block.tensor
            def _(pe):
                pe.wait_ge(s["small_in"], 80)
                for c in range(DC):
                    last = nc.tensor.matmul(w_ps[:, c, :], kvcT[:, c * P:(c + 1) * P], wkr[:, :], start=True, stop=True)
                last.then_inc(s["wkr_done"], 1)
                pe.wait_ge(s["wcat_ready"], 1)
                pe.wait_ge(s["filled"], 2)
                for b in range(B):
                    pe.wait_ge(ctx_in[b % 2], 16 * (b // 2 + 1))
                    for j in range(CT):
                        q, m = divmod(j, 4)
                        if m == 0:
                            wait(pe, s["k_ready"], GROUPS_K * b + q - 1)
                        for c in range(DC):
                            last = nc.tensor.matmul(ps[(GROUPS_K * b + q) % 2][:, m, :], ctx[:, b % 2, c, j * P:(j + 1) * P], wcat[:, c, :],
                                                    start=c == 0, stop=c == DC - 1)
                        if m == 3 or j == CT - 1:
                            last.then_inc(s["k_done"], 1)
                    pe.wait_ge(s["k_values"], GROUPS_K * (b + 1))
                    wait(pe, s["mean_ready"], b)
                    for j in range(CT):
                        last = nc.tensor.matmul(mean_ps[:, :], ones[:, :], rows[:, b % 2, j, 0:KVC], start=j == 0, stop=j == CT - 1)
                    last.then_inc(s["mean_done"], 1)
                pe.wait_ge(s["wide_in"], 64)
                for i in range(2):
                    for m in range(8):
                        h = 8 * i + m
                        last = nc.tensor.matmul(a_ps[i][0:QC, m * KVC:(m + 1) * KVC], uqT[:, h, :], ukT[:, h, :], start=True, stop=True)
                    last.then_inc(s["a_done"], 1)
                for h in range(H1):
                    pe.wait_ge(s["a_used"], h + 1)
                    last = nc.tensor.matmul(a_ps[h % 2][0:KVC, 0:D], uvT[:, h, :], wo1[:, h, :], start=True, stop=True)
                    last.then_inc(s["a_done"], 1)

            @block.scalar
            def _(act):
                act.wait_ge(s["wkr_done"], 1)
                nc.scalar.activation(wcat[:, :, KVC:ROW], w_ps[:, :, :], ACT.Copy).then_inc(s["wcat_ready"], 1)
                for b in range(B):
                    wait(act, rows_out[b % 2], 32 * (b // 2))
                    for q in range(GROUPS_K):
                        m = min(4, CT - 4 * q)
                        act.wait_ge(s["k_done"], GROUPS_K * b + q + 1)
                        nc.scalar.activation(rows[:, b % 2, 4 * q:4 * q + m, 0:KVC], ps[(GROUPS_K * b + q) % 2][:, 0:m, 0:KVC], ACT.Copy).then_inc(s["k_values"], 1)
                    act.wait_ge(s["mean_done"], b + 1)
                    act.wait_ge(s["filled"], 2)
                    nc.scalar.activation(mean[:, b, 0:KVC], mean_ps[:, :], ACT.Copy, scale=1.0 / CTX).then_inc(s["mean_ready"], 1)
                for i in range(2):
                    act.wait_ge(s["a_done"], i + 1)
                    nc.scalar.activation(wabs[:, 8 * i:8 * i + 8, :], a_ps[i][0:QC, :].rearrange("p (m k) -> p m k", m=8), ACT.Copy).then_inc(s["a_used"], 1)
                for h in range(H1):
                    act.wait_ge(s["a_done"], h + 3)
                    nc.scalar.activation(wvo[KVC * (h % 2):KVC * (h % 2) + KVC, h // 2, :], a_ps[h % 2][0:KVC, 0:D], ACT.Copy).then_inc(s["a_used"], 1)

            @block.vector
            def _(dve):
                n_rope = 0
                dve.wait_ge(s["small_in"], 80)
                for b in range(B):
                    for q in range(GROUPS_K):
                        g, m = GROUPS_K * b + q, min(4, CT - 4 * q)
                        bank = ps[g % 2]
                        dve.wait_ge(s["k_values"], g + 1)
                        if q == 0:
                            wait(dve, rows_out[b % 2], 32 * (b // 2))
                        out = rows[:, b % 2, 4 * q:4 * q + m, KVC:ROW]
                        tile = slice(4 * q, 4 * q + m)
                        u = turned[:, g % 2, 0:m, :]
                        nc.vector.tensor_tensor(out, bank[:, 0:m, KVC:ROW], cos[:, tile, :], ALU.mult).then_inc(s["rope"], 1)
                        nc.vector.tensor_tensor(u[:, :, 0:RH], bank[:, 0:m, KVC + RH:ROW], sin[:, tile, 0:RH], ALU.mult).then_inc(s["rope"], 1)
                        nc.vector.tensor_tensor(u[:, :, RH:R1], bank[:, 0:m, KVC:KVC + RH], sin[:, tile, RH:R1], ALU.mult).then_inc(s["rope"], 1)
                        n_rope += 3
                        dve.wait_ge(s["rope"], n_rope)
                        nc.vector.tensor_tensor(out, out, u, ALU.add).then_inc(s["k_ready"], 1)


def window_attention(nc, t, x, hhl, wabs, wvo):
    with Scope(nc, "win") as sc:
        HB = 2
        wdq32, wdq = sc.sb("wdq32", [P, DC, QC]), sc.sb("wdq", [P, 2, DC, QC], BF16)
        wqr, wqt = sc.sb("wqr", [QC, H1, R1]), sc.sb("wqt", [QC, H1, R1])
        cosq, sinq = sc.sb("cosq", [P, S]), sc.sb("sinq", [P, S])
        qc = sc.sb("qc", [QC, TOK])
        qT = sc.sb("qT", [P, TOK, H1])
        cq, sq = sc.sb("cq", [P, 2, SPAN]), sc.sb("sq", [P, 2, SPAN])
        ident = sc.sb("ident", [P, P])
        own = sc.sb("own", [P, BK])
        own1 = sc.sb("own1", [P, BK])
        seg_i, seg = sc.sb("seg_i", [P, BLOCKS], I32), sc.sb("seg", [P, BLOCKS])
        place = sc.sb("place", [P, WIN])
        key = sc.sb("key", [P, BLOCKS, WIN])
        bad = sc.sb("bad", [P, BLOCKS, WIN])
        none = sc.sb("none", [P, BLOCKS])
        keep = sc.sb("keep", [P, BLOCKS])
        near = sc.sb("near", [BK + 1, 5, STEP_BLOCKS, ROW])
        keyT = sc.sb("keyT", [P, 2, STEP_BLOCKS, BK])
        picked = sc.sb("picked", [P, 2, STEP_BLOCKS, BK])
        sc9 = sc.sb("sc9", [P, 2, STEP_BLOCKS, WIN])
        top = sc.sb("top", [P, 2, STEP_BLOCKS])
        pr = sc.sb("pr", [P, 2, STEP_BLOCKS, BK + 1])
        prT = sc.sb("prT", [BK + 1, 2, STEP_BLOCKS, P])
        ol = sc.sb("ol", [P, 2, H1 // 2, P])
        names = ["in_", "w_hi", "w_lo", "qc_done", "qc_ready", "r_done", "cs_ready", "n_copied", "r_ready", "mask", "kt_done", "kt_ready",
                 "sc_done", "picked_", "rest", "e_ready", "pr_ready", "pt_done", "pt_ready", "o_done", "o_used", "y_done", "added"]
        s = {n: sc.sem(n) for n in names}
        near_in = [sc.sem(f"near_in{i}") for i in range(5)]
        TSTEP = P // (BQ * STEP_BLOCKS)
        b8 = [sc.ps(f"b{i}", [P, 512]) for i in range(8)]
        with nc.Block() as block:
            @block.sync
            def _(sp):
                for dst, src in ((wdq32[:, :, :], "wdq_l"), (wqr[:, :, :], "wqr_l"), (wqt[:, :, :], "wqt_l"), (cosq[:, :], "cosq_l"), (sinq[:, :], "sinq_l"),
                                 (ident[:, :], "ident_l"), (own[:, :], "own_l"), (own1[:, :], "own1_l"), (seg_i[:, :], "segq_l"), (place[:, :], "place_l")):
                    sp.dma_start(dst, t[src]).then_inc(s["in_"], 16)
                for n in range(NSTEP):
                    wait(sp, s["o_done"], n - 4)
                    sp.dma_start(near[:, n % 5, :, :].rearrange("p m n -> p (m n)"), t["near_s"][n]).then_inc(near_in[n % 5], 16)

            @block.tensor
            def _(pe):
                pe.wait_ge(s["in_"], 160)
                pe.wait_ge(s["w_lo"], 1)
                for f in range(HB):
                    for c in range(DC):
                        for a, w in ((0, 0), (0, 1), (1, 0)):
                            last = nc.tensor.matmul(b8[f][0:QC, :], wdq[:, w, c, :], hhl[:, a, c, f * SPAN:(f + 1) * SPAN],
                                                    start=(c, a, w) == (0, 0, 0), stop=(c, a) == (DC - 1, 1))
                    last.then_inc(s["qc_done"], 1)
                for q in range(H1 // 2 * HB):
                    hp, f = divmod(q, HB)
                    pe.wait_ge(s["qc_ready"], HB)
                    for par in range(2):
                        wait(pe, s["n_copied"], 2 * (q - 1) + par + 1)
                        nc.tensor.matmul(b8[par][0:KVC, :], wabs[:, 2 * hp + par, :], qc[:, f * SPAN:(f + 1) * SPAN], start=True, stop=True).then_inc(s["r_done"], 1)
                    wait(pe, s["cs_ready"], 2 * (q - 1))
                    for w, k in ((wqr, 0), (wqt, 1)):
                        last = nc.tensor.matmul(b8[2 + 2 * (q % 2) + k][:, :], w[:, 2 * hp:2 * hp + 2, :].rearrange("p h r -> p (h r)"),
                                                qc[:, f * SPAN:(f + 1) * SPAN], start=True, stop=True)
                    last.then_inc(s["r_done"], 1)
                pe.wait_ge(s["n_copied"], 2 * HB * (H1 // 2))
                pe.wait_ge(s["cs_ready"], 2 * HB * (H1 // 2))

                def keys(n):
                    pe.wait_ge(near_in[n % 5], 16 * (n // 5 + 1))
                    wait(pe, s["kt_ready"], n - 1)
                    for m in range(STEP_BLOCKS):
                        last = nc.tensor.transpose(b8[n % 2][:, m * BK:(m + 1) * BK], near[0:BK, n % 5, m, :], ident[0:BK, 0:BK])
                    last.then_inc(s["kt_done"], 1)

                def score(n):
                    pe.wait_ge(s["kt_ready"], n + 1)
                    if n == 0:
                        pe.wait_ge(s["r_ready"], H1 * HB)
                    wait(pe, s["picked_"], n - 1)
                    for m in range(STEP_BLOCKS):
                        t0 = (STEP_BLOCKS * n + m) * BQ
                        last = nc.tensor.matmul(b8[2 + n % 2][:, m * BK:(m + 1) * BK], qT[:, t0:t0 + BQ, :].rearrange("p t h -> p (t h)"),
                                                keyT[:, n % 2, m, :], start=True, stop=True)
                    last.then_inc(s["sc_done"], 1)

                def turn(n):
                    pe.wait_ge(s["pr_ready"], n + 1)
                    wait(pe, s["pt_ready"], n - 1)
                    for m in range(STEP_BLOCKS):
                        last = nc.tensor.transpose(b8[4 + n % 2][0:BK + 1, m * P:(m + 1) * P], pr[:, n % 2, m, :], ident[:, :])
                    last.then_inc(s["pt_done"], 1)

                def value(n):
                    pe.wait_ge(s["pt_ready"], n + 1)
                    wait(pe, s["o_used"], 2 * n)
                    for m in range(STEP_BLOCKS):
                        last = nc.tensor.matmul(b8[6][0:KVC, m * P:(m + 1) * P], near[:, n % 5, m, 0:KVC], prT[:, n % 2, m, :], start=True, stop=True)
                    last.then_inc(s["o_done"], 1)

                def project(n):
                    pe.wait_ge(s["o_used"], 2 * TSTEP * (n + 1))
                    wait(pe, s["added"], n)
                    for hp in range(H1 // 2):
                        last = nc.tensor.matmul(b8[7][:, 0:D], ol[:, n % 2, hp, :], wvo[:, hp, :], start=hp == 0, stop=hp == H1 // 2 - 1)
                    last.then_inc(s["y_done"], 1)

                keys(0)
                keys(1)
                for n in range(NSTEP + 3):
                    if n < NSTEP:
                        score(n)
                    if n + 2 < NSTEP:
                        keys(n + 2)
                    if 1 <= n < NSTEP + 1:
                        turn(n - 1)
                    if 2 <= n < NSTEP + 2:
                        value(n - 2)
                    if 3 <= n and (n - 2) % TSTEP == 0:
                        project((n - 2) // TSTEP - 1)

            @block.scalar
            def _(act):
                act.wait_ge(s["in_"], 160)
                nc.scalar.activation(wdq[:, 0, :, :], wdq32[:, :, :], ACT.Copy).then_inc(s["w_hi"], 1)
                for f in range(HB):
                    act.wait_ge(s["qc_done"], f + 1)
                    nc.scalar.activation(qc[:, f * SPAN:(f + 1) * SPAN], b8[f][0:QC, :], ACT.Copy).then_inc(s["qc_ready"], 1)
                for q in range(H1 // 2 * HB):
                    hp, f = divmod(q, HB)
                    for par in range(2):
                        act.wait_ge(s["r_done"], 3 * q + par + 1)
                        nc.scalar.activation(qT[0:KVC, f * SPAN:(f + 1) * SPAN, 2 * hp + par], b8[par][0:KVC, :], ACT.Copy).then_inc(s["n_copied"], 1)

                def copy_keys(n):
                    act.wait_ge(s["kt_done"], n + 1)
                    wait(act, s["sc_done"], n - 1)
                    nc.scalar.activation(keyT[:, n % 2, :, :].rearrange("p m k -> p (m k)"), b8[n % 2][:, 0:STEP_BLOCKS * BK], ACT.Copy).then_inc(s["kt_ready"], 1)

                def exps(n):
                    act.wait_ge(s["rest"], 3 * n + 3)
                    nc.scalar.activation(sc9[:, n % 2, :, :], sc9[:, n % 2, :, :], ACT.Exp).then_inc(s["e_ready"], 1)

                def copy_weights(n):
                    act.wait_ge(s["pt_done"], n + 1)
                    wait(act, s["o_done"], n - 1)
                    nc.scalar.activation(prT[:, n % 2, :, :].rearrange("p m k -> p (m k)"), b8[4 + n % 2][0:BK + 1, :], ACT.Copy).then_inc(s["pt_ready"], 1)

                def copy_out(n):
                    act.wait_ge(s["o_done"], n + 1)
                    tile, t0 = n // TSTEP, n % TSTEP * STEP_BLOCKS * BQ
                    if n % TSTEP == 0:
                        wait(act, s["y_done"], tile - 1)
                    src = b8[6][0:KVC, :].rearrange("p (t g e) -> p e g t", g=H1 // 2, e=2)
                    for e in range(2):
                        nc.scalar.activation(ol[KVC * e:KVC * e + KVC, tile % 2, :, t0:t0 + STEP_BLOCKS * BQ], src[:, e, :, :], ACT.Copy).then_inc(s["o_used"], 1)

                copy_keys(0)
                copy_keys(1)
                for n in range(NSTEP + 2):
                    if n + 2 < NSTEP:
                        copy_keys(n + 2)
                    if n < NSTEP:
                        exps(n)
                    if 1 <= n < NSTEP + 1:
                        copy_weights(n - 1)
                    if 2 <= n:
                        copy_out(n - 2)

            @block.gpsimd
            def _(pool):
                for q in range(H1 // 2 * HB):
                    hp, f = divmod(q, HB)
                    pool.wait_ge(s["cs_ready"], 2 * q + 2)
                    for par in range(2):
                        rows = slice(R1 * par, R1 * par + R1)
                        nc.gpsimd.tensor_tensor(qT[KVC:P, f * SPAN:(f + 1) * SPAN, 2 * hp + par], cq[rows, q % 2, :], sq[rows, q % 2, :], ALU.add).then_inc(s["r_ready"], 1)

            @block.vector
            def _(dve):
                V = nc.vector
                dve.wait_ge(s["in_"], 160)
                dve.wait_ge(s["w_hi"], 1)
                V.tensor_tensor(wdq[:, 1, :, :], wdq32[:, :, :], wdq[:, 0, :, :], ALU.subtract).then_inc(s["w_lo"], 1)
                steps = [0]

                def link(ins):
                    steps[0] += 1
                    ins.then_inc(s["mask"], 1)
                    dve.wait_ge(s["mask"], steps[0])

                wide = [P, BLOCKS, WIN]
                link(V.tensor_copy(seg[:, :], seg_i[:, :]))
                link(V.tensor_tensor(key[:, :, :], seg[:, :].unsqueeze(2).to_broadcast(wide), place[:, :].unsqueeze(1).to_broadcast(wide), ALU.add))
                link(V.tensor_scalar(bad[:, :, :], key[:, :, :], 0.0, NEG, ALU.is_lt, ALU.mult))
                link(V.tensor_scalar(key[:, :, :], key[:, :, :], float(CTX - 1), NEG, ALU.is_gt, ALU.mult))
                link(V.tensor_tensor(bad[:, :, :], bad[:, :, :], key[:, :, :], ALU.add))
                link(V.tensor_reduce(none[:, :], bad[:, :, :], AX.X, ALU.max))
                link(V.tensor_scalar(none[:, :], none[:, :], NEG, None, ALU.is_equal))
                link(V.tensor_scalar(keep[:, :], none[:, :], -1.0, 1.0, ALU.mult, ALU.add))
                for q in range(H1 // 2 * HB):
                    hp, f = divmod(q, HB)
                    dve.wait_ge(s["r_done"], 3 * q + 3)
                    wait(dve, s["r_ready"], 2 * (q - 1))
                    for k, (out, tab) in enumerate(((cq, cosq), (sq, sinq))):
                        V.tensor_tensor(out[:, q % 2, :].rearrange("p (b t) -> p b t", t=S), b8[2 + 2 * (q % 2) + k][:, :].rearrange("p (b t) -> p b t", t=S),
                                        tab[:, :].unsqueeze(1).to_broadcast([P, SPAN // S, S]), ALU.mult).then_inc(s["cs_ready"], 1)

                def pick(n):
                    dve.wait_ge(s["sc_done"], n + 1)
                    V.tensor_tensor(picked[:, n % 2, :, :], b8[2 + n % 2][:, 0:STEP_BLOCKS * BK].rearrange("p (m k) -> p m k", m=STEP_BLOCKS),
                                    own[:, :].unsqueeze(1).to_broadcast([P, STEP_BLOCKS, BK]), ALU.mult).then_inc(s["picked_"], 1)
                    dve.wait_ge(s["picked_"], n + 1)
                    blocks = slice(STEP_BLOCKS * n, STEP_BLOCKS * n + STEP_BLOCKS)
                    w = sc9[:, n % 2, :, :]
                    link(V.reduce_sum(w, picked[:, n % 2, :, :].rearrange("p m (q j) -> p m j q", j=WIN), AX.X))
                    V.tensor_tensor(w, w, bad[:, blocks, :], ALU.add).then_inc(s["rest"], 1)
                    dve.wait_ge(s["rest"], 3 * n + 1)
                    V.tensor_reduce(top[:, n % 2, :], w, AX.X, ALU.max).then_inc(s["rest"], 1)
                    dve.wait_ge(s["rest"], 3 * n + 2)
                    V.tensor_tensor(w, w, top[:, n % 2, :].unsqueeze(2).to_broadcast([P, STEP_BLOCKS, WIN]), ALU.subtract).then_inc(s["rest"], 1)

                def weigh(n):
                    blocks = slice(STEP_BLOCKS * n, STEP_BLOCKS * n + STEP_BLOCKS)
                    w = sc9[:, n % 2, :, :]
                    total = top[:, n % 2, :]
                    dve.wait_ge(s["e_ready"], n + 1)
                    link(V.reduce_sum(total, w, AX.X))
                    link(V.reciprocal(total, total))
                    link(V.tensor_tensor(total, total, keep[:, blocks], ALU.mult))
                    link(V.tensor_tensor(w, w, total.unsqueeze(2).to_broadcast([P, STEP_BLOCKS, WIN]), ALU.mult))
                    wait(dve, s["pt_done"], n - 1)
                    for m in range(STEP_BLOCKS):
                        V.tensor_tensor(pr[:, n % 2, m, 0:BK].rearrange("p (q j) -> p q j", j=WIN), own1[:, :].rearrange("p (q j) -> p q j", j=WIN),
                                        w[:, m, :].unsqueeze(1).to_broadcast([P, BQ, WIN]), ALU.mult).then_inc(s["mask"], 1)
                        steps[0] += 1
                    V.tensor_copy(pr[:, n % 2, :, BK:BK + 1], none[:, blocks].unsqueeze(2)).then_inc(s["pr_ready"], 1)

                for n in range(NSTEP + 3):
                    if n < NSTEP:
                        pick(n)
                    if 1 <= n < NSTEP + 1:
                        weigh(n - 1)
                    if 3 <= n and (n - 2) % TSTEP == 0:
                        tile = (n - 2) // TSTEP - 1
                        dve.wait_ge(s["y_done"], tile + 1)
                        V.tensor_tensor(x[:, tile, :], b8[7][:, 0:D], x[:, tile, :], ALU.add).then_inc(s["added"], 1)


def feed_forward(nc, t, x, hhl, wq):
    with Scope(nc, "ffn") as sc:
        scales, dscale = sc.sb("scales", [P, 2, FC]), sc.sb("dscale", [P, D])
        silu, h = sc.sb("silu", [P, 2, SPAN]), sc.sb("h", [P, 2, SPAN])
        hs = sc.sb("hs", [P, 2, FC, TOK], BF16)
        y = sc.sb("y", [P, 2, D])
        gate_w, up_w = (wq[:, k, :].rearrange("p (c n) -> p c n", c=DC) for k in (0, 1))
        down_w = wq[:, 2, :].rearrange("p (c n) -> p c n", c=FC)
        up_ps = [sc.ps(f"up{i}", [P, SPAN]) for i in range(4)]
        y_ps = [sc.ps(f"y{i}", [P, D]) for i in range(2)]
        s = {n: sc.sem(n) for n in ["in_", "up_done", "silu_done", "h_done", "h_hi", "h_lo", "y_done", "scaled", "added", "out_"]}
        with nc.Block() as block:
            @block.sync
            def _(sp):
                sp.dma_start(scales[:, :, :], t["scales_l"]).then_inc(s["in_"], 16)
                sp.dma_start(dscale[:, :], t["dscale_l"]).then_inc(s["in_"], 16)
                for n in range(TT):
                    sp.wait_ge(s["added"], n + 1)
                    sp.dma_start(t["out_l"][n], x[:, n, :]).then_inc(s["out_"], 16)
                sp.wait_ge(s["out_"], 16 * TT)

            @block.tensor
            def _(pe):
                for f in range(STEPS):
                    for k in range(FC):
                        q = FC * f + k
                        wait(pe, s["h_done"], q - 1)
                        for g, w in enumerate((gate_w, up_w)):
                            for c in range(DC):
                                for a in range(2):
                                    last = nc.tensor.matmul(up_ps[2 * (q % 2) + g][:, :], w[:, c, k * P:(k + 1) * P], hhl[:, a, c, f * SPAN:(f + 1) * SPAN],
                                                            start=(c, a) == (0, 0), stop=(c, a) == (DC - 1, 1))
                            last.then_inc(s["up_done"], 1)
                for n in range(TT):
                    pe.wait_ge(s["h_lo"], FC * (n * P // SPAN + 1))
                    wait(pe, s["scaled"], n - 1)
                    for k in range(FC):
                        for a in range(2):
                            last = nc.tensor.matmul(y_ps[n % 2][:, :], hs[:, a, k, n * P:(n + 1) * P], down_w[:, k, :],
                                                    start=(k, a) == (0, 0), stop=(k, a) == (FC - 1, 1))
                    last.then_inc(s["y_done"], 1)

            @block.scalar
            def _(act):
                act.wait_ge(s["in_"], 32)
                for f in range(STEPS):
                    for k in range(FC + 1):
                        q = FC * f + k
                        if k < FC:
                            act.wait_ge(s["up_done"], 2 * q + 1)
                            wait(act, s["h_done"], q - 1)
                            nc.scalar.activation(silu[:, q % 2, :], up_ps[2 * (q % 2)][:, :], ACT.Silu, scale=scales[:, 0, k:k + 1]).then_inc(s["silu_done"], 1)
                        if k:
                            act.wait_ge(s["h_done"], q)
                            nc.scalar.activation(hs[:, 0, k - 1, f * SPAN:(f + 1) * SPAN], h[:, (q - 1) % 2, :], ACT.Copy).then_inc(s["h_hi"], 1)

            @block.vector
            def _(dve):
                dve.wait_ge(s["in_"], 32)
                for f in range(STEPS):
                    for k in range(FC + 1):
                        q = FC * f + k
                        if k < FC:
                            dve.wait_ge(s["silu_done"], q + 1)
                            dve.wait_ge(s["up_done"], 2 * q + 2)
                            wait(dve, s["h_lo"], q - 1)
                            nc.vector.scalar_tensor_tensor(h[:, q % 2, :], up_ps[2 * (q % 2) + 1][:, :], scales[:, 1, k:k + 1], silu[:, q % 2, :],
                                                           ALU.mult, ALU.mult).then_inc(s["h_done"], 1)
                        if k:
                            dve.wait_ge(s["h_hi"], q)
                            cols = slice(f * SPAN, (f + 1) * SPAN)
                            nc.vector.tensor_tensor(hs[:, 1, k - 1, cols], h[:, (q - 1) % 2, :], hs[:, 0, k - 1, cols], ALU.subtract).then_inc(s["h_lo"], 1)
                for n in range(TT):
                    dve.wait_ge(s["y_done"], n + 1)
                    wait(dve, s["added"], n - 1)
                    nc.vector.tensor_tensor(y[:, n % 2, :], y_ps[n % 2][:, :], dscale[:, :], ALU.mult).then_inc(s["scaled"], 1)
                    dve.wait_ge(s["scaled"], n + 1)
                    nc.vector.tensor_tensor(x[:, n, :], x[:, n, :], y[:, n % 2, :], ALU.add).then_inc(s["added"], 1)


def program(nc, t):
    def scratch(name, shape, dt):
        t[name] = nc.dram_tensor(name, shape, dt, kind="Internal").ap()

    scratch("kv_s", [B, P, 2 * DC * KP], BF16)
    scratch("tab_s", [B, P, 2 * KT * HALF], F32)
    scratch("wq_s", [KVH, P, 2, DC * REP * HD], BF16)
    scratch("wkv_s", [KVH, P, 2, DC * 2 * HD], BF16)
    scratch("wo_s", [KVH, P, 2, REP * D], BF16)
    scratch("ktab_s", [B * TAB_ROWS, ROW], F32)
    scratch("near_s", [BLOCKS // STEP_BLOCKS, BK + 1, STEP_BLOCKS * ROW], F32)
    with Scope(nc, "all") as top:
        x = top.sb("x", [P, TT, D])
        x_in = top.sem("x_in")
        with nc.Block() as block:
            @block.sync
            def _(sp):
                sp.dma_start(x[:, :, :], t["x_l"]).then_inc(x_in, 16)
                sp.wait_ge(x_in, 16)
        prepare(nc, t)
        attend(nc, t, x)
        with Scope(nc, "rest") as rest:
            hhl = rest.sb("hhl", [P, 2, DC, TOK], BF16)
            wq = rest.sb("wq", [P, 3, DC * FI], BF16)
            wabs, wvo = rest.sb("wabs", [QC, H1, KVC]), rest.sb("wvo", [P, H1 // 2, D])
            key_table(nc, t, wabs, wvo)
            with Scope(nc, "l0") as l0:
                gates = l0.sb("gates", [P, TT, EXPERTS])
                with Scope(nc, "exact") as exact:
                    h32 = exact.sb("h32", [P, DC, TOK])
                    normalize(nc, t, "norm2", x, hhl, h32)
                    route(nc, t, h32, gates)
                experts(nc, t, x, hhl, gates, wq)
            normalize(nc, t, "norm3", x, hhl)
            window_attention(nc, t, x, hhl, wabs, wvo)
            normalize(nc, t, "norm4", x, hhl)
            feed_forward(nc, t, x, hhl, wq)


def layout(i):
    def rows(a, n):
        return np.ascontiguousarray(a.reshape(n, P, -1).transpose(1, 0, 2))

    ctx = np.zeros((B, P, DC, KP - S), np.float32)
    ctx[..., :CTX] = np.asarray(i["ctx_2048"]).transpose(0, 2, 1).reshape(B, DC, P, CTX).transpose(0, 2, 1, 3)
    pos = np.zeros((B, KP), np.int32)
    pos[:, :S] = i["itok_BxS_4096_4607"]
    pos[:, S:NK] = i["pos_BxS2"]
    wq = np.asarray(i["L0_xattn_Wq"]).T.reshape(DC, P, KVH, REP * HD).transpose(1, 2, 0, 3)
    wk, wv = (np.asarray(i[f"L0_xattn_W{n}"]).T.reshape(DC, P, KVH, HD).transpose(1, 2, 0, 3) for n in "kv")
    wo = np.asarray(i["L0_xattn_Wo"]).reshape(D, KVH * REP, HD).transpose(2, 1, 0)
    flat = lambda a: np.ascontiguousarray(a).reshape(P, -1)
    gate, up, down = (np.asarray(i[f"L0_ffn_w_{n}"]) for n in ("gate", "up", "down"))
    sg, su = (np.asarray(i[f"L0_ffn_sw_{n}"]).reshape(D, 2, M).transpose(1, 0, 2) for n in ("gate", "up"))
    gate, up = np.concatenate([gate, sg]), np.concatenate([up, su])
    down = np.concatenate([down, np.asarray(i["L0_ffn_sw_down"]).reshape(2, M, D)])
    def turned(a):
        return np.ascontiguousarray(np.asarray(a).T)

    def chunks(a):
        a = np.asarray(a)
        return np.ascontiguousarray(a.reshape(-1, P, a.shape[-1]).transpose(1, 0, 2))

    freq = (1.0 / 10000.0 ** (np.arange(RH, dtype=np.float32) / RH)).astype(np.float32)
    angle = (np.arange(CT * P, dtype=np.float32)[:, None] * freq).astype(np.float32)
    cos, sin = np.cos(angle), np.sin(angle)
    key_cos = rows(np.concatenate([cos, cos], -1), CT).reshape(P, CT, R1)
    key_sin = rows(np.concatenate([-sin, sin], -1), CT).reshape(P, CT, R1)
    query_cos = np.ascontiguousarray(np.tile(cos[:S], (1, 4)).T)
    query_sin = np.ascontiguousarray(np.tile(np.concatenate([-sin[:S], sin[:S]], -1), (1, 2)).T)
    wqr = np.asarray(i["L1_xattn_W_qr"]).reshape(QC, H1, R1)
    seg_ids = np.asarray(i["itok_BxS_0_1023"]).reshape(BLOCKS, BQ)
    seg_keys = np.zeros((BK + 1, BLOCKS), np.int32)
    seg_keys[:BK] = np.repeat(seg_ids, WIN, 1).T
    seg_rows = np.ascontiguousarray(np.repeat(seg_ids, H1, 1).T.astype(np.int32))
    place = np.broadcast_to(np.arange(WIN, dtype=np.float32) - LOOKBACK, (P, WIN)).copy()
    lim = np.empty((BK + 1, 3), np.float32)
    lim[:BK, 0], lim[:BK, 1], lim[:BK, 2] = np.arange(BK) % WIN - LOOKBACK, 0, CTX - 1
    lim[BK] = 0, CTX, CTX
    own = np.repeat(np.repeat(np.eye(BQ, dtype=np.float32), H1, 0), WIN, 1)
    ups = np.zeros((EXPERTS, D, UPW), np.float32)
    for (r0, n), (c0, _) in zip(UP_ROWS, UP_COLS):
        ups[:, :, c0:c0 + n] = gate[:, :, r0:r0 + n]
        ups[:, :, c0 + 64:c0 + 64 + n] = up[:, :, r0:r0 + n]
    downs = np.zeros((EXPERTS, 2 * P, D), np.float32)
    downs[:, :M] = down
    return {
        "x_l": rows(np.asarray(i["x"]).reshape(TOK, D), TT),
        "ctx_l": ctx,
        "pos_l": np.ascontiguousarray(pos.reshape(B * KT, P).T),
        "invf_l": np.broadcast_to((1.0 / 10000.0 ** (np.arange(0, HD, 2, dtype=np.float32) / HD)).astype(np.float32), (P, HALF)).copy(),
        "ident_l": np.eye(P, dtype=np.float32),
        "wq_l": flat(wq),
        "wkv_l": flat(np.concatenate([wk, wv], -1)),
        "wo_l": flat(wo),
        "kvc_l": chunks(i["L1_xattn_W_kvc"]),
        "kvcT_l": turned(i["L1_xattn_W_kvc"]),
        "wkr_l": np.asarray(i["L1_xattn_W_kr"]),
        "cosk_l": key_cos, "sink_l": key_sin, "cosq_l": query_cos, "sinq_l": query_sin,
        "uqT_l": np.ascontiguousarray(np.asarray(i["L1_xattn_W_uq"]).reshape(QC, H1, HD1).transpose(2, 1, 0)),
        "ukT_l": np.ascontiguousarray(np.asarray(i["L1_xattn_W_uk"]).reshape(KVC, H1, HD1).transpose(2, 1, 0)),
        "uvT_l": np.ascontiguousarray(np.asarray(i["L1_xattn_W_uv"]).reshape(KVC, H1, HD1).transpose(2, 1, 0)),
        "wo1_l": np.ascontiguousarray(np.asarray(i["L1_xattn_W_o"]).reshape(H1, HD1, D).transpose(1, 0, 2)),
        "wdq_l": chunks(i["L1_xattn_W_dq"]),
        "wqr_l": wqr, "wqt_l": np.ascontiguousarray(np.concatenate([wqr[..., RH:], wqr[..., :RH]], -1)),
        "segk_l": seg_keys, "segq_l": seg_rows, "lim_l": lim, "place_l": place, "own_l": own * np.float32(SCALE1), "own1_l": own,
        "f8_l": np.concatenate([chunks(i[f"L1_ffn_{n}_w"]).reshape(P, -1) for n in ("gate", "up", "down")], 1),
        "scales_l": np.ascontiguousarray(np.stack([np.asarray(i[f"L1_ffn_{n}_scale"]).reshape(FC, P) for n in ("gate", "up")]).transpose(2, 0, 1)),
        "dscale_l": np.broadcast_to(np.asarray(i["L1_ffn_down_scale"]), (P, D)).copy(),
        "gate_w_l": np.ascontiguousarray(np.asarray(i["L0_ffn_gate_w"]).reshape(DC, P, E_ALL).transpose(1, 0, 2)),
        "up_l": np.ascontiguousarray(ups.reshape(EXPERTS, DC, P, UPW).transpose(0, 2, 1, 3)),
        "down_l": np.ascontiguousarray(downs.reshape(EXPERTS, 2, P, D).transpose(0, 2, 1, 3)),
        "kw_l": np.ascontiguousarray(np.broadcast_to(np.asarray(i["L0_xattn_k_norm_w"]), (P, HD))),
        "qw_l": np.ascontiguousarray(np.broadcast_to(np.asarray(i["L0_xattn_q_norm_w"]), (P, HD))),
    }


def kernel(**inputs):
    import concourse.bacc as bacc
    from concourse.bass_utils import run_bass_kernel_spmd

    nc = bacc.Bacc("TRN2", target_bir_lowering=False, num_devices=1)
    arrays = layout(inputs)
    t = {n: nc.dram_tensor(f"in_{n}", a.shape, mybir.dt.from_np(a.dtype), kind="ExternalInput").ap() for n, a in arrays.items()}
    t["out_l"] = nc.dram_tensor("out", [TT, P, D], F32, kind="ExternalOutput").ap()
    program(nc, t)
    r = run_bass_kernel_spmd(nc, [{f"in_{n}": a for n, a in arrays.items()}], core_ids=[0])
    return r.results[0]["out"].reshape(B, S, D)
```

```python
import concourse.bass as bass
from concourse import mybir
from contextlib import ExitStack
import numpy as np

F32 = mybir.dt.float32
BF16 = mybir.dt.bfloat16
I32 = mybir.dt.int32
U32 = mybir.dt.uint32
ALU = mybir.AluOpType
ACT = mybir.ActivationFunctionType
AX = mybir.AxisListType

P = 128
B, S, D = 4, 256, 256
TOK = B * S
TT = TOK // P
CTX = 1601
DC = D // P
KVH, REP, HD = 4, 4, 128
NK = S + CTX
KT = -(-NK // P)
KP = KT * P
BANKS = [(k, min(512, NK - k)) for k in range(0, NK, 512)]
NB = len(BANKS)
PAIRS = (KT + 1) // 2
HALF = HD // 2
ROUND = 1.5 * 2 ** 23
TURN = (6.28125, 0.0019340515136718750, 2 * np.pi - 6.28125 - 0.0019340515136718750)
PI_DOWN = float(np.nextafter(np.float32(np.pi), np.float32(0)))
LN_EPS = 1e-5
RMS_EPS = 1e-6
TILES = 2 * REP
GROUPS = B * KVH

H1, HD1, KVC, QC, R1 = 16, 128, 64, 96, 64
LOOKBACK = 8
WIN = LOOKBACK + 1
ROW = KVC + R1
CT = -(-CTX // P)
TAB_ROWS = CTX + 1
BQ = P // H1
BLOCKS = TOK // BQ
BK = BQ * WIN
STEP_BLOCKS = 4
NEG = -1e30
SCALE1 = 1.0 / float(np.sqrt(np.float32(HD1 + R1)))
RH = R1 // 2
NSTEP = BLOCKS // STEP_BLOCKS

FI = 768
FC = FI // P
E4M3_MAX = 448.0
QUANT_STEPS = 10


class Scope:

    def __init__(self, nc, name):
        self.nc, self.name, self.stack, self.sems = nc, name, ExitStack(), []

    def __enter__(self):
        self.stack.__enter__()
        return self

    def __exit__(self, *a):
        if self.sems:
            self.nc.clear_and_free_semaphores(self.sems)
            self.nc.all_engine_barrier()
        return self.stack.__exit__(*a)

    def sb(self, name, shape, dt=F32):
        return self.stack.enter_context(self.nc.sbuf_tensor(f"{self.name}_{name}", shape, dt))

    def ps(self, name, shape, dt=F32):
        return self.stack.enter_context(self.nc.psum_tensor(f"{self.name}_{name}", shape, dt))

    def sem(self, name):
        self.sems.append(self.nc.alloc_semaphore(name=f"{self.name}_{name}"))
        return self.sems[-1]


def wait(eng, sem, value):
    if not isinstance(value, int) or value > 0:
        eng.wait_ge(sem, value)


def prepare(nc, t, x):
    with Scope(nc, "prep") as sc:
        xh = sc.sb("xhat", [P, TT, D])
        stats = sc.sb("stats", [P, TT, 6])
        mv = sc.sb("mv", [P, TT, 2])
        ident = sc.sb("ident", [P, P])
        kv32 = sc.sb("kv32", [P, 2, DC, KP])
        kvhl = sc.sb("kvhl", [P, 2, 2, DC, KP], BF16)
        w32 = [sc.sb(f"w32_{i}", [P, n]) for i, n in enumerate((4096, 2048))]
        whl = [sc.sb(f"whl{i}", [P, 2, n], BF16) for i, n in enumerate((4096, 2048))]
        pos_i = sc.sb("pos_i", [P, B * KT], I32)
        pos = sc.sb("pos", [P, B * KT])
        invf = sc.sb("invf", [P, HALF])
        ang = sc.sb("ang", [P, B, KT, HALF])
        trig = sc.sb("trig", [P, B, 2, KT, HALF])
        nhalf = sc.sb("nhalf", [P, TT])
        halfpi = sc.sb("halfpi", [P, 1])
        xT_ps = [sc.ps(f"xT{i}", [P, DC, P]) for i in range(2)]
        GROUPS_K = -(-CT // 4)
        wcat = sc.sb("wcat", [P, DC, ROW])
        kvcT, wkr = sc.sb("kvcT", [KVC, D]), sc.sb("wkr", [KVC, R1])
        cos, sin = sc.sb("cos", [P, CT, R1]), sc.sb("sin", [P, CT, R1])
        turned = sc.sb("turned", [P, 2, 4, R1])
        rows = sc.sb("rows", [P, 2, CT, ROW])
        ones = sc.sb("ones", [P, 1])
        mean = sc.sb("mean", [1, B, ROW])
        w_ps = sc.ps("w", [P, DC, R1])
        ps = [sc.ps(f"k{i}", [P, 4, ROW]) for i in range(2)]
        mean_ps = sc.ps("mean_sum", [1, KVC])

        names = ["x_in", "small_in", "table_in", "t_out", "mean_out", "w_hi", "w_lo", "kv_hi", "kv_lo0", "kv_lo1", "xT_done", "xT_used",
                 "norm", "rstd_ready", "xhat_ready", "filled", "angle", "trig_reduced", "trig_ready",
                 "wkr_done", "wcat_ready", "k_done", "k_values", "rope", "k_ready", "mean_done", "mean_ready"]
        s = {n: sc.sem(n) for n in names}
        kv_in, kv_out, w_in, w_out, rows_out = ([sc.sem(f"{n}{i}") for i in range(2)] for n in ("kv_in", "kv_out", "w_in", "w_out", "rows_out"))
        WEIGHTS = [("wq_l", "wq_s", 4096), ("wkv_l", "wkv_s", 2048), ("wo_l", "wo_s", 4096)]

        with nc.Block() as block:
            @block.sync
            def _(sp):
                sp.dma_start(x[:, :, :], t["x_l"]).then_inc(s["x_in"], 16)
                for dst, src in ((ident, "ident_l"), (pos_i, "pos_l"), (invf, "invf_l")):
                    sp.dma_start(dst[:, :], t[src]).then_inc(s["small_in"], 16)
                sp.dma_start(kv32[:, 0, :, S:KP], t["ctx_l"][0]).then_inc(kv_in[0], 16)
                for dst, src in ((wcat[:, :, 0:KVC], "kvc_l"), (kvcT[:, :], "kvcT_l"), (wkr[:, :], "wkr_l"), (cos[:, :, :], "cosk_l"), (sin[:, :, :], "sink_l")):
                    sp.dma_start(dst, t[src]).then_inc(s["table_in"], 16)
                for i, (src, _, n) in enumerate(WEIGHTS[:2]):
                    sp.dma_start(w32[i][:, :], t[src]).then_inc(w_in[i], 16)
                    if i == 0:
                        sp.dma_start(kv32[:, 1, :, S:KP], t["ctx_l"][1]).then_inc(kv_in[1], 16)
                for b in range(B):
                    sp.wait_ge(s["kv_lo0"], b + 1)
                    sp.wait_ge(s["kv_lo1"], b + 1)
                    sp.dma_start(t["kv_s"][b], kvhl[:, b % 2, :, :, :].rearrange("p a c k -> p (a c k)")).then_inc(kv_out[b % 2], 16)
                    if b + 2 < B:
                        sp.wait_ge(s["k_done"], GROUPS_K * (b + 1))
                        sp.dma_start(kv32[:, b % 2, :, S:KP], t["ctx_l"][b + 2]).then_inc(kv_in[b % 2], 16)
                    if b == 0:
                        sp.wait_ge(s["w_lo"], 1)
                        sp.dma_start(w32[0][:, :], t["wo_l"]).then_inc(w_in[0], 16)
                    sp.wait_ge(s["k_ready"], GROUPS_K * (b + 1))
                    sp.wait_ge(s["k_values"], GROUPS_K * (b + 1))
                    base, full = b * TAB_ROWS, (CT - 1) * P
                    sp.dma_start(t["ktab_s"][base:base + full, :].rearrange("(j p) n -> p j n", p=P), rows[:, b % 2, 0:CT - 1, :]).then_inc(rows_out[b % 2], 16)
                    sp.dma_start(t["ktab_s"][base + full:base + CTX, :], rows[0:CTX - full, b % 2, CT - 1, :]).then_inc(rows_out[b % 2], 16)
                    if b == 2:
                        sp.wait_ge(s["trig_ready"], 2)
                        for b2 in range(B):
                            sp.dma_start(t["tab_s"][b2], trig[:, b2, :, :, :].rearrange("p a k f -> p (a k f)")).then_inc(s["t_out"], 16)
                sp.wait_ge(s["mean_ready"], B)
                for b in range(B):
                    sp.dma_start(t["ktab_s"][b * TAB_ROWS + CTX:(b + 1) * TAB_ROWS, :], mean[:, b, :]).then_inc(s["mean_out"], 16)
                for i in range(2):
                    sp.wait_ge(kv_out[i], 16 * (B // 2))
                    sp.wait_ge(rows_out[i], 32 * (B // 2))
                sp.wait_ge(s["t_out"], 16 * B)
                sp.wait_ge(s["mean_out"], 16 * B)

            @block.tensor
            def _(pe):
                def turn_tokens(b):
                    for n in (2 * b, 2 * b + 1):
                        pe.wait_ge(s["xhat_ready"], n + 1)
                        wait(pe, s["xT_used"], n - 1)
                        for c in range(DC):
                            last = nc.tensor.transpose(xT_ps[n % 2][:, c, :], xh[:, n, c * P:(c + 1) * P], ident[:, :])
                        last.then_inc(s["xT_done"], 1)

                pe.wait_ge(s["small_in"], 48)
                turn_tokens(0)
                pe.wait_ge(s["table_in"], 80)
                for c in range(DC):
                    last = nc.tensor.matmul(w_ps[:, c, :], kvcT[:, c * P:(c + 1) * P], wkr[:, :], start=True, stop=True)
                last.then_inc(s["wkr_done"], 1)
                pe.wait_ge(s["wcat_ready"], 1)
                pe.wait_ge(s["filled"], 4)
                for b in range(B):
                    if b + 1 < B:
                        turn_tokens(b + 1)
                    pe.wait_ge(kv_in[b % 2], 16 * (b // 2 + 1))
                    for j in range(CT):
                        q, m = divmod(j, 4)
                        if m == 0:
                            wait(pe, s["k_ready"], GROUPS_K * b + q - 1)
                        for c in range(DC):
                            last = nc.tensor.matmul(ps[(GROUPS_K * b + q) % 2][:, m, :], kv32[:, b % 2, c, S + j * P:S + (j + 1) * P], wcat[:, c, :],
                                                    start=c == 0, stop=c == DC - 1)
                        if m == 3 or j == CT - 1:
                            last.then_inc(s["k_done"], 1)
                    pe.wait_ge(s["k_values"], GROUPS_K * (b + 1))
                    wait(pe, s["mean_ready"], b)
                    for j in range(CT):
                        last = nc.tensor.matmul(mean_ps[:, :], ones[:, :], rows[:, b % 2, j, 0:KVC], start=j == 0, stop=j == CT - 1)
                    last.then_inc(s["mean_done"], 1)

            @block.scalar
            def _(act):
                def weight(i):
                    n = WEIGHTS[i][2]
                    act.wait_ge(w_in[i % 2], 16 * (i // 2 + 1))
                    wait(act, w_out[i % 2], 32 * (i // 2))
                    nc.scalar.activation(whl[i % 2][:, 0, :], w32[i % 2][:, :], ACT.Copy).then_inc(s["w_hi"], 1)

                def weight_out(i):
                    _, dst, n = WEIGHTS[i]
                    act.wait_ge(s["w_hi"], i + 1)
                    act.wait_ge(s["w_lo"], i + 1)
                    dram = t[dst].rearrange("g p a n -> a p g n")
                    for a in range(2):
                        act.dma_start(dram[a], whl[i % 2][:, a, :].rearrange("p (g n) -> p g n", g=4)).then_inc(w_out[i % 2], 16)

                def high(b):
                    for n in (2 * b, 2 * b + 1):
                        act.wait_ge(s["xT_done"], n + 1)
                        for c in range(DC):
                            wait(act, s[f"kv_lo{c}"], b - 1)
                        o = (n % 2) * P
                        nc.scalar.activation(kv32[:, b % 2, :, o:o + P], xT_ps[n % 2][:, :, :], ACT.Copy).then_inc(s["xT_used"], 1)
                    act.wait_ge(kv_in[b % 2], 16 * (b // 2 + 1))
                    act.wait_ge(s["xT_used"], 2 * b + 2)
                    wait(act, kv_out[b % 2], 16 * (b // 2))
                    for c in range(DC):
                        nc.scalar.activation(kvhl[:, b % 2, 0, c, :], kv32[:, b % 2, c, :], ACT.Copy).then_inc(s["kv_hi"], 1)

                def values(b):
                    wait(act, rows_out[b % 2], 32 * (b // 2))
                    for q in range(GROUPS_K):
                        m = min(4, CT - 4 * q)
                        act.wait_ge(s["k_done"], GROUPS_K * b + q + 1)
                        nc.scalar.activation(rows[:, b % 2, 4 * q:4 * q + m, 0:KVC], ps[(GROUPS_K * b + q) % 2][:, 0:m, 0:KVC],
                                             ACT.Copy).then_inc(s["k_values"], 1)

                def mean_row(b):
                    act.wait_ge(s["mean_done"], b + 1)
                    act.wait_ge(s["filled"], 4)
                    nc.scalar.activation(mean[:, b, 0:KVC], mean_ps[:, :], ACT.Copy, scale=1.0 / CTX).then_inc(s["mean_ready"], 1)

                high(0)
                act.wait_ge(s["wkr_done"], 1)
                nc.scalar.activation(wcat[:, :, KVC:ROW], w_ps[:, :, :], ACT.Copy).then_inc(s["wcat_ready"], 1)
                values(0)
                weight(0)
                high(1)
                weight_out(0)
                mean_row(0)
                values(1)
                weight(1)
                weight_out(1)
                high(2)
                mean_row(1)
                weight(2)
                act.wait_ge(s["trig_reduced"], 1)
                act.wait_ge(s["filled"], 4)
                cosines, sines = (trig[:, :, a, :, :].rearrange("p b k f -> p b (k f)") for a in range(2))
                nc.scalar.activation(sines, sines, ACT.Sin).then_inc(s["trig_ready"], 1)
                nc.scalar.activation(cosines, cosines, ACT.Sin, bias=halfpi[:, 0:1], scale=-1.0).then_inc(s["trig_ready"], 1)
                values(2)
                weight_out(2)
                high(3)
                mean_row(2)
                values(3)
                mean_row(3)
                act.wait_ge(w_out[0], 64)
                act.wait_ge(w_out[1], 32)

            @block.gpsimd
            def _(pool):
                nc.gpsimd.memset(nhalf[:, :], -0.5).then_inc(s["filled"], 1)
                nc.gpsimd.memset(ones[:, :], 1.0).then_inc(s["filled"], 1)
                nc.gpsimd.memset(mean[:, :, :], 0.0).then_inc(s["filled"], 1)
                nc.gpsimd.memset(halfpi[:, :], np.pi / 2).then_inc(s["filled"], 1)
                pool.wait_ge(s["filled"], 4)
                pool.wait_ge(s["norm"], 2 * TT + 1)
                nc.gpsimd.tensor_tensor(mv[:, :, 1], mv[:, :, 1], nhalf[:, :], ALU.pow).then_inc(s["rstd_ready"], 1)

                def weight_low(i):
                    n = WEIGHTS[i][2]
                    pool.wait_ge(s["w_hi"], i + 1)
                    nc.gpsimd.tensor_tensor(whl[i % 2][:, 1, :], w32[i % 2][:, :], whl[i % 2][:, 0, :], ALU.subtract).then_inc(s["w_lo"], 1)

                for b in range(B):
                    pool.wait_ge(s["kv_hi"], DC * b + 2)
                    nc.gpsimd.tensor_tensor(kvhl[:, b % 2, 1, 1, :], kv32[:, b % 2, 1, :], kvhl[:, b % 2, 0, 1, :], ALU.subtract).then_inc(s["kv_lo1"], 1)
                    if b < len(WEIGHTS):
                        weight_low(b)

            @block.vector
            def _(dve):
                V = nc.vector
                dve.wait_ge(s["x_in"], 16)
                for n in range(TT):
                    V.bn_stats(stats[:, n, :], x[:, n, :]).then_inc(s["norm"], 1)
                for n in range(TT):
                    dve.wait_ge(s["norm"], n + 1)
                    V.bn_aggr(mv[:, n, :], stats[:, n, :]).then_inc(s["norm"], 1)
                dve.wait_ge(s["norm"], 2 * TT)
                V.tensor_scalar(mv[:, :, 1], mv[:, :, 1], LN_EPS, None, ALU.add).then_inc(s["norm"], 1)
                dve.wait_ge(s["rstd_ready"], 1)
                for n in range(TT):
                    V.tensor_scalar(xh[:, n, :], x[:, n, :], mv[:, n, 0:1], mv[:, n, 1:2], ALU.subtract, ALU.mult).then_inc(s["xhat_ready"], 1)
                steps = [0]

                def link(ins):
                    steps[0] += 1
                    ins.then_inc(s["angle"], 1)
                    dve.wait_ge(s["angle"], steps[0])

                def low(b):
                    dve.wait_ge(s["kv_hi"], DC * b + 1)
                    V.tensor_tensor(kvhl[:, b % 2, 1, 0, :], kv32[:, b % 2, 0, :], kvhl[:, b % 2, 0, 0, :], ALU.subtract).then_inc(s["kv_lo0"], 1)

                def rope(b):
                    for q in range(GROUPS_K):
                        g, m = GROUPS_K * b + q, min(4, CT - 4 * q)
                        bank = ps[g % 2]
                        dve.wait_ge(s["k_values"], g + 1)
                        if q == 0:
                            wait(dve, rows_out[b % 2], 32 * (b // 2))
                        out = rows[:, b % 2, 4 * q:4 * q + m, KVC:ROW]
                        tile = slice(4 * q, 4 * q + m)
                        u = turned[:, g % 2, 0:m, :]
                        V.tensor_tensor(out, bank[:, 0:m, KVC:ROW], cos[:, tile, :], ALU.mult).then_inc(s["rope"], 1)
                        V.tensor_tensor(u[:, :, 0:RH], bank[:, 0:m, KVC + RH:ROW], sin[:, tile, 0:RH], ALU.mult).then_inc(s["rope"], 1)
                        V.tensor_tensor(u[:, :, RH:R1], bank[:, 0:m, KVC:KVC + RH], sin[:, tile, RH:R1], ALU.mult).then_inc(s["rope"], 1)
                        dve.wait_ge(s["rope"], 3 * (g + 1))
                        V.tensor_tensor(out, out, u, ALU.add).then_inc(s["k_ready"], 1)

                angle = ang[:, :, :, :].rearrange("p b k f -> p b (k f)")
                turns, red = (trig[:, :, a, :, :].rearrange("p b k f -> p b (k f)") for a in (0, 1))
                dve.wait_ge(s["small_in"], 48)
                dve.wait_ge(s["table_in"], 80)
                link(V.tensor_copy(pos[:, :], pos_i[:, :]))
                for b in range(B):
                    link(V.tensor_tensor(ang[:, b, :, :], pos[:, b * KT:(b + 1) * KT].unsqueeze(2).to_broadcast([P, KT, HALF]),
                                         invf[:, :].unsqueeze(1).to_broadcast([P, KT, HALF]), ALU.mult))
                low(0)
                link(V.tensor_scalar(turns, angle, 1 / (2 * np.pi), None, ALU.mult))
                rope(0)
                link(V.tensor_scalar(turns, turns, ROUND, -ROUND, ALU.add, ALU.add))
                link(V.scalar_tensor_tensor(red, turns, -TURN[0], angle, ALU.mult, ALU.add))
                low(1)
                link(V.scalar_tensor_tensor(red, turns, -TURN[1], red, ALU.mult, ALU.add))
                rope(1)
                link(V.scalar_tensor_tensor(red, turns, -TURN[2], red, ALU.mult, ALU.add))
                link(V.tensor_scalar(red, red, PI_DOWN, -PI_DOWN, ALU.min, ALU.max))
                link(V.tensor_scalar(turns, red, -1.0, None, ALU.mult))
                V.tensor_tensor(turns, turns, red, ALU.max).then_inc(s["trig_reduced"], 1)
                low(2)
                rope(2)
                low(3)
                rope(3)


SLOTS = [
    ([], [("KV", 0)], [("KV", 1)]),
    ([("AT-", 1)], [("KV", 2)], [("WO-", 1)]),
    ([], [("Q", 0)], [("KV", 3)]),
    ([], [("Q", 1)], [("KV", 4)]),
    ([("KT", 0)], [("KV", 5)], [("KV", 6)]),
    ([("AT", 0)], [("KV", 7)], [("QT", 0)]),
    ([("KT", 1)], [("WO", 0)], [("QT", 1)]),
    ([("KT", 2)], [("KT", 3)], []),
]
FIRST_GROUP = [("KV", 0), ("KV", 1), ("KV", 2), ("Q", 0), ("KV", 3), ("Q", 1), ("KV", 4), ("KV", 5), ("KV", 6),
               ("KV", 7), ("QT", 0), ("QT", 1), ("KT", 0), ("KT", 1), ("KT", 2), ("KT", 3)]
POOL_ORDER = [x for x in FIRST_GROUP if x[0] in ("KV", "Q")]
PER_GROUP = {"KV": PAIRS, "Q": 2, "KT": NB, "QT": 2, "AT": 2, "WO": 2}
ROPE_STEPS = 8
ROPE_STEPS_FIRST = 6


def tasks_of(place, prep, first, last):
    found = []
    for kind, n in place:
        if kind[-1] == "-":
            if not first:
                found.append((kind[:-1], n, -1))
        elif kind in ("AT", "WO"):
            if not last:
                found.append((kind, n, 0))
        elif prep:
            found.append((kind, n, 1))
    return found


def projected(i, prep):
    return [x for place in SLOTS[i - 1] for x in place if x[0] in ("KV", "Q")] if i and prep else []


def attend(nc, t, x, groups=GROUPS):
    with Scope(nc, "att") as sc:
        kvT = sc.sb("kvT", [P, 2, 2, DC, KP], BF16)
        tab = sc.sb("tab", [P, 2, 2, KT, HALF])
        wkv = sc.sb("wkv", [P, 2, 2, DC, 2 * HD], BF16)
        wq = sc.sb("wq", [P, 2, 2, DC, REP * HD], BF16)
        wo = sc.sb("wo", [P, 2, 2, REP, D], BF16)
        kw, qw, ident = sc.sb("kw", [P, HD]), sc.sb("qw", [P, HD]), sc.sb("ident", [P, P])
        nhalf = sc.sb("nhalf", [P, REP])
        eps = sc.sb("eps", [P, 2, REP])
        kvraw = sc.sb("kvraw", [P, 4, 2, 2 * HD])
        qraw = sc.sb("qraw", [P, 2, REP, HD])
        kjunk = sc.sb("kjunk", [P, 4, 2, HD], BF16)
        qjunk = sc.sb("qjunk", [P, 2, REP, HD], BF16)
        kss, qss = sc.sb("kss", [P, 4, 2]), sc.sb("qss", [P, 2, REP])
        scaled, cosd, sind = (sc.sb(n, [P, REP, HD]) for n in ("scaled", "cosd", "sind"))
        rs = sc.sb("rs", [P, REP])
        rs_first = sc.sb("rs_first", [P, len(POOL_ORDER), REP])
        kp = sc.sb("kp", [P, 2 * PAIRS, HD])
        qp = sc.sb("qp", [P, 2, REP, HD])
        K = sc.sb("K", [P, 2, 2, KP], BF16)
        V = sc.sb("V", [P, 2, KT, 2, HD], BF16)
        Q = sc.sb("Q", [P, 2, 2, TILES, P], BF16)
        mx = sc.sb("mx", [P, 2, NB])
        negmax = sc.sb("negmax", [P, 4])
        es = sc.sb("es", [P, 4, NB])
        rsum, rinv = sc.sb("rsum", [P, 4]), sc.sb("rinv", [P, 4])
        prob = sc.sb("prob", [P, 2, KP])
        pT = sc.sb("pT", [P, 2, 2, KT, P], BF16)
        attn = sc.sb("attn", [P, TILES, HD])
        aT = sc.sb("aT", [P, 2, 2, REP, P], BF16)

        scores = sc.ps("scores", [P, NB * 512])
        pT_ps = [sc.ps(f"pT{i}", [P, 4, P]) for i in range(2)]
        out_ps = sc.ps("out", [P, 2, HD])
        aux = sc.ps("aux", [P, 512])

        names = ["const", "pad", "kv_done", "kvraw_ready", "vhi_ready", "k_ss", "v_lo", "q_done", "qraw_ready", "q_ss",
                 "kt_done", "kt_hi", "kt_lo", "qt_done", "qt_hi", "qt_lo", "at_done", "at_hi", "at_lo",
                 "wo_done", "x_added", "kp_done", "qp_done", "rope", "rope_first", "norm_first", "qk_done", "bank_max", "negmax_ready",
                 "exp_done", "pt_done", "pt_hi", "pt_lo", "pv_done", "sum_ready", "rinv_ready", "o_done"]
        s = {n: sc.sem(n) for n in names}
        load, wq_load, tab_load = ([sc.sem(f"{n}{i}") for i in range(2)] for n in ("load", "wq_load", "tab_load"))
        wo_load = [sc.sem(f"wo_load{i}") for i in range(2)]
        DONE = {"KV": "kv_done", "Q": "q_done", "KT": "kt_done", "QT": "qt_done", "AT": "at_done", "WO": "wo_done"}
        FREE = {"KV": "kvraw_ready", "Q": "qraw_ready", "KT": "kt_lo", "QT": "qt_lo", "AT": "at_lo", "WO": "x_added"}

        def nth(kind, n, g):
            return PER_GROUP[kind] * g + n + 1

        def pair(j):
            return min(2, KT - 2 * j)

        def quad(i):
            return min(4, KT - 4 * i)

        def each_group(eng, group, tail):
            group(0, 0, True, groups > 1)
            group(1, 1, False, groups > 2)
            if groups > 4:
                with eng.Fori(1, groups // 2 - 1) as p:
                    group(2 * p, 0, False, True)
                    group(2 * p + 1, 1, False, True)
            if groups > 2:
                group(groups - 2, 0, False, True)
                group(groups - 1, 1, False, False)
            tail(groups)

        with nc.Block() as block:
            @block.sync
            def _(sp):
                def load_group(n, par, b, h):
                    if not isinstance(n, int) or n >= 2:
                        sp.wait_ge(s["kp_done"], nth("KV", PAIRS - 1, n - 2))
                        sp.wait_ge(s["qp_done"], nth("Q", 1, n - 2))
                    for dst, src in ((wkv[:, par, :, :, :].rearrange("p a c n -> p (a c n)"), t["wkv_s"][h]),
                                     (kvT[:, par, :, :, :].rearrange("p a c k -> p (a c k)"), t["kv_s"][b])):
                        sp.dma_start(dst, src).then_inc(load[par], 16)
                    sp.dma_start(wq[:, par, :, :, :].rearrange("p a c n -> p (a c n)"), t["wq_s"][h]).then_inc(wq_load[par], 16)
                    sp.dma_start(tab[:, par, :, :, :].rearrange("p a k f -> p (a k f)"), t["tab_s"][b]).then_inc(tab_load[par], 16)
                    if isinstance(n, int) and n == 0:
                        for dst, src in ((kw, "kw_l"), (qw, "qw_l"), (ident, "ident_l")):
                            sp.dma_start(dst[:, :], t[src]).then_inc(s["const"], 16)
                    if not isinstance(n, int) or n >= 2:
                        sp.wait_ge(s["wo_done"], nth("WO", 1, n - 2))
                    sp.dma_start(wo[:, par, :, :, :].rearrange("p a h n -> p (a h n)"), t["wo_s"][h]).then_inc(wo_load[par], 16)

                load_group(0, 0, 0, 0)
                load_group(1, 1, 0, 1)
                if groups > 2:
                    with sp.Fori(1, groups // 2) as p:
                        for u in range(2):
                            load_group(2 * p + u, u, p // 2, 2 * (p % 2) + u)

            @block.tensor
            def _(pe):
                before = []

                def task(kind, n, ahead, g, u):
                    gt = g + ahead
                    par = (u + ahead) % 2
                    if before:
                        bk, bn, bg = before.pop()
                        wait(pe, s[FREE[bk]], nth(bk, bn, bg))
                    before.append((kind, n, gt))
                    if kind == "KV":
                        if n == 0:
                            pe.wait_ge(load[par], 32 * (gt // 2 + 1))
                        for m in range(pair(n)):
                            o = aux[:, m * 256:(m + 1) * 256]
                            k0 = (2 * n + m) * P
                            for c in range(DC):
                                for a, w in ((0, 0), (0, 1), (1, 0)):
                                    last = nc.tensor.matmul(o, kvT[:, par, a, c, k0:k0 + P], wkv[:, par, w, c, :],
                                                            start=(c, a, w) == (0, 0, 0), stop=(c, a) == (DC - 1, 1))
                    elif kind == "Q":
                        if n == 0:
                            pe.wait_ge(wq_load[par], 16 * (gt // 2 + 1))
                        for c in range(DC):
                            for a, w in ((0, 0), (0, 1), (1, 0)):
                                last = nc.tensor.matmul(aux[:, :], kvT[:, par, a, c, n * P:(n + 1) * P], wq[:, par, w, c, :],
                                                        start=(c, a, w) == (0, 0, 0), stop=(c, a) == (DC - 1, 1))
                    elif kind == "KT":
                        pe.wait_ge(s["kp_done"], nth("KV", min(2 * n + 1, PAIRS - 1), gt))
                        for m in range(quad(n)):
                            last = nc.tensor.transpose(aux[:, m * P:(m + 1) * P], kp[:, 4 * n + m, :], ident[:, :])
                    elif kind == "QT":
                        pe.wait_ge(s["qp_done"], nth("Q", n, gt))
                        for m in range(REP):
                            last = nc.tensor.transpose(aux[:, m * P:(m + 1) * P], qp[:, n, m, :], ident[:, :])
                    elif kind == "AT":
                        pe.wait_ge(s["o_done"], TILES * gt + 4 * n + 4)
                        for m in range(REP):
                            last = nc.tensor.transpose(aux[:, m * P:(m + 1) * P], attn[:, 4 * n + m, :], ident[:, :])
                    else:
                        if n == 0:
                            pe.wait_ge(wo_load[par], 16 * (gt // 2 + 1))
                        pe.wait_ge(s["at_lo"], nth("AT", n, gt))
                        for m in range(REP):
                            for a, w in ((0, 0), (0, 1), (1, 0)):
                                last = nc.tensor.matmul(aux[:, 0:D], aT[:, n, a, m, :], wo[:, par, w, m, :],
                                                        start=(m, a, w) == (0, 0, 0), stop=(m, a) == (REP - 1, 1))
                    last.then_inc(s[DONE[kind]], 1)

                def form_scores(g, u, i):
                    tile = TILES * g + i
                    if i == 0:
                        pe.wait_ge(s["qt_lo"], nth("QT", 1, g))
                    for k, (lo, n) in enumerate(BANKS):
                        if i == 0:
                            pe.wait_ge(s["kt_lo"], nth("KT", k, g))
                        wait(pe, s["exp_done"], NB * (tile - 1) + k + 1)
                        for a, w in ((0, 0), (0, 1), (1, 0)):
                            last = nc.tensor.matmul(scores[:, lo:lo + n], Q[:, u, a, i, :], K[:, u, w, lo:lo + n],
                                                    start=(a, w) == (0, 0), stop=a == 1)
                        last.then_inc(s["qk_done"], 1)

                def turn_probs(tile, i, j):
                    wait(pe, s["exp_done"], NB * tile + j + 1)
                    wait(pe, s["pt_lo"], NB * tile + j - 1)
                    for m in range(quad(j)):
                        k0 = (4 * j + m) * P
                        last = nc.tensor.transpose(pT_ps[j % 2][:, m, :], prob[:, i % 2, k0:k0 + P], ident[:, :])
                    last.then_inc(s["pt_done"], 1)

                def apply_values(tile, i, j, g, par):
                    if i == 0 and j == 0:
                        pe.wait_ge(s["v_lo"], nth("KV", PAIRS - 1, g))
                    if j == 0:
                        wait(pe, s["o_done"], tile)
                    pe.wait_ge(s["pt_lo"], NB * tile + j + 1)
                    for m in range(quad(j)):
                        k = 4 * j + m
                        for a, w in ((0, 0), (0, 1), (1, 0)):
                            last = nc.tensor.matmul(out_ps[:, i % 2, :], pT[:, i % 2, a, k, :], V[:, par, k, w, :],
                                                    start=(k, a, w) == (0, 0, 0), stop=(k, a) == (KT - 1, 1))
                    if j == NB - 1:
                        last.then_inc(s["pv_done"], 1)

                def slot(i, g, u, first, prep, last):
                    ahead, amid, behind = (tasks_of(place, prep, first, last) for place in SLOTS[i])
                    old = not (first and i == 0) and not (last and i > 0)
                    tile, oi = TILES * g + i - 1, (i - 1) % TILES
                    og, opar = (g, u) if i else (g - 1, 1 - u)
                    if old:
                        turn_probs(tile, oi, 0)
                        turn_probs(tile, oi, 1)
                    if not last:
                        form_scores(g, u, i)
                    for x_ in ahead:
                        task(*x_, g, u)
                    if old:
                        apply_values(tile, oi, 0, og, opar)
                        turn_probs(tile, oi, 2)
                        apply_values(tile, oi, 1, og, opar)
                        turn_probs(tile, oi, 3)
                    for x_ in amid:
                        task(*x_, g, u)
                    if old:
                        apply_values(tile, oi, 2, og, opar)
                        apply_values(tile, oi, 3, og, opar)
                    for x_ in behind:
                        task(*x_, g, u)

                def group(g, u, first, prep):
                    if before:
                        bk, bn, _ = before.pop()
                        before.append((bk, bn, g if bk in ("KT", "QT", "KV", "Q") else g - 1))
                    for i in range(TILES):
                        slot(i, g, u, first, prep, False)

                def tail(g):
                    bk, bn, _ = before.pop()
                    before.append((bk, bn, g - 1))
                    for i in range(3):
                        slot(i, g, 0, False, False, True)

                for kind, n in FIRST_GROUP:
                    if (kind, n) == ("QT", 0):
                        pe.wait_ge(s["const"], 48)
                    task(kind, n, 0, 0, 0)
                each_group(pe, group, tail)

            def halves(kind, n, gt, par):
                if kind == "KT":
                    return [K[:, par, a, 512 * n:512 * n + P * quad(n)] for a in range(2)]
                if kind == "QT":
                    return [Q[:, par, a, REP * n:REP * n + REP, :].rearrange("p h q -> p (h q)") for a in range(2)]
                return [aT[:, n, a, :, :].rearrange("p h q -> p (h q)") for a in range(2)]

            def rope(eng, order, kind, n, g, par, first=False):
                linked = s["rope_first" if first else "rope"]
                base = ROPE_STEPS_FIRST * order if first else ROPE_STEPS * (len(POOL_ORDER) * (g - 1) + order)

                def step(k):
                    eng.wait_ge(linked, base + k)

                if kind == "KV":
                    m, raw, weight, ss, out = pair(n), kvraw[:, n % 4, :, 0:HD], kw, kss[:, n % 4, :], kp[:, 2 * n:2 * n + pair(n), :]
                    cos, sin = (tab[:, par, a, 2 * n:2 * n + m, :] for a in range(2))
                    shape = [P, m, HALF]
                    eng.wait_ge(s["kvraw_ready"], nth("KV", n, g))
                else:
                    m, raw, weight, ss, out = REP, qraw[:, n, :, :], qw, qss[:, n, :], qp[:, n, :, :]
                    shape = [P, m, HALF]
                    cos, sin = (tab[:, par, a, n:n + 1, :].to_broadcast(shape) for a in range(2))
                    eng.wait_ge(s["qraw_ready"], nth("Q", n, g))
                a, b, c = scaled[:, 0:m, :], cosd[:, 0:m, :], sind[:, 0:m, :]
                eng.tensor_tensor(a, raw[:, 0:m, :], weight[:, :].unsqueeze(1).to_broadcast([P, m, HD]), ALU.mult).then_inc(linked, 1)
                step(1)
                eng.tensor_tensor(b.rearrange("p m (e f) -> p m e f", e=2), a.rearrange("p m (e f) -> p m e f", e=2),
                                  cos.unsqueeze(2).to_broadcast([P, m, 2, HALF]), ALU.mult).then_inc(linked, 1)
                eng.tensor_tensor(c[:, :, 0:HALF], a[:, :, HALF:HD], sin, ALU.mult).then_inc(linked, 1)
                eng.tensor_tensor(c[:, :, HALF:HD], a[:, :, 0:HALF], sin, ALU.mult).then_inc(linked, 1)
                scale = rs_first[:, order, 0:m] if first else rs[:, 0:m]
                if not first:
                    eng.wait_ge(s["k_ss" if kind == "KV" else "q_ss"], nth(kind, n, g))
                    eng.tensor_tensor(scale, ss[:, 0:m], eps[:, 0 if kind == "KV" else 1, 0:m], ALU.add).then_inc(linked, 1)
                step(3)
                eng.tensor_tensor(b[:, :, 0:HALF], b[:, :, 0:HALF], c[:, :, 0:HALF], ALU.subtract).then_inc(linked, 1)
                if not first:
                    step(5)
                    eng.tensor_tensor(scale, scale, nhalf[:, 0:m], ALU.pow).then_inc(linked, 1)
                else:
                    step(4)
                    eng.wait_ge(s["norm_first"], 2 * order + 2)
                eng.tensor_tensor(b[:, :, HALF:HD], b[:, :, HALF:HD], c[:, :, HALF:HD], ALU.add).then_inc(linked, 1)
                step(ROPE_STEPS_FIRST if first else ROPE_STEPS)
                if kind == "KV":
                    wait(eng, s["kt_done"], nth("KT", n // 2, g - 1))
                else:
                    wait(eng, s["qt_done"], nth("QT", n, g - 1))
                eng.tensor_tensor(out, b, scale.unsqueeze(2).to_broadcast([P, m, HD]), ALU.mult)\
                    .then_inc(s["kp_done" if kind == "KV" else "qp_done"], 1)

            @block.scalar
            def _(act):
                def task(kind, n, ahead, g, u):
                    gt = g + ahead
                    par = (u + ahead) % 2
                    if kind == "WO":
                        return
                    act.wait_ge(s[DONE[kind]], nth(kind, n, gt))
                    if kind == "KV":
                        m = pair(n)
                        bank = aux[:, :].rearrange("p (m k) -> p m k", m=2)
                        wait(act, s["kp_done"], nth("KV", n, gt) - 4)
                        wait(act, s["v_lo"], nth("KV", n, gt) - 4)
                        nc.scalar.activation(kvraw[:, n % 4, 0:m, :], bank[:, 0:m, :], ACT.Copy).then_inc(s["kvraw_ready"], 1)
                    elif kind == "Q":
                        wait(act, s["qp_done"], nth("Q", n, gt - 1))
                        nc.scalar.activation(qraw[:, n, :, :].rearrange("p h d -> p (h d)"), aux[:, :], ACT.Copy).then_inc(s["qraw_ready"], 1)
                    else:
                        hi, _ = halves(kind, n, gt, par)
                        nc.scalar.activation(hi, aux[:, 0:hi.shape[-1]], ACT.Copy).then_inc(s[kind.lower() + "_hi"], 1)

                def values_high(kind, n, gt, par):
                    if kind == "KV":
                        m = pair(n)
                        if n == 0:
                            wait(act, s["pv_done"], TILES * (gt - 1))
                        act.wait_ge(s["kvraw_ready"], nth("KV", n, gt))
                        nc.scalar.activation(V[:, par, 2 * n:2 * n + m, 0, :], kvraw[:, n % 4, 0:m, HD:2 * HD], ACT.Copy).then_inc(s["vhi_ready"], 1)

                def probs_high(tile, i, j):
                    act.wait_ge(s["pt_done"], NB * tile + j + 1)
                    m = quad(j)
                    nc.scalar.activation(pT[:, i % 2, 0, 4 * j:4 * j + m, :], pT_ps[j % 2][:, 0:m, :], ACT.Copy).then_inc(s["pt_hi"], 1)

                def exponent(tile, i, k):
                    if k == 0:
                        act.wait_ge(s["negmax_ready"], tile + 1)
                    lo, n = BANKS[k]
                    nc.scalar.activation(prob[:, i % 2, lo:lo + n], scores[:, lo:lo + n], ACT.Exp, bias=negmax[:, i % 4:i % 4 + 1],
                                         scale=1.0, accum_out=es[:, i % 4, k:k + 1]).then_inc(s["exp_done"], 1)

                def output(tile, i):
                    act.wait_ge(s["pv_done"], tile + 1)
                    act.wait_ge(s["rinv_ready"], tile + 1)
                    nc.scalar.activation(attn[:, i, :], out_ps[:, i % 2, :], ACT.Copy, scale=rinv[:, i % 4:i % 4 + 1]).then_inc(s["o_done"], 1)

                def slot(i, g, u, first, prep, last):
                    ahead, amid, behind = (tasks_of(place, prep, first, last) for place in SLOTS[i])
                    tile, oi = TILES * g + i, (i - 1) % TILES
                    old = not (first and i == 0) and not (last and i > 0)
                    if old:
                        probs_high(tile - 1, oi, 0)
                        probs_high(tile - 1, oi, 1)
                    if not (first and i < 2) and not (last and i > 1):
                        output(tile - 2, (i - 2) % TILES)
                    for kind, n in projected(i, prep):
                        values_high(kind, n, g + 1, 1 - u)
                    for x_ in ahead:
                        task(*x_, g, u)
                    if old:
                        probs_high(tile - 1, oi, 2)
                    if not last:
                        exponent(tile, i, 0)
                    if old:
                        probs_high(tile - 1, oi, 3)
                    if not last:
                        exponent(tile, i, 1)
                    for x_ in amid:
                        task(*x_, g, u)
                    if not last:
                        exponent(tile, i, 2)
                        exponent(tile, i, 3)
                    for x_ in behind:
                        task(*x_, g, u)

                act.wait_ge(s["pad"], 4)
                for kind, n in FIRST_GROUP:
                    task(kind, n, 0, 0, 0)
                    values_high(kind, n, 0, 0)
                each_group(act, lambda g, u, first, prep: [slot(i, g, u, first, prep, False) for i in range(TILES)],
                           lambda g: [slot(i, g, 0, False, False, True) for i in range(3)])

            @block.vector
            def _(dve):
                def task(kind, n, ahead, g, u):
                    gt = g + ahead
                    par = (u + ahead) % 2
                    if kind in ("KV", "Q"):
                        return
                    if kind == "WO":
                        dve.wait_ge(s["wo_done"], nth("WO", n, gt))
                        tile = 2 * (gt // KVH) + n
                        acc = x[:, tile, :] if isinstance(tile, int) else x[:, bass.ds(tile, 1), :].rearrange("p a d -> p (a d)")
                        nc.vector.tensor_tensor(acc, aux[:, 0:D], acc, ALU.add).then_inc(s["x_added"], 1)
                    else:
                        hi, lo = halves(kind, n, gt, par)
                        dve.wait_ge(s[kind.lower() + "_hi"], nth(kind, n, gt))
                        nc.vector.tensor_tensor(lo, aux[:, 0:hi.shape[-1]], hi, ALU.subtract).then_inc(s[kind.lower() + "_lo"], 1)

                def raw_rows(kind, n, gt, par):
                    if kind == "KV":
                        m = pair(n)
                        dve.wait_ge(s["kvraw_ready"], nth("KV", n, gt))
                        for q in range(m):
                            k_rows = kvraw[:, n % 4, q, 0:HD]
                            last = nc.vector.scalar_tensor_tensor(kjunk[:, n % 4, q, :], k_rows, 1.0 / HD, k_rows,
                                                                  ALU.mult, ALU.mult, accum_out=kss[:, n % 4, q:q + 1])
                        last.then_inc(s["k_ss"], 1)
                        dve.wait_ge(s["vhi_ready"], nth("KV", n, gt))
                        nc.vector.tensor_tensor(V[:, par, 2 * n:2 * n + m, 1, :], kvraw[:, n % 4, 0:m, HD:2 * HD], V[:, par, 2 * n:2 * n + m, 0, :],
                                                ALU.subtract).then_inc(s["v_lo"], 1)
                    elif kind == "Q":
                        dve.wait_ge(s["qraw_ready"], nth("Q", n, gt))
                        for q in range(REP):
                            last = nc.vector.scalar_tensor_tensor(qjunk[:, n, q, :], qraw[:, n, q, :], 1.0, qraw[:, n, q, :],
                                                                  ALU.mult, ALU.mult, accum_out=qss[:, n, q:q + 1])
                        last.then_inc(s["q_ss"], 1)

                def row_max(tile, i):
                    for k, (lo, n) in enumerate(BANKS):
                        dve.wait_ge(s["qk_done"], NB * tile + k + 1)
                        nc.vector.reduce_max(mx[:, i % 2, k:k + 1], scores[:, lo:lo + n], AX.X).then_inc(s["bank_max"], 1)
                    dve.wait_ge(s["bank_max"], NB * tile + NB)
                    nc.vector.tensor_reduce(negmax[:, i % 4:i % 4 + 1], mx[:, i % 2, :], AX.X, ALU.max, negate=True).then_inc(s["negmax_ready"], 1)

                def row_sum(tile, i):
                    dve.wait_ge(s["exp_done"], NB * tile + NB)
                    nc.vector.reduce_sum(rsum[:, i % 4:i % 4 + 1], es[:, i % 4, :], AX.X).then_inc(s["sum_ready"], 1)
                    dve.wait_ge(s["sum_ready"], tile + 1)
                    nc.vector.reciprocal(rinv[:, i % 4:i % 4 + 1], rsum[:, i % 4:i % 4 + 1]).then_inc(s["rinv_ready"], 1)

                def probs_low(tile, i, j):
                    dve.wait_ge(s["pt_hi"], NB * tile + j + 1)
                    m = quad(j)
                    nc.vector.tensor_tensor(pT[:, i % 2, 1, 4 * j:4 * j + m, :], pT_ps[j % 2][:, 0:m, :], pT[:, i % 2, 0, 4 * j:4 * j + m, :],
                                            ALU.subtract).then_inc(s["pt_lo"], 1)

                def slot(i, g, u, first, prep, last):
                    ahead, amid, behind = (tasks_of(place, prep, first, last) for place in SLOTS[i])
                    tile, oi = TILES * g + i, (i - 1) % TILES
                    old = not (first and i == 0) and not (last and i > 0)
                    if old:
                        probs_low(tile - 1, oi, 0)
                        probs_low(tile - 1, oi, 1)
                    if not last:
                        row_max(tile, i)
                    for x_ in ahead:
                        task(*x_, g, u)
                    if old:
                        row_sum(tile - 1, oi)
                        probs_low(tile - 1, oi, 2)
                        probs_low(tile - 1, oi, 3)
                    for kind, n in projected(i, prep):
                        raw_rows(kind, n, g + 1, 1 - u)
                    for x_ in amid + behind:
                        task(*x_, g, u)

                dve.wait_ge(s["pad"], 4)
                dve.wait_ge(s["const"], 48)
                dve.wait_ge(tab_load[0], 16)
                for kind, n in FIRST_GROUP:
                    task(kind, n, 0, 0, 0)
                    raw_rows(kind, n, 0, 0)
                    if kind in ("KV", "Q"):
                        rope(dve, POOL_ORDER.index((kind, n)), kind, n, 0, 0, first=True)
                each_group(dve, lambda g, u, first, prep: [slot(i, g, u, first, prep, False) for i in range(TILES)],
                           lambda g: [slot(i, g, 0, False, False, True) for i in range(3)])

            @block.gpsimd
            def _(pool):
                def prep(g, par):
                    pool.wait_ge(tab_load[par], 16 * (g // 2 + 1))
                    for order, (kind, n) in enumerate(POOL_ORDER):
                        rope(pool, order, kind, n, g, par)

                nc.gpsimd.memset(nhalf[:, :], -0.5).then_inc(s["pad"], 1)
                nc.gpsimd.memset(prob[:, :, NK:KP], 0.0).then_inc(s["pad"], 1)
                nc.gpsimd.memset(eps[:, 0, :], RMS_EPS).then_inc(s["pad"], 1)
                nc.gpsimd.memset(eps[:, 1, :], RMS_EPS * HD).then_inc(s["pad"], 1)
                pool.wait_ge(s["pad"], 4)
                pool.wait_ge(s["const"], 48)
                for order, (kind, n) in enumerate(POOL_ORDER):
                    ss, m = (kss[:, n % 4, :], pair(n)) if kind == "KV" else (qss[:, n, :], REP)
                    scale = rs_first[:, order, 0:m]
                    pool.wait_ge(s["k_ss" if kind == "KV" else "q_ss"], nth(kind, n, 0))
                    nc.gpsimd.tensor_tensor(scale, ss[:, 0:m], eps[:, 0 if kind == "KV" else 1, 0:m], ALU.add).then_inc(s["norm_first"], 1)
                    pool.wait_ge(s["norm_first"], 2 * order + 1)
                    nc.gpsimd.tensor_tensor(scale, scale, nhalf[:, 0:m], ALU.pow).then_inc(s["norm_first"], 1)
                pool.wait_ge(s["kp_done"], PAIRS)
                pool.wait_ge(s["qp_done"], 2)
                prep(1, 1)
                if groups > 2:
                    with pool.Fori(1, groups // 2) as p:
                        prep(2 * p, 0)
                        prep(2 * p + 1, 1)


E_ALL, TOPK, GRP, TOP_GRP = 32, 6, 4, 2
M = 176
EXPERTS = E_ALL + 2
UP_ROWS = [(0, 64), (64, 64), (128, M - 128)]
UP_COLS = [(0, 128), (128, 128), (256, 64 + M - 128)]
UPW = UP_COLS[-1][0] + UP_COLS[-1][1]
SPAN = 512
STEPS = TOK // SPAN
assert NSTEP == EXPERTS - 2


def normalize(nc, t, name, x, hhl, h32=None, loads=()):
    with Scope(nc, name) as sc:
        xn = sc.sb("xn", [P, TT, D])
        stats, mv, nhalf, ident = sc.sb("stats", [P, TT, 6]), sc.sb("mv", [P, TT, 2]), sc.sb("nhalf", [P, TT]), sc.sb("ident", [P, P])
        ps = [sc.ps(f"t{i}", [P, DC, P]) for i in range(4)]
        names = ["ident_in", "half_set", "stat", "var_ready", "rstd_ready", "xn_ready", "t_done", "t_hi", "t_lo"]
        s = {n: sc.sem(n) for n in names}
        with nc.Block() as block:
            @block.sync
            def _(sp):
                sp.dma_start(ident[:, :], t["ident_l"]).then_inc(s["ident_in"], 16)
                for dst, src, loaded in loads:
                    sp.dma_start(dst, src).then_inc(loaded, 16)

            @block.gpsimd
            def _(pool):
                nc.gpsimd.memset(nhalf[:, :], -0.5).then_inc(s["half_set"], 1)
                pool.wait_ge(s["half_set"], 1)
                pool.wait_ge(s["var_ready"], 1)
                nc.gpsimd.tensor_tensor(mv[:, :, 1], mv[:, :, 1], nhalf[:, :], ALU.pow).then_inc(s["rstd_ready"], 1)

            @block.tensor
            def _(pe):
                pe.wait_ge(s["ident_in"], 16)
                for n in range(TT):
                    pe.wait_ge(s["xn_ready"], n + 1)
                    wait(pe, s["t_lo"], n - 3)
                    for c in range(DC):
                        last = nc.tensor.transpose(ps[n % 4][:, c, :], xn[:, n, c * P:(c + 1) * P], ident[:, :])
                    last.then_inc(s["t_done"], 1)

            @block.scalar
            def _(act):
                for n in range(TT):
                    act.wait_ge(s["t_done"], n + 1)
                    if h32 is not None:
                        nc.scalar.activation(h32[:, :, n * P:(n + 1) * P], ps[n % 4][:, :, :], ACT.Copy)
                    nc.scalar.activation(hhl[:, 0, :, n * P:(n + 1) * P], ps[n % 4][:, :, :], ACT.Copy).then_inc(s["t_hi"], 1)

            @block.vector
            def _(dve):
                for n in range(TT):
                    nc.vector.bn_stats(stats[:, n, :], x[:, n, :]).then_inc(s["stat"], 1)
                for n in range(TT):
                    dve.wait_ge(s["stat"], n + 1)
                    nc.vector.bn_aggr(mv[:, n, :], stats[:, n, :]).then_inc(s["stat"], 1)
                dve.wait_ge(s["stat"], 2 * TT)
                nc.vector.tensor_scalar(mv[:, :, 1], mv[:, :, 1], LN_EPS, None, ALU.add).then_inc(s["var_ready"], 1)
                dve.wait_ge(s["rstd_ready"], 1)
                for n in range(TT):
                    nc.vector.tensor_scalar(xn[:, n, :], x[:, n, :], mv[:, n, 0:1], mv[:, n, 1:2], ALU.subtract, ALU.mult).then_inc(s["xn_ready"], 1)
                for n in range(TT):
                    dve.wait_ge(s["t_hi"], n + 1)
                    nc.vector.tensor_tensor(hhl[:, 1, :, n * P:(n + 1) * P], ps[n % 4][:, :, :], hhl[:, 0, :, n * P:(n + 1) * P],
                                            ALU.subtract).then_inc(s["t_lo"], 1)


def route(nc, t, x, hhl, gates, wabs, wvo, loads):
    with Scope(nc, "route") as sc:
        h32 = sc.sb("h32", [P, DC, TOK])
        gw = sc.sb("gw", [P, DC, E_ALL])
        logit, sig, sel = (sc.sb(n, [P, TT, E_ALL]) for n in ("logit", "sig", "sel"))
        strict, same, pa, pb = (sc.sb(n, [P, TT, E_ALL]) for n in ("strict", "same", "pa", "pb"))
        best = sc.sb("best", [P, TT, 8])
        gmax = sc.sb("gmax", [P, TT, 8])
        gsel = sc.sb("gsel", [P, TT, GRP])
        few = sc.sb("few", [P, TT])
        uqT, ukT, uvT, wo1 = (sc.sb(n, [P, H1, w]) for n, w in (("uqT", QC), ("ukT", KVC), ("uvT", KVC), ("wo1", D)))
        s = {n: sc.sem(n) for n in ["gw_in", "logits_done", "sig_ready", "step", "wide_in", "a_done", "a_used"]}
        EPG = E_ALL // GRP
        normalize(nc, t, "norm2", x, hhl, h32, [(gw[:, :, :], t["gate_w_l"], s["gw_in"])] + [
            (dst[:, :, :], t[src], s["wide_in"]) for dst, src in ((uqT, "uqT_l"), (ukT, "ukT_l"), (uvT, "uvT_l"), (wo1, "wo1_l"))] + loads)
        ps = sc.ps("logits", [P, TT, E_ALL])
        a_ps = [sc.ps(f"a{i}", [P, 512]) for i in range(4)]
        with nc.Block() as block:
            @block.tensor
            def _(pe):
                pe.wait_ge(s["gw_in"], 16)
                for n in range(TT):
                    for c in range(DC):
                        last = nc.tensor.matmul(ps[:, n, :], h32[:, c, n * P:(n + 1) * P], gw[:, c, :], start=c == 0, stop=c == DC - 1)
                last.then_inc(s["logits_done"], 1)
                pe.wait_ge(s["wide_in"], 64)
                for i in range(2):
                    for m in range(8):
                        h = 8 * i + m
                        last = nc.tensor.matmul(a_ps[i][0:QC, m * KVC:(m + 1) * KVC], uqT[:, h, :], ukT[:, h, :], start=True, stop=True)
                    last.then_inc(s["a_done"], 1)
                for h in range(H1):
                    wait(pe, s["a_used"], h - 1)
                    last = nc.tensor.matmul(a_ps[(h + 2) % 4][0:KVC, 0:D], uvT[:, h, :], wo1[:, h, :], start=True, stop=True)
                    last.then_inc(s["a_done"], 1)

            @block.scalar
            def _(act):
                act.wait_ge(s["step"], 1)
                nc.scalar.activation(sig[:, :, :], logit[:, :, :], ACT.Sigmoid).then_inc(s["sig_ready"], 1)
                for i in range(2):
                    act.wait_ge(s["a_done"], i + 1)
                    nc.scalar.activation(wabs[:, 8 * i:8 * i + 8, :], a_ps[i][0:QC, :].rearrange("p (m k) -> p m k", m=8), ACT.Copy).then_inc(s["a_used"], 1)
                for h in range(H1):
                    act.wait_ge(s["a_done"], h + 3)
                    nc.scalar.activation(wvo[KVC * (h % 2):KVC * (h % 2) + KVC, h // 2, :], a_ps[(h + 2) % 4][0:KVC, 0:D], ACT.Copy).then_inc(s["a_used"], 1)

            @block.vector
            def _(dve):
                steps = [0]
                V = nc.vector

                def link(ins):
                    steps[0] += 1
                    ins.then_inc(s["step"], 1)
                    dve.wait_ge(s["step"], steps[0])

                def wide(ap, n):
                    return ap.to_broadcast([P, TT, n])

                def choose(vals, n, k, width, out):
                    for m in range(TT):
                        link(V.max(best[:, m, :], vals[:, m, 0:width]))
                    v, st, eq, a, b = vals[:, :, 0:n], strict[:, :, 0:n], same[:, :, 0:n], pa[:, :, 0:n], pb[:, :, 0:n]
                    link(V.tensor_tensor(st, v, wide(best[:, :, k - 1:k], n), ALU.is_gt))
                    link(V.tensor_tensor(eq, v, wide(best[:, :, k - 1:k], n), ALU.is_equal))
                    link(V.reduce_sum(few[:, :], st, AX.X))
                    link(V.tensor_scalar(few[:, :], few[:, :], -1.0, float(k), ALU.mult, ALU.add))
                    link(V.tensor_copy(a, eq))
                    shift = 1
                    while shift < n:
                        link(V.tensor_copy(b[:, :, 0:shift], a[:, :, 0:shift]))
                        link(V.tensor_tensor(b[:, :, shift:n], a[:, :, shift:n], a[:, :, 0:n - shift], ALU.add))
                        a, b = b, a
                        shift *= 2
                    link(V.tensor_tensor(a, a, wide(few[:, :].unsqueeze(2), n), ALU.is_le))
                    link(V.tensor_tensor(eq, eq, a, ALU.mult))
                    link(V.tensor_tensor(out, st, eq, ALU.add))

                dve.wait_ge(s["logits_done"], 1)
                link(V.tensor_copy(logit[:, :, :], ps[:, :, :]))
                link(V.memset(gmax[:, :, :], -3e38))
                link(V.tensor_reduce(gmax[:, :, 0:GRP], logit[:, :, :].rearrange("p t (g e) -> p t g e", g=GRP), AX.X, ALU.max))
                choose(gmax, GRP, TOP_GRP, 8, gsel[:, :, :])
                dve.wait_ge(s["sig_ready"], 1)
                spread = gsel[:, :, :].unsqueeze(3).to_broadcast([P, TT, GRP, EPG])
                grouped = lambda a: a[:, :, :].rearrange("p t (g e) -> p t g e", g=GRP)
                link(V.tensor_tensor(grouped(logit), grouped(logit), spread, ALU.mult))
                link(V.tensor_scalar(gsel[:, :, :], gsel[:, :, :], 1e30, -1e30, ALU.mult, ALU.add))
                link(V.tensor_tensor(grouped(logit), grouped(logit), spread, ALU.add))
                choose(logit, E_ALL, TOPK, E_ALL, sel[:, :, :])
                link(V.tensor_tensor(sel[:, :, :], sel[:, :, :], sig[:, :, :], ALU.mult))
                link(V.reduce_sum(few[:, :], sel[:, :, :], AX.X))
                link(V.reciprocal(few[:, :], few[:, :]))
                link(V.memset(gates[:, :, E_ALL:EXPERTS], 1.0))
                link(V.tensor_tensor(gates[:, :, 0:E_ALL], sel[:, :, :], wide(few[:, :].unsqueeze(2), E_ALL), ALU.mult))


def experts(nc, t, x, hhl, wabs, wvo, wq):
    with Scope(nc, "moe") as sc:
        gates = sc.sb("gates", [P, TT, EXPERTS])
        seg_i, seg = sc.sb("seg_i", [BK + 1, BLOCKS], I32), sc.sb("seg", [BK + 1, BLOCKS])
        lim = sc.sb("lim", [BK + 1, 3])
        index = sc.sb("index", [BK + 1, BLOCKS], U32)
        turn = sc.sb("turn", [BK + 1, 2, STEP_BLOCKS], U32)
        rows = sc.sb("rows", [BK + 1, 2, STEP_BLOCKS, ROW])
        held = sc.sb("held", [1, 3])
        zero = sc.sb("zero", [BK + 1, STEP_BLOCKS], U32)
        NQ = 3 * DC * FI
        PART = NQ // NSTEP
        w8 = sc.sb("w8", [P, NQ])
        magic, y8, over = sc.sb("magic", [P, PART]), sc.sb("y8", [P, PART]), sc.sb("over", [P, PART])
        wq_flat = wq[:, :, :].rearrange("p k n -> p (k n)")
        up32, down32 = sc.sb("up32", [P, 2, DC, UPW]), sc.sb("down32", [P, 2, 2, D])
        up, down = sc.sb("up", [P, 2, 2, DC, UPW], BF16), sc.sb("down", [P, 2, 2, 2, D], BF16)
        silu = sc.sb("silu", [P, 2, 3, SPAN])
        h = sc.sb("h", [P, 2, 2, SPAN])
        hs = sc.sb("hs", [P, 2, 2, 2, SPAN], BF16)
        R = M - P
        names = ["seg_in", "w8_in", "indexed", "turned", "zero_set", "held_set", "quant",
                 "w_hi", "w_lo", "up_done", "silu_done", "h_done", "h_hi", "h_lo", "y_done", "added"]
        s = {n: sc.sem(n) for n in names}
        load = [sc.sem(f"load{i}") for i in range(2)]
        gathered = [sc.sem(f"gathered{i}") for i in range(2)]
        stored = [sc.sem(f"stored{i}") for i in range(2)]
        TILES_STEP = SPAN // P

        def weights_of(e, u):
            src_u, src_d = (t[n][bass.ds(e, 1)] if not isinstance(e, int) else t[n][e:e + 1] for n in ("up_l", "down_l"))
            return ((up32[:, u, :, :], src_u.rearrange("e p c n -> p (e c) n")), (down32[:, u, :, :], src_d.rearrange("e p c n -> p (e c) n")))

        route(nc, t, x, hhl, gates, wabs, wvo, [(dst, src, load[0]) for dst, src in weights_of(0, 0)] + [
            (seg_i[:, :], t["segk_l"], s["seg_in"]), (lim[:, :], t["lim_l"], s["seg_in"])] + [
            (dst, src, load[1]) for dst, src in weights_of(1, 1)] + [(w8[:, :], t["f8_l"], s["w8_in"])])
        up_ps = [sc.ps(f"up{i}", [P, SPAN]) for i in range(6)]
        y_ps = [sc.ps(f"y{i}", [P, 2, D]) for i in range(2)]

        def each_pair(eng, expert, tail=None):
            expert(0, 0, True)
            expert(1, 1, False)
            with eng.Fori(1, EXPERTS // 2) as p:
                expert(2 * p, 0, False)
                expert(2 * p + 1, 1, False)
            if tail:
                tail(STEPS * EXPERTS)

        with nc.Block() as block:
            @block.sync
            def _(sp):
                def fetch(e, u):
                    sp.wait_ge(s["w_lo"], 2 * e - 2)
                    for dst, src in weights_of(e, u):
                        sp.dma_start(dst, src).then_inc(load[u], 16)

                def store(n, u):
                    sp.wait_ge(gathered[u], 64 * ((n - u) // 2 + 1))
                    dst = t["near_s"][n:n + 1] if isinstance(n, int) else t["near_s"][bass.ds(n, 1)]
                    sp.dma_start(dst.rearrange("s p m -> p (s m)"), rows[:, u, :, :].rearrange("p m n -> p (m n)")).then_inc(stored[u], 16)

                fetch(2, 0)
                fetch(3, 1)
                store(0, 0)
                with sp.Fori(2, EXPERTS // 2) as p:
                    fetch(2 * p, 0)
                    store(2 * p - 3, 1)
                    fetch(2 * p + 1, 1)
                    store(2 * p - 2, 0)
                store(NSTEP - 1, 1)
                for u in range(2):
                    sp.wait_ge(stored[u], 16 * (NSTEP // 2) + 1)

            @block.gpsimd
            def _(pool):
                nc.gpsimd.memset(zero[:, :], 0).then_inc(s["zero_set"], 1)
                nc.gpsimd.memset(held[:, :], 0.0).then_inc(s["held_set"], 1)
                pool.wait_ge(s["zero_set"], 1)
                pool.wait_ge(s["indexed"], 2 + B)

                def split(e, u, first):
                    pool.wait_ge(s["w_hi"], 2 * e + 1)
                    nc.gpsimd.tensor_tensor(up[:, u, 1, :, :], up32[:, u, :, :], up[:, u, 0, :, :], ALU.subtract).then_inc(s["w_lo"], 1)
                    pool.wait_ge(s["w_hi"], 2 * e + 2)
                    nc.gpsimd.tensor_tensor(down[:, u, 1, :, :], down32[:, u, :, :], down[:, u, 0, :, :], ALU.subtract).then_inc(s["w_lo"], 1)
                    if not isinstance(e, int):
                        gather(e - 2, u)

                def gather(n, u):
                    pool.wait_ge(stored[u], 16 * ((n - u) // 2) + 1)
                    nc.gpsimd.tensor_tensor(turn[:, u, :], index[:, bass.ds(STEP_BLOCKS * n, STEP_BLOCKS)], zero[:, :], ALU.add).then_inc(s["turned"], 1)
                    pool.wait_ge(s["held_set"], n + 1)
                    pool.wait_ge(s["turned"], n + 1)
                    nc.gpsimd.tensor_tensor(held[:, u:u + 1], held[:, 2:3], held[:, 2:3], ALU.add).then_inc(s["held_set"], 1)
                    for m in range(STEP_BLOCKS):
                        pool.indirect_dma_start(out=rows[:, u, m, :], out_offset=None, in_=t["ktab_s"],
                                                in_offset=bass.IndirectOffsetOnAxis(ap=turn[:, u, m:m + 1], axis=0)).then_inc(gathered[u], 16)
                each_pair(pool, split)

            def unit_parts():
                return ((0, P), (1, R))

            @block.tensor
            def _(pe):
                def gate_up(q, hf, e, u):
                    if hf == 0:
                        pe.wait_ge(s["w_lo"], 2 * e + 1)
                    for k, (c0, n) in enumerate(UP_COLS):
                        o = up_ps[3 * hf + k][0:n, :]
                        wait(pe, s["h_done"], 3 * (q - 2) + k + 1)
                        for c in range(DC):
                            for a, w in ((0, 0), (0, 1), (1, 0)):
                                last = nc.tensor.matmul(o, up[:, u, w, c, c0:c0 + n], hhl[:, a, c, hf * SPAN:(hf + 1) * SPAN],
                                                        start=(c, a, w) == (0, 0, 0), stop=(c, a) == (DC - 1, 1))
                        last.then_inc(s["up_done"], 1)

                def down_rows(q, hf, e, u):
                    pe.wait_ge(s["w_lo"], 2 * e + 2)
                    pe.wait_ge(s["h_lo"], 2 * q + 2)
                    for m in range(TILES_STEP):
                        if m % 2 == 0:
                            wait(pe, s["added"], TILES_STEP * (q - 1) + m + 2)
                        o = y_ps[m // 2][:, m % 2, :]
                        for part, n in unit_parts():
                            for a, w in ((0, 0), (0, 1), (1, 0)):
                                last = nc.tensor.matmul(o, hs[0:n, hf, a, part, m * P:(m + 1) * P], down[0:n, u, w, part, :],
                                                        start=(part, a, w) == (0, 0, 0), stop=(part, a) == (1, 1))
                        if m % 2:
                            last.then_inc(s["y_done"], 1)

                def expert(e, u, first):
                    q = STEPS * e
                    gate_up(q, 0, e, u)
                    if not first:
                        down_rows(q - 1, 1, e - 1, 1 - u)
                    gate_up(q + 1, 1, e, u)
                    down_rows(q, 0, e, u)

                each_pair(pe, expert, lambda q: down_rows(q - 1, 1, EXPERTS - 1, 1))

            @block.scalar
            def _(act):
                def weights_high(e, u):
                    act.wait_ge(load[u], 32 * (e // 2 + 1) if isinstance(e, int) else 32 * ((e - u) // 2 + 1))
                    wait(act, s["up_done"], 6 * (e - 1))
                    nc.scalar.activation(up[:, u, 0, :, :], up32[:, u, :, :], ACT.Copy).then_inc(s["w_hi"], 1)
                    wait(act, s["y_done"], 4 * (e - 1))
                    nc.scalar.activation(down[:, u, 0, :, :], down32[:, u, :, :], ACT.Copy).then_inc(s["w_hi"], 1)

                def gates_of(q, hf):
                    for k, (_, n) in enumerate(UP_ROWS):
                        act.wait_ge(s["up_done"], 3 * q + k + 1)
                        wait(act, s["h_done"], 3 * (q - 2) + k + 1)
                        nc.scalar.activation(silu[64:64 + n, hf, k, :], up_ps[3 * hf + k][0:n, :], ACT.Silu).then_inc(s["silu_done"], 1)

                def high(q, hf):
                    for part, n in unit_parts():
                        act.wait_ge(s["h_done"], 3 * q + 2 + part)
                        wait(act, s["y_done"], 2 * (q - 1))
                        nc.scalar.activation(hs[0:n, hf, 0, part, :], h[0:n, hf, part, :], ACT.Copy).then_inc(s["h_hi"], 1)

                def expert(e, u):
                    q = STEPS * e
                    gates_of(q, 0)
                    high(q, 0)
                    if not (isinstance(e, int) and e == EXPERTS - 1):
                        weights_high(e + 1, 1 - u)
                    gates_of(q + 1, 1)
                    high(q + 1, 1)

                weights_high(0, 0)
                expert(0, 0)
                expert(1, 1)
                with act.Fori(1, EXPERTS // 2 - 1) as p:
                    expert(2 * p, 0)
                    expert(2 * p + 1, 1)
                expert(EXPERTS - 2, 0)
                expert(EXPERTS - 1, 1)

            @block.vector
            def _(dve):
                V = nc.vector

                def hidden(q, hf):
                    for k, (r0, n) in enumerate(UP_ROWS):
                        dve.wait_ge(s["silu_done"], 3 * q + k + 1)
                        if k == 0:
                            wait(dve, s["h_lo"], 2 * (q - 1))
                        out = h[r0 % P:r0 % P + n, hf, r0 // P, :]
                        nc.vector.tensor_tensor(out, up_ps[3 * hf + k][64:64 + n, :], silu[64:64 + n, hf, k, :], ALU.mult).then_inc(s["h_done"], 1)

                def low(q, hf):
                    for part, n in unit_parts():
                        dve.wait_ge(s["h_hi"], 2 * q + part + 1)
                        nc.vector.tensor_tensor(hs[0:n, hf, 1, part, :], h[0:n, hf, part, :], hs[0:n, hf, 0, part, :], ALU.subtract).then_inc(s["h_lo"], 1)

                def add(q, hf, e):
                    for m in range(TILES_STEP):
                        tile = TILES_STEP * hf + m
                        dve.wait_ge(s["y_done"], 2 * q + m // 2 + 1)
                        wait(dve, s["added"], TILES_STEP * (q - 1) + m + 1)
                        g = gates[:, tile, e:e + 1] if isinstance(e, int) else gates[:, tile, bass.ds(e, 1)]
                        nc.vector.scalar_tensor_tensor(x[:, tile, :], y_ps[m // 2][:, m % 2, :], g, x[:, tile, :], ALU.mult, ALU.add).then_inc(s["added"], 1)

                steps = [0]

                def link(ins):
                    steps[0] += 1
                    ins.then_inc(s["indexed"], 1)
                    dve.wait_ge(s["indexed"], steps[0])

                def key_indices():
                    dve.wait_ge(s["seg_in"], 32)
                    link(V.tensor_copy(seg[:, :], seg_i[:, :]))
                    link(V.tensor_scalar(seg[:, :], seg[:, :], lim[:, 0:1], lim[:, 1:2], ALU.add, ALU.max))
                    for b in range(B):
                        cols = slice(b * BLOCKS // B, (b + 1) * BLOCKS // B)
                        link(V.tensor_scalar(index[:, cols], seg[:, cols], lim[:, 2:3], float(b * TAB_ROWS), ALU.min, ALU.add))

                def quantize(n):
                    part = bass.ds(PART * n, PART)
                    w, done = w8[:, part], QUANT_STEPS * n

                    def then(ins, k):
                        ins.then_inc(s["quant"], 1)
                        dve.wait_ge(s["quant"], done + k)

                    then(V.tensor_scalar(magic[:, :].bitcast(I32), w.bitcast(I32), 0x7F800000, None, ALU.bitwise_and), 1)
                    then(V.tensor_scalar(magic[:, :], magic[:, :], 2.0 ** -6, 1.5 * 2 ** 20, ALU.max, ALU.mult), 2)
                    then(V.tensor_tensor(y8[:, :], w, magic[:, :], ALU.add), 3)
                    then(V.tensor_tensor(y8[:, :], y8[:, :], magic[:, :], ALU.subtract), 4)
                    then(V.tensor_scalar(over[:, :], y8[:, :], E4M3_MAX, 3e38, ALU.is_gt, ALU.mult), 5)
                    then(V.tensor_scalar(magic[:, :], y8[:, :], -E4M3_MAX, 3e38, ALU.is_lt, ALU.mult), 6)
                    then(V.tensor_tensor(over[:, :], over[:, :], magic[:, :], ALU.add), 7)
                    then(V.tensor_scalar(over[:, :], over[:, :], 10.0, None, ALU.mult), 8)
                    then(V.scalar_tensor_tensor(y8[:, :], y8[:, :], 1.0, over[:, :], ALU.mult, ALU.add), 9)
                    then(V.tensor_tensor(wq_flat[:, part], y8[:, :], over[:, :], ALU.subtract), QUANT_STEPS)

                for u in range(2):
                    V.memset(rows[:, u, 0, 0:1], 0.0).then_inc(stored[u], 1)
                key_indices()

                dve.wait_ge(s["w8_in"], 16)

                def expert(e, u, first):
                    q = STEPS * e
                    hidden(q, 0)
                    low(q, 0)
                    if not first:
                        add(q - 1, 1, e - 1)
                    hidden(q + 1, 1)
                    low(q + 1, 1)
                    add(q, 0, e)
                    if not isinstance(e, int):
                        quantize(e - 2)

                each_pair(dve, expert, lambda q: add(q - 1, 1, EXPERTS - 1))


def window_attention(nc, t, x, hhl, wabs, wvo):
    with Scope(nc, "win") as sc:
        HB = 2
        DEPTH = 10
        wdq32, wdq = sc.sb("wdq32", [P, DC, QC]), sc.sb("wdq", [P, 2, DC, QC], BF16)
        wqr32, wqt32 = sc.sb("wqr32", [QC, H1, R1]), sc.sb("wqt32", [QC, H1, R1])
        parts = [sc.sb(f"parts{i}", [QC, 2, H1, R1], BF16) for i in range(3)]
        cosq, sinq = sc.sb("cosq", [P, S]), sc.sb("sinq", [P, S])
        qc = sc.sb("qc", [QC, 2, TOK], BF16)
        qT = sc.sb("qT", [P, TOK, H1])
        cq, sq = sc.sb("cq", [P, 2, SPAN]), sc.sb("sq", [P, 2, SPAN])
        ident = sc.sb("ident", [P, P])
        own = sc.sb("own", [P, BK])
        own1 = sc.sb("own1", [P, BK])
        seg_i, seg = sc.sb("seg_i", [P, BLOCKS], I32), sc.sb("seg", [P, BLOCKS])
        place = sc.sb("place", [P, WIN])
        key = sc.sb("key", [P, BLOCKS, WIN])
        bad = sc.sb("bad", [P, BLOCKS, WIN])
        none = sc.sb("none", [P, BLOCKS])
        keep = sc.sb("keep", [P, BLOCKS])
        near = sc.sb("near", [BK + 1, DEPTH, STEP_BLOCKS, ROW])
        keyT = sc.sb("keyT", [P, 2, STEP_BLOCKS, BK])
        picked = sc.sb("picked", [P, 2, STEP_BLOCKS, BK])
        sc9 = sc.sb("sc9", [P, 3, STEP_BLOCKS, WIN])
        top = sc.sb("top", [P, 2, STEP_BLOCKS])
        pr = sc.sb("pr", [P, 3, STEP_BLOCKS, BK + 1])
        prT = sc.sb("prT", [BK + 1, 2, STEP_BLOCKS, P])
        ol = sc.sb("ol", [P, 2, H1 // 2, P])
        names = ["in_", "w_hi", "w_lo", "qc_done", "qc_hi", "qc_lo", "parts_hi", "parts_lo0", "parts_lo", "r_done", "cs_ready", "n_copied", "r_ready", "mask", "kt_done", "kt_ready",
                 "sc_done", "picked_", "rest", "e_ready", "w_ready", "pr_mean", "pr_ready", "pt_done", "pt_ready", "o_done", "o_used", "y_done", "added"]
        s = {n: sc.sem(n) for n in names}
        near_in = [sc.sem(f"near_in{i}") for i in range(DEPTH)]
        TSTEP = P // (BQ * STEP_BLOCKS)
        normalize(nc, t, "norm3", x, hhl, None, [(dst, t[src], s["in_"]) for dst, src in (
            (wdq32[:, :, :], "wdq_l"), (wqr32[:, :, :], "wqr_l"), (wqt32[:, :, :], "wqt_l"), (cosq[:, :], "cosq_l"), (sinq[:, :], "sinq_l"),
            (ident[:, :], "ident_l"), (own[:, :], "own_l"), (own1[:, :], "own1_l"), (seg_i[:, :], "segq_l"), (place[:, :], "place_l"))])
        b8 = [sc.ps(f"b{i}", [P, 512]) for i in range(8)]
        with nc.Block() as block:
            @block.sync
            def _(sp):
                for n in range(NSTEP):
                    wait(sp, s["o_done"], n - DEPTH + 1)
                    sp.dma_start(near[:, n % DEPTH, :, :].rearrange("p m n -> p (m n)"), t["near_s"][n]).then_inc(near_in[n % DEPTH], 16)

            @block.tensor
            def _(pe):
                pe.wait_ge(s["in_"], 160)
                pe.wait_ge(s["w_lo"], 1)
                for f in range(HB):
                    for c in range(DC):
                        for a, w in ((0, 0), (0, 1), (1, 0)):
                            last = nc.tensor.matmul(b8[f][0:QC, :], wdq[:, w, c, :], hhl[:, a, c, f * SPAN:(f + 1) * SPAN],
                                                    start=(c, a, w) == (0, 0, 0), stop=(c, a) == (DC - 1, 1))
                    last.then_inc(s["qc_done"], 1)
                for q in range(H1 // 2 * HB):
                    hp, f = divmod(q, HB)
                    pe.wait_ge(s["qc_lo"], HB)
                    pe.wait_ge(s["parts_lo0"], 1)
                    for par in range(2):
                        wait(pe, s["n_copied"], 2 * (q - 1) + par + 1)
                        for a, w in ((0, 0), (0, 1), (1, 0)):
                            last = nc.tensor.matmul(b8[par][0:KVC, :], parts[0][:, w, 2 * hp + par, :], qc[:, a, f * SPAN:(f + 1) * SPAN],
                                                    start=(a, w) == (0, 0), stop=a == 1)
                        last.then_inc(s["r_done"], 1)
                    wait(pe, s["cs_ready"], 2 * (q - 1))
                    pe.wait_ge(s["parts_lo"], 2)
                    for k in range(2):
                        for a, w in ((0, 0), (0, 1), (1, 0)):
                            last = nc.tensor.matmul(b8[2 + 2 * (q % 2) + k][:, :], parts[1 + k][:, w, 2 * hp:2 * hp + 2, :].rearrange("p h r -> p (h r)"),
                                                    qc[:, a, f * SPAN:(f + 1) * SPAN], start=(a, w) == (0, 0), stop=a == 1)
                    last.then_inc(s["r_done"], 1)
                pe.wait_ge(s["n_copied"], 2 * HB * (H1 // 2))
                pe.wait_ge(s["cs_ready"], 2 * HB * (H1 // 2))

                def keys(n):
                    pe.wait_ge(near_in[n % DEPTH], 16 * (n // DEPTH + 1))
                    wait(pe, s["kt_ready"], n - 1)
                    for m in range(STEP_BLOCKS):
                        last = nc.tensor.transpose(b8[n % 2][:, m * BK:(m + 1) * BK], near[0:BK, n % DEPTH, m, :], ident[0:BK, 0:BK])
                    last.then_inc(s["kt_done"], 1)

                def score(n):
                    pe.wait_ge(s["kt_ready"], n + 1)
                    if n == 0:
                        pe.wait_ge(s["r_ready"], H1 * HB)
                    wait(pe, s["picked_"], n - 1)
                    for m in range(STEP_BLOCKS):
                        t0 = (STEP_BLOCKS * n + m) * BQ
                        last = nc.tensor.matmul(b8[2 + n % 2][:, m * BK:(m + 1) * BK], qT[:, t0:t0 + BQ, :].rearrange("p t h -> p (t h)"),
                                                keyT[:, n % 2, m, :], start=True, stop=True)
                    last.then_inc(s["sc_done"], 1)

                def turn(n):
                    pe.wait_ge(s["pr_ready"], n + 1)
                    pe.wait_ge(s["pr_mean"], n + 1)
                    wait(pe, s["pt_ready"], n - 1)
                    for m in range(STEP_BLOCKS):
                        last = nc.tensor.transpose(b8[4 + n % 2][0:BK + 1, m * P:(m + 1) * P], pr[:, n % 3, m, :], ident[:, :])
                    last.then_inc(s["pt_done"], 1)

                def value(n):
                    pe.wait_ge(s["pt_ready"], n + 1)
                    wait(pe, s["o_used"], 2 * n)
                    for m in range(STEP_BLOCKS):
                        last = nc.tensor.matmul(b8[6][0:KVC, m * P:(m + 1) * P], near[:, n % DEPTH, m, 0:KVC], prT[:, n % 2, m, :], start=True, stop=True)
                    last.then_inc(s["o_done"], 1)

                def project(n):
                    pe.wait_ge(s["o_used"], 2 * TSTEP * (n + 1))
                    wait(pe, s["added"], n)
                    for hp in range(H1 // 2):
                        last = nc.tensor.matmul(b8[7][:, 0:D], ol[:, n % 2, hp, :], wvo[:, hp, :], start=hp == 0, stop=hp == H1 // 2 - 1)
                    last.then_inc(s["y_done"], 1)

                keys(0)
                keys(1)
                for n in range(NSTEP + 5):
                    if n < NSTEP:
                        score(n)
                    if 3 <= n < NSTEP + 3:
                        turn(n - 3)
                    if n + 2 < NSTEP:
                        keys(n + 2)
                    if 4 <= n < NSTEP + 4:
                        value(n - 4)
                    if 5 <= n and (n - 4) % TSTEP == 0:
                        project((n - 4) // TSTEP - 1)

            @block.scalar
            def _(act):
                act.wait_ge(s["in_"], 160)
                nc.scalar.activation(wdq[:, 0, :, :], wdq32[:, :, :], ACT.Copy).then_inc(s["w_hi"], 1)
                for i, w in enumerate((wabs, wqr32, wqt32)):
                    nc.scalar.activation(parts[i][:, 0, :, :], w[:, :, :], ACT.Copy).then_inc(s["parts_hi"], 1)
                for f in range(HB):
                    act.wait_ge(s["qc_done"], f + 1)
                    nc.scalar.activation(qc[:, 0, f * SPAN:(f + 1) * SPAN], b8[f][0:QC, :], ACT.Copy).then_inc(s["qc_hi"], 1)
                for q in range(H1 // 2 * HB):
                    hp, f = divmod(q, HB)
                    for par in range(2):
                        act.wait_ge(s["r_done"], 3 * q + par + 1)
                        nc.scalar.activation(qT[0:KVC, f * SPAN:(f + 1) * SPAN, 2 * hp + par], b8[par][0:KVC, :], ACT.Copy).then_inc(s["n_copied"], 1)

                def copy_keys(n):
                    act.wait_ge(s["kt_done"], n + 1)
                    wait(act, s["sc_done"], n - 1)
                    nc.scalar.activation(keyT[:, n % 2, :, :].rearrange("p m k -> p (m k)"), b8[n % 2][:, 0:STEP_BLOCKS * BK], ACT.Copy).then_inc(s["kt_ready"], 1)

                def exps(n):
                    act.wait_ge(s["rest"], 3 * n + 3)
                    nc.scalar.activation(sc9[:, n % 3, :, :], sc9[:, n % 3, :, :], ACT.Exp).then_inc(s["e_ready"], 1)

                def copy_weights(n):
                    act.wait_ge(s["pt_done"], n + 1)
                    wait(act, s["o_done"], n - 1)
                    nc.scalar.activation(prT[:, n % 2, :, :].rearrange("p m k -> p (m k)"), b8[4 + n % 2][0:BK + 1, :], ACT.Copy).then_inc(s["pt_ready"], 1)

                def copy_out(n):
                    act.wait_ge(s["o_done"], n + 1)
                    tile, t0 = n // TSTEP, n % TSTEP * STEP_BLOCKS * BQ
                    if n % TSTEP == 0:
                        wait(act, s["y_done"], tile - 1)
                    src = b8[6][0:KVC, :].rearrange("p (t g e) -> p e g t", g=H1 // 2, e=2)
                    for e in range(2):
                        nc.scalar.activation(ol[KVC * e:KVC * e + KVC, tile % 2, :, t0:t0 + STEP_BLOCKS * BQ], src[:, e, :, :], ACT.Copy).then_inc(s["o_used"], 1)

                copy_keys(0)
                copy_keys(1)
                for n in range(NSTEP + 4):
                    if 3 <= n < NSTEP + 3:
                        copy_weights(n - 3)
                    if n + 2 < NSTEP:
                        copy_keys(n + 2)
                    if 4 <= n:
                        copy_out(n - 4)
                    if n < NSTEP:
                        exps(n)

            @block.gpsimd
            def _(pool):
                pool.wait_ge(s["in_"], 160)
                for i, w in ((1, wqr32), (2, wqt32)):
                    pool.wait_ge(s["parts_hi"], i + 1)
                    nc.gpsimd.tensor_tensor(parts[i][:, 1, :, :], w[:, :, :], parts[i][:, 0, :, :], ALU.subtract).then_inc(s["parts_lo"], 1)
                for q in range(H1 // 2 * HB):
                    hp, f = divmod(q, HB)
                    pool.wait_ge(s["cs_ready"], 2 * q + 2)
                    for par in range(2):
                        rows = slice(R1 * par, R1 * par + R1)
                        nc.gpsimd.tensor_tensor(qT[KVC:P, f * SPAN:(f + 1) * SPAN, 2 * hp + par], cq[rows, q % 2, :], sq[rows, q % 2, :], ALU.add).then_inc(s["r_ready"], 1)

                for n in range(NSTEP):
                    pool.wait_ge(s["w_ready"], n + 1)
                    wait(pool, s["pt_done"], n - 2)
                    nc.gpsimd.tensor_tensor(pr[:, n % 3, :, 0:BK].rearrange("p m (q j) -> p m q j", j=WIN),
                                            own1[:, :].rearrange("p (q j) -> p q j", j=WIN).unsqueeze(1).to_broadcast([P, STEP_BLOCKS, BQ, WIN]),
                                            sc9[:, n % 3, :, :].unsqueeze(2).to_broadcast([P, STEP_BLOCKS, BQ, WIN]), ALU.mult).then_inc(s["pr_ready"], 1)

            @block.vector
            def _(dve):
                V = nc.vector
                dve.wait_ge(s["in_"], 160)
                dve.wait_ge(s["w_hi"], 1)
                V.tensor_tensor(wdq[:, 1, :, :], wdq32[:, :, :], wdq[:, 0, :, :], ALU.subtract).then_inc(s["w_lo"], 1)
                dve.wait_ge(s["parts_hi"], 1)
                V.tensor_tensor(parts[0][:, 1, :, :], wabs[:, :, :], parts[0][:, 0, :, :], ALU.subtract).then_inc(s["parts_lo0"], 1)
                for f in range(HB):
                    dve.wait_ge(s["qc_hi"], f + 1)
                    cols = slice(f * SPAN, (f + 1) * SPAN)
                    V.tensor_tensor(qc[:, 1, cols], b8[f][0:QC, :], qc[:, 0, cols], ALU.subtract).then_inc(s["qc_lo"], 1)
                steps = [0]

                def link(ins):
                    steps[0] += 1
                    ins.then_inc(s["mask"], 1)
                    dve.wait_ge(s["mask"], steps[0])

                for q in range(H1 // 2 * HB):
                    dve.wait_ge(s["r_done"], 3 * q + 3)
                    wait(dve, s["r_ready"], 2 * (q - 1))
                    for k, (out, tab) in enumerate(((cq, cosq), (sq, sinq))):
                        V.tensor_tensor(out[:, q % 2, :].rearrange("p (b t) -> p b t", t=S), b8[2 + 2 * (q % 2) + k][:, :].rearrange("p (b t) -> p b t", t=S),
                                        tab[:, :].unsqueeze(1).to_broadcast([P, SPAN // S, S]), ALU.mult).then_inc(s["cs_ready"], 1)

                wide = [P, BLOCKS, WIN]
                link(V.tensor_copy(seg[:, :], seg_i[:, :]))
                link(V.tensor_tensor(key[:, :, :], seg[:, :].unsqueeze(2).to_broadcast(wide), place[:, :].unsqueeze(1).to_broadcast(wide), ALU.add))
                link(V.tensor_scalar(bad[:, :, :], key[:, :, :], 0.0, NEG, ALU.is_lt, ALU.mult))
                link(V.tensor_scalar(key[:, :, :], key[:, :, :], float(CTX - 1), NEG, ALU.is_gt, ALU.mult))
                link(V.tensor_tensor(bad[:, :, :], bad[:, :, :], key[:, :, :], ALU.add))
                link(V.tensor_reduce(none[:, :], bad[:, :, :], AX.X, ALU.max))
                link(V.tensor_scalar(none[:, :], none[:, :], NEG, None, ALU.is_equal))
                link(V.tensor_scalar(keep[:, :], none[:, :], -1.0, 1.0, ALU.mult, ALU.add))

                def pick(n):
                    dve.wait_ge(s["sc_done"], n + 1)
                    wait(dve, s["pr_ready"], n - 2)
                    V.tensor_tensor(picked[:, n % 2, :, :], b8[2 + n % 2][:, 0:STEP_BLOCKS * BK].rearrange("p (m k) -> p m k", m=STEP_BLOCKS),
                                    own[:, :].unsqueeze(1).to_broadcast([P, STEP_BLOCKS, BK]), ALU.mult).then_inc(s["picked_"], 1)
                    dve.wait_ge(s["picked_"], n + 1)
                    blocks = slice(STEP_BLOCKS * n, STEP_BLOCKS * n + STEP_BLOCKS)
                    w = sc9[:, n % 3, :, :]
                    link(V.reduce_sum(w, picked[:, n % 2, :, :].rearrange("p m (q j) -> p m j q", j=WIN), AX.X))
                    V.tensor_tensor(w, w, bad[:, blocks, :], ALU.add).then_inc(s["rest"], 1)
                    dve.wait_ge(s["rest"], 3 * n + 1)
                    V.tensor_reduce(top[:, n % 2, :], w, AX.X, ALU.max).then_inc(s["rest"], 1)
                    dve.wait_ge(s["rest"], 3 * n + 2)
                    V.tensor_tensor(w, w, top[:, n % 2, :].unsqueeze(2).to_broadcast([P, STEP_BLOCKS, WIN]), ALU.subtract).then_inc(s["rest"], 1)

                def weigh(n):
                    blocks = slice(STEP_BLOCKS * n, STEP_BLOCKS * n + STEP_BLOCKS)
                    w = sc9[:, n % 3, :, :]
                    total = top[:, n % 2, :]
                    dve.wait_ge(s["e_ready"], n + 1)
                    link(V.reduce_sum(total, w, AX.X))
                    link(V.reciprocal(total, total))
                    link(V.tensor_tensor(total, total, keep[:, blocks], ALU.mult))
                    V.tensor_tensor(w, w, total.unsqueeze(2).to_broadcast([P, STEP_BLOCKS, WIN]), ALU.mult).then_inc(s["w_ready"], 1)
                    wait(dve, s["pt_done"], n - 2)
                    V.tensor_copy(pr[:, n % 3, :, BK:BK + 1], none[:, blocks].unsqueeze(2)).then_inc(s["pr_mean"], 1)

                for n in range(NSTEP + 5):
                    if n < NSTEP:
                        pick(n)
                    if 1 <= n < NSTEP + 1:
                        weigh(n - 1)
                    if 5 <= n and (n - 4) % TSTEP == 0:
                        tile = (n - 4) // TSTEP - 1
                        dve.wait_ge(s["y_done"], tile + 1)
                        V.tensor_tensor(x[:, tile, :], b8[7][:, 0:D], x[:, tile, :], ALU.add).then_inc(s["added"], 1)


def feed_forward(nc, t, x, hhl, wq):
    with Scope(nc, "ffn") as sc:
        scales, dscale = sc.sb("scales", [P, 2, FC]), sc.sb("dscale", [P, D])
        silu, h = sc.sb("silu", [P, 2, SPAN]), sc.sb("h", [P, 2, SPAN])
        hs = sc.sb("hs", [P, 2, FC, TOK], BF16)
        y = sc.sb("y", [P, 2, D])
        gate_w, up_w = (wq[:, k, :].rearrange("p (c n) -> p c n", c=DC) for k in (0, 1))
        down_w = wq[:, 2, :].rearrange("p (c n) -> p c n", c=FC)
        s = {n: sc.sem(n) for n in ["in_", "up_done", "silu_done", "h_done", "h_hi", "h_lo", "y_done", "scaled", "added", "out_"]}
        normalize(nc, t, "norm4", x, hhl, None, [(scales[:, :, :], t["scales_l"], s["in_"]), (dscale[:, :], t["dscale_l"], s["in_"])])
        up_ps = [sc.ps(f"up{i}", [P, SPAN]) for i in range(4)]
        y_ps = [sc.ps(f"y{i}", [P, D]) for i in range(2)]
        with nc.Block() as block:
            @block.sync
            def _(sp):
                for n in range(TT):
                    sp.wait_ge(s["added"], n + 1)
                    sp.dma_start(t["out_l"][n], x[:, n, :]).then_inc(s["out_"], 16)
                sp.wait_ge(s["out_"], 16 * TT)

            @block.tensor
            def _(pe):
                for f in range(STEPS):
                    for k in range(FC):
                        q = FC * f + k
                        wait(pe, s["h_done"], q - 1)
                        for g, w in enumerate((gate_w, up_w)):
                            for c in range(DC):
                                for a in range(2):
                                    last = nc.tensor.matmul(up_ps[2 * (q % 2) + g][:, :], w[:, c, k * P:(k + 1) * P], hhl[:, a, c, f * SPAN:(f + 1) * SPAN],
                                                            start=(c, a) == (0, 0), stop=(c, a) == (DC - 1, 1))
                            last.then_inc(s["up_done"], 1)
                for n in range(TT):
                    pe.wait_ge(s["h_lo"], FC * (n * P // SPAN + 1))
                    wait(pe, s["scaled"], n - 1)
                    for k in range(FC):
                        for a in range(2):
                            last = nc.tensor.matmul(y_ps[n % 2][:, :], hs[:, a, k, n * P:(n + 1) * P], down_w[:, k, :],
                                                    start=(k, a) == (0, 0), stop=(k, a) == (FC - 1, 1))
                    last.then_inc(s["y_done"], 1)

            @block.scalar
            def _(act):
                act.wait_ge(s["in_"], 32)
                for f in range(STEPS):
                    for k in range(FC + 1):
                        q = FC * f + k
                        if k < FC:
                            act.wait_ge(s["up_done"], 2 * q + 1)
                            wait(act, s["h_done"], q - 1)
                            nc.scalar.activation(silu[:, q % 2, :], up_ps[2 * (q % 2)][:, :], ACT.Silu, scale=scales[:, 0, k:k + 1]).then_inc(s["silu_done"], 1)
                        if k:
                            act.wait_ge(s["h_done"], q)
                            nc.scalar.activation(hs[:, 0, k - 1, f * SPAN:(f + 1) * SPAN], h[:, (q - 1) % 2, :], ACT.Copy).then_inc(s["h_hi"], 1)

            @block.vector
            def _(dve):
                dve.wait_ge(s["in_"], 32)
                for f in range(STEPS):
                    for k in range(FC + 1):
                        q = FC * f + k
                        if k < FC:
                            dve.wait_ge(s["silu_done"], q + 1)
                            dve.wait_ge(s["up_done"], 2 * q + 2)
                            wait(dve, s["h_lo"], q - 1)
                            nc.vector.scalar_tensor_tensor(h[:, q % 2, :], up_ps[2 * (q % 2) + 1][:, :], scales[:, 1, k:k + 1], silu[:, q % 2, :],
                                                           ALU.mult, ALU.mult).then_inc(s["h_done"], 1)
                        if k:
                            dve.wait_ge(s["h_hi"], q)
                            cols = slice(f * SPAN, (f + 1) * SPAN)
                            nc.vector.tensor_tensor(hs[:, 1, k - 1, cols], h[:, (q - 1) % 2, :], hs[:, 0, k - 1, cols], ALU.subtract).then_inc(s["h_lo"], 1)
                for n in range(TT):
                    dve.wait_ge(s["y_done"], n + 1)
                    wait(dve, s["added"], n - 1)
                    nc.vector.tensor_tensor(y[:, n % 2, :], y_ps[n % 2][:, :], dscale[:, :], ALU.mult).then_inc(s["scaled"], 1)
                    dve.wait_ge(s["scaled"], n + 1)
                    nc.vector.tensor_tensor(x[:, n, :], x[:, n, :], y[:, n % 2, :], ALU.add).then_inc(s["added"], 1)


def program(nc, t):
    def scratch(name, shape, dt):
        t[name] = nc.dram_tensor(name, shape, dt, kind="Internal").ap()

    scratch("kv_s", [B, P, 2 * DC * KP], BF16)
    scratch("tab_s", [B, P, 2 * KT * HALF], F32)
    scratch("wq_s", [KVH, P, 2, DC * REP * HD], BF16)
    scratch("wkv_s", [KVH, P, 2, DC * 2 * HD], BF16)
    scratch("wo_s", [KVH, P, 2, REP * D], BF16)
    scratch("ktab_s", [B * TAB_ROWS, ROW], F32)
    scratch("near_s", [BLOCKS // STEP_BLOCKS, BK + 1, STEP_BLOCKS * ROW], F32)
    with Scope(nc, "all") as top:
        x = top.sb("x", [P, TT, D])
        prepare(nc, t, x)
        attend(nc, t, x)
        with Scope(nc, "rest") as rest:
            hhl = rest.sb("hhl", [P, 2, DC, TOK], BF16)
            wq = rest.sb("wq", [P, 3, DC * FI], BF16)
            wabs, wvo = rest.sb("wabs", [QC, H1, KVC]), rest.sb("wvo", [P, H1 // 2, D])
            experts(nc, t, x, hhl, wabs, wvo, wq)
            window_attention(nc, t, x, hhl, wabs, wvo)
            feed_forward(nc, t, x, hhl, wq)


def layout(i):
    def rows(a, n):
        return np.ascontiguousarray(a.reshape(n, P, -1).transpose(1, 0, 2))

    ctx = np.zeros((B, P, DC, KP - S), np.float32)
    ctx[..., :CTX] = np.asarray(i["ctx_2048"]).transpose(0, 2, 1).reshape(B, DC, P, CTX).transpose(0, 2, 1, 3)
    pos = np.zeros((B, KP), np.int32)
    pos[:, :S] = i["itok_BxS_4096_4607"]
    pos[:, S:NK] = i["pos_BxS2"]
    wq = np.asarray(i["L0_xattn_Wq"]).T.reshape(DC, P, KVH, REP * HD).transpose(1, 2, 0, 3)
    wk, wv = (np.asarray(i[f"L0_xattn_W{n}"]).T.reshape(DC, P, KVH, HD).transpose(1, 2, 0, 3) for n in "kv")
    wo = np.asarray(i["L0_xattn_Wo"]).reshape(D, KVH * REP, HD).transpose(2, 1, 0)
    flat = lambda a: np.ascontiguousarray(a).reshape(P, -1)
    gate, up, down = (np.asarray(i[f"L0_ffn_w_{n}"]) for n in ("gate", "up", "down"))
    sg, su = (np.asarray(i[f"L0_ffn_sw_{n}"]).reshape(D, 2, M).transpose(1, 0, 2) for n in ("gate", "up"))
    gate, up = np.concatenate([gate, sg]), np.concatenate([up, su])
    down = np.concatenate([down, np.asarray(i["L0_ffn_sw_down"]).reshape(2, M, D)])
    def turned(a):
        return np.ascontiguousarray(np.asarray(a).T)

    def chunks(a):
        a = np.asarray(a)
        return np.ascontiguousarray(a.reshape(-1, P, a.shape[-1]).transpose(1, 0, 2))

    freq = (1.0 / 10000.0 ** (np.arange(RH, dtype=np.float32) / RH)).astype(np.float32)
    angle = (np.arange(CT * P, dtype=np.float32)[:, None] * freq).astype(np.float32)
    cos, sin = np.cos(angle), np.sin(angle)
    key_cos = rows(np.concatenate([cos, cos], -1), CT).reshape(P, CT, R1)
    key_sin = rows(np.concatenate([-sin, sin], -1), CT).reshape(P, CT, R1)
    query_cos = np.ascontiguousarray(np.tile(cos[:S], (1, 4)).T)
    query_sin = np.ascontiguousarray(np.tile(np.concatenate([-sin[:S], sin[:S]], -1), (1, 2)).T)
    wqr = np.asarray(i["L1_xattn_W_qr"]).reshape(QC, H1, R1)
    seg_ids = np.asarray(i["itok_BxS_0_1023"]).reshape(BLOCKS, BQ)
    seg_keys = np.zeros((BK + 1, BLOCKS), np.int32)
    seg_keys[:BK] = np.repeat(seg_ids, WIN, 1).T
    seg_rows = np.ascontiguousarray(np.repeat(seg_ids, H1, 1).T.astype(np.int32))
    place = np.broadcast_to(np.arange(WIN, dtype=np.float32) - LOOKBACK, (P, WIN)).copy()
    lim = np.empty((BK + 1, 3), np.float32)
    lim[:BK, 0], lim[:BK, 1], lim[:BK, 2] = np.arange(BK) % WIN - LOOKBACK, 0, CTX - 1
    lim[BK] = 0, CTX, CTX
    own = np.repeat(np.repeat(np.eye(BQ, dtype=np.float32), H1, 0), WIN, 1)
    ups = np.zeros((EXPERTS, D, UPW), np.float32)
    for (r0, n), (c0, _) in zip(UP_ROWS, UP_COLS):
        ups[:, :, c0:c0 + n] = gate[:, :, r0:r0 + n]
        ups[:, :, c0 + 64:c0 + 64 + n] = up[:, :, r0:r0 + n]
    downs = np.zeros((EXPERTS, 2 * P, D), np.float32)
    downs[:, :M] = down
    return {
        "x_l": rows(np.asarray(i["x"]).reshape(TOK, D), TT),
        "ctx_l": ctx,
        "pos_l": np.ascontiguousarray(pos.reshape(B * KT, P).T),
        "invf_l": np.broadcast_to((1.0 / 10000.0 ** (np.arange(0, HD, 2, dtype=np.float32) / HD)).astype(np.float32), (P, HALF)).copy(),
        "ident_l": np.eye(P, dtype=np.float32),
        "wq_l": flat(wq),
        "wkv_l": flat(np.concatenate([wk, wv], -1)),
        "wo_l": flat(wo),
        "kvc_l": chunks(i["L1_xattn_W_kvc"]),
        "kvcT_l": turned(i["L1_xattn_W_kvc"]),
        "wkr_l": np.asarray(i["L1_xattn_W_kr"]),
        "cosk_l": key_cos, "sink_l": key_sin, "cosq_l": query_cos, "sinq_l": query_sin,
        "uqT_l": np.ascontiguousarray(np.asarray(i["L1_xattn_W_uq"]).reshape(QC, H1, HD1).transpose(2, 1, 0)),
        "ukT_l": np.ascontiguousarray(np.asarray(i["L1_xattn_W_uk"]).reshape(KVC, H1, HD1).transpose(2, 1, 0)),
        "uvT_l": np.ascontiguousarray(np.asarray(i["L1_xattn_W_uv"]).reshape(KVC, H1, HD1).transpose(2, 1, 0)),
        "wo1_l": np.ascontiguousarray(np.asarray(i["L1_xattn_W_o"]).reshape(H1, HD1, D).transpose(1, 0, 2)),
        "wdq_l": chunks(i["L1_xattn_W_dq"]),
        "wqr_l": wqr, "wqt_l": np.ascontiguousarray(np.concatenate([wqr[..., RH:], wqr[..., :RH]], -1)),
        "segk_l": seg_keys, "segq_l": seg_rows, "lim_l": lim, "place_l": place, "own_l": own * np.float32(SCALE1), "own1_l": own,
        "f8_l": np.concatenate([chunks(i[f"L1_ffn_{n}_w"]).reshape(P, -1) for n in ("gate", "up", "down")], 1),
        "scales_l": np.ascontiguousarray(np.stack([np.asarray(i[f"L1_ffn_{n}_scale"]).reshape(FC, P) for n in ("gate", "up")]).transpose(2, 0, 1)),
        "dscale_l": np.broadcast_to(np.asarray(i["L1_ffn_down_scale"]), (P, D)).copy(),
        "gate_w_l": np.ascontiguousarray(np.asarray(i["L0_ffn_gate_w"]).reshape(DC, P, E_ALL).transpose(1, 0, 2)),
        "up_l": np.ascontiguousarray(ups.reshape(EXPERTS, DC, P, UPW).transpose(0, 2, 1, 3)),
        "down_l": np.ascontiguousarray(downs.reshape(EXPERTS, 2, P, D).transpose(0, 2, 1, 3)),
        "kw_l": np.ascontiguousarray(np.broadcast_to(np.asarray(i["L0_xattn_k_norm_w"]), (P, HD))),
        "qw_l": np.ascontiguousarray(np.broadcast_to(np.asarray(i["L0_xattn_q_norm_w"]), (P, HD))),
    }


def kernel(**inputs):
    import concourse.bacc as bacc
    from concourse.bass_utils import run_bass_kernel_spmd

    nc = bacc.Bacc("TRN2", target_bir_lowering=False, num_devices=1)
    arrays = layout(inputs)
    t = {n: nc.dram_tensor(f"in_{n}", a.shape, mybir.dt.from_np(a.dtype), kind="ExternalInput").ap() for n, a in arrays.items()}
    t["out_l"] = nc.dram_tensor("out", [TT, P, D], F32, kind="ExternalOutput").ap()
    program(nc, t)
    r = run_bass_kernel_spmd(nc, [{f"in_{n}": a for n, a in arrays.items()}], core_ids=[0])
    return r.results[0]["out"].reshape(B, S, D)
```
